# Optimizing a Trainium2 kernel written in Bass

```python
import numpy as np
import jax
import jax.numpy as jnp

def _softmax(x, axis=-1):
    return jax.nn.softmax(x, axis=axis)

def _gelu(x):
    return jax.nn.gelu(x, approximate=True)

def _silu(x):
    return jax.nn.silu(x)

def _sigmoid(x):
    return jax.nn.sigmoid(x)

def _layernorm(x, axis=-1, eps=1e-05):
    m = jnp.mean(x, axis=axis, keepdims=True)
    v = jnp.var(x, axis=axis, keepdims=True)
    return (x - m) / jnp.sqrt(v + eps)

def _scatter_add(tgt, idx, src, axis=0):
    return tgt.at[idx].add(src)

def _segment_sum(src, seg, n):
    return jax.ops.segment_sum(src, seg, n)
kernel_name = 'mk_decoder_preln_d2_seqx_r4_38a69a'

def setup_inputs(seed: int=0):
    np.random.seed(seed)
    _w = jnp.asarray

    def _rec_inputs():
        import jax
        import jax.numpy as jnp
        _rk = jax.random.key(seed)
        x = -0.0003929 + 0.9999 * jax.random.normal(jax.random.fold_in(_rk, 1), (8, 256, 256), jnp.float32)
        _lenS = 256 - jax.random.randint(jax.random.fold_in(_rk, 7), (8,), 0, max(1, 256 // 4) + 1, jnp.int32)
        _lenS2 = 256 - jax.random.randint(jax.random.fold_in(_rk, 8), (8,), 0, max(1, 256 // 4) + 1, jnp.int32)
        _ctx_768P = jax.random.normal(jax.random.fold_in(_rk, 11), (8, 16, 192), jnp.float32)
        _ctx_768c = jax.random.dirichlet(jax.random.fold_in(_rk, 511), 0.3 * jnp.ones((16,), jnp.float32), (8, 256))
        _ctx_768t = jnp.einsum('bsk,bkd->bsd', _ctx_768c, _ctx_768P)
        _ctx_768t = _ctx_768t * jax.lax.rsqrt(jnp.mean(jnp.square(_ctx_768t)) + 1e-12) * 0.953939
        ctx_768 = -7.36909e-05 + 0.999899 * (_ctx_768t + 0.3 * jax.random.normal(jax.random.fold_in(_rk, 611), (8, 256, 192), jnp.float32))
        return (x, ctx_768)
    x, ctx_768 = _rec_inputs()

    def _L0_attn_setup():
        import jax, jax.numpy as jnp
        import numpy as np
        L, H, D_MODEL, D_FF = (4, 16, 256, 1024)
        HD = D_MODEL // H
        LN_EPS = 1e-05
        ATT_EPS = 1e-06
        CHUNK = 128

        def _ln(x, g, b):
            m = jnp.mean(x, axis=-1, keepdims=True)
            v = jnp.var(x, axis=-1, keepdims=True)
            return (x - m) * jax.lax.rsqrt(v + LN_EPS) * g + b

        def _feature_map(x):
            return jax.nn.elu(x) + 1.0

        def _causal_linear_attention(q, k, v):
            B, S, Hn, D = q.shape
            nC = S // CHUNK
            q = q.reshape(B, nC, CHUNK, Hn, D)
            k = k.reshape(B, nC, CHUNK, Hn, D)
            v = v.reshape(B, nC, CHUNK, Hn, D)
            KV = jnp.einsum('bnchd,bnche->bnhde', k, v)
            Ks = jnp.sum(k, axis=2)
            KVcum = jnp.cumsum(KV, axis=1) - KV
            Kcum = jnp.cumsum(Ks, axis=1) - Ks
            inter = jnp.einsum('bnchd,bnhde->bnche', q, KVcum)
            den_inter = jnp.einsum('bnchd,bnhd->bnch', q, Kcum)
            scores = jnp.einsum('bnchd,bnkhd->bnhck', q, k)
            mask = jnp.tril(jnp.ones((CHUNK, CHUNK), dtype=bool))
            scores = jnp.where(mask, scores, 0.0)
            intra = jnp.einsum('bnhck,bnkhe->bnche', scores, v)
            den_intra = jnp.transpose(jnp.sum(scores, axis=-1), (0, 1, 3, 2))
            out = (inter + intra) / (den_inter + den_intra + ATT_EPS)[..., None]
            return out.reshape(B, S, Hn, D)

        def _forward(x, Wq, bq, Wk, bk, Wv, bv, Wo, bo, W1, b1, W2, b2, g1, be1, g2, be2, gf, bef):
            B, S, Dm = x.shape
            for l in range(L):
                q = (x @ Wq[l] + bq[l]).reshape(B, S, H, HD)
                k = (x @ Wk[l] + bk[l]).reshape(B, S, H, HD)
                v = (x @ Wv[l] + bv[l]).reshape(B, S, H, HD)
                att = _causal_linear_attention(_feature_map(q), _feature_map(k), v)
                x = x + att.reshape(B, S, Dm) @ Wo[l] + bo[l]
                y = x = _ln(x, g1[l], be1[l])
                y = jax.nn.gelu(y @ W1[l] + b1[l], approximate=False)
                y = y @ W2[l] + b2[l]
                x = _ln(x + y, g2[l], be2[l])
            return _ln(x, gf, bef)
        key = jax.random.key(seed)
        ks = jax.random.split(key, 8)
        B, S = (2, 1024)
        sc = 0.02

        def w(k, shape):
            return jax.random.normal(k, shape, jnp.float32) * sc
        return {'x': jax.random.normal(ks[0], (B, S, D_MODEL), jnp.float32), 'Wq': w(ks[1], (L, D_MODEL, D_MODEL)), 'bq': jnp.zeros((L, D_MODEL), jnp.float32), 'Wk': w(ks[2], (L, D_MODEL, D_MODEL)), 'bk': jnp.zeros((L, D_MODEL), jnp.float32), 'Wv': w(ks[3], (L, D_MODEL, D_MODEL)), 'bv': jnp.zeros((L, D_MODEL), jnp.float32), 'Wo': w(ks[4], (L, D_MODEL, D_MODEL)), 'bo': jnp.zeros((L, D_MODEL), jnp.float32), 'W1': w(ks[5], (L, D_MODEL, D_FF)), 'b1': jnp.zeros((L, D_FF), jnp.float32), 'W2': w(ks[6], (L, D_FF, D_MODEL)), 'b2': jnp.zeros((L, D_MODEL), jnp.float32), 'g1': jnp.ones((L, D_MODEL), jnp.float32), 'be1': jnp.zeros((L, D_MODEL), jnp.float32), 'g2': jnp.ones((L, D_MODEL), jnp.float32), 'be2': jnp.zeros((L, D_MODEL), jnp.float32), 'gf': jnp.ones((D_MODEL,), jnp.float32), 'bef': jnp.zeros((D_MODEL,), jnp.float32)}
    _L0_attn_all = _L0_attn_setup()
    _L0_attn_in = {k: v for k, v in _L0_attn_all.items() if k in ('Wq', 'bq', 'Wk', 'bk', 'Wv', 'bv', 'Wo', 'bo', 'W1', 'b1', 'W2', 'b2', 'g1', 'be1', 'g2', 'be2', 'gf', 'bef')}
    del _L0_attn_all

    def _L0_xattn_setup():
        import jax, jax.numpy as jnp
        import numpy as np
        EPS = 1e-08
        key = jax.random.key(seed)
        kv, kt, k1, k2, k3, k4 = jax.random.split(key, 6)
        B, S = (16, 256)
        VD, TD, H = (256, 192, 128)
        visual_features = jax.random.normal(kv, (B, S, VD), dtype=jnp.float32)
        text_features = jax.random.normal(kt, (B, S, TD), dtype=jnp.float32)
        Wv = jax.random.normal(k1, (H, VD), dtype=jnp.float32) * (1.0 / np.sqrt(VD))
        bv = jax.random.normal(k2, (H,), dtype=jnp.float32) * 0.01
        Wt = jax.random.normal(k3, (H, TD), dtype=jnp.float32) * (1.0 / np.sqrt(TD))
        bt = jax.random.normal(k4, (H,), dtype=jnp.float32) * 0.01
        return {'visual_features': visual_features, 'text_features': text_features, 'Wv': Wv, 'bv': bv, 'Wt': Wt, 'bt': bt}
    _L0_xattn_all = _L0_xattn_setup()
    _L0_xattn_in = {k: v for k, v in _L0_xattn_all.items() if k in ('Wv', 'bv', 'Wt', 'bt')}
    del _L0_xattn_all

    def _L0_ffn_setup():
        import jax, jax.numpy as jnp
        import numpy as np
        B, S, D, E = (4, 1024, 256, 8)
        key = jax.random.key(seed)
        ks = jax.random.split(key, 6)
        scale = 1.0 / np.sqrt(D)
        return {'tokens': jax.random.normal(ks[0], (B, S, D), dtype=jnp.float32), 'gate_w': jax.random.normal(ks[1], (D, E), dtype=jnp.float32) * scale, 'w0': jax.random.normal(ks[2], (D, D), dtype=jnp.float32) * scale, 'b0': jax.random.normal(ks[3], (D,), dtype=jnp.float32) * 0.01, 'w1': jax.random.normal(ks[4], (D, D), dtype=jnp.float32) * scale, 'b1': jax.random.normal(ks[5], (D,), dtype=jnp.float32) * 0.01}
    _L0_ffn_all = _L0_ffn_setup()
    _L0_ffn_in = {k: v for k, v in _L0_ffn_all.items() if k in ('gate_w', 'w0', 'b0', 'w1', 'b1')}
    del _L0_ffn_all

    def _L1_attn_setup():
        import jax, jax.numpy as jnp
        import numpy as np
        from jax import lax
        D_MODEL = 256
        D_INNER = 512
        N_STATE = 16
        DT_RANK = 64
        K_CONV = 4
        SCALE_BITS = 15

        def _dyadic_scan(u_flat, decay_flat):
            B, L, F = u_flat.shape

            def step(h, xs):
                d_t, u_t = xs
                h = d_t * h + u_t
                return (h, h)
            h0 = jnp.zeros((B, F), dtype=u_flat.dtype)
            _, hs = lax.scan(step, h0, (decay_flat.transpose(1, 0, 2), u_flat.transpose(1, 0, 2)))
            return hs.transpose(1, 0, 2)
        key = jax.random.key(seed)
        ks = jax.random.split(key, 12)
        s = lambda fan_in: 1.0 / np.sqrt(fan_in)
        inp = {'hidden_states': jax.random.normal(ks[0], (2, 256, D_MODEL), dtype=jnp.float32), 'in_proj_w': jax.random.uniform(ks[1], (2 * D_INNER, D_MODEL), minval=-s(D_MODEL), maxval=s(D_MODEL)), 'in_proj_b': jax.random.uniform(ks[2], (2 * D_INNER,), minval=-s(D_MODEL), maxval=s(D_MODEL)), 'conv_w': jax.random.uniform(ks[3], (D_INNER, 1, K_CONV), minval=-s(K_CONV), maxval=s(K_CONV)), 'conv_b': jax.random.uniform(ks[4], (D_INNER,), minval=-s(K_CONV), maxval=s(K_CONV)), 'x_proj_w': jax.random.uniform(ks[5], (DT_RANK + 2 * N_STATE, D_INNER), minval=-s(D_INNER), maxval=s(D_INNER)), 'dt_proj_w': jax.random.uniform(ks[6], (D_INNER, DT_RANK), minval=-s(DT_RANK), maxval=s(DT_RANK)), 'dt_proj_b': jax.random.uniform(ks[7], (D_INNER,), minval=-4.0, maxval=-2.0), 'out_proj_w': jax.random.uniform(ks[8], (D_MODEL, D_INNER), minval=-s(D_INNER), maxval=s(D_INNER)), 'out_proj_b': jax.random.uniform(ks[9], (D_MODEL,), minval=-s(D_INNER), maxval=s(D_INNER)), 'A_log': jnp.log(jnp.broadcast_to(jnp.arange(1, N_STATE + 1, dtype=jnp.float32), (D_INNER, N_STATE))), 'D': jnp.ones((D_INNER,), dtype=jnp.float32)}
        return inp
    _L1_attn_all = _L1_attn_setup()
    _L1_attn_in = {k: v for k, v in _L1_attn_all.items() if k in ('in_proj_w', 'in_proj_b', 'conv_w', 'conv_b', 'x_proj_w', 'dt_proj_w', 'dt_proj_b', 'out_proj_w', 'out_proj_b', 'A_log', 'D')}
    del _L1_attn_all

    def _L1_xattn_setup():
        import jax, jax.numpy as jnp
        import numpy as np
        HEADS = 8
        DIM_HEAD = 64
        QUERY_DIM = 256
        CONTEXT_DIM = 192
        INNER = HEADS * DIM_HEAD
        key = jax.random.key(seed)
        ks = jax.random.split(key, 7)
        B, Sq, Skv = (4, 1024, 256)
        x = jax.random.normal(ks[0], (B, Sq, QUERY_DIM), dtype=jnp.float32)
        context = jax.random.normal(ks[1], (B, Skv, CONTEXT_DIM), dtype=jnp.float32)
        Wq = jax.random.normal(ks[2], (QUERY_DIM, INNER), dtype=jnp.float32) * QUERY_DIM ** (-0.5)
        Wk = jax.random.normal(ks[3], (CONTEXT_DIM, INNER), dtype=jnp.float32) * CONTEXT_DIM ** (-0.5)
        Wv = jax.random.normal(ks[4], (CONTEXT_DIM, INNER), dtype=jnp.float32) * CONTEXT_DIM ** (-0.5)
        Wo = jax.random.normal(ks[5], (INNER, QUERY_DIM), dtype=jnp.float32) * INNER ** (-0.5)
        bo = jax.random.normal(ks[6], (QUERY_DIM,), dtype=jnp.float32) * 0.01
        return {'x': x, 'context': context, 'Wq': Wq, 'Wk': Wk, 'Wv': Wv, 'Wo': Wo, 'bo': bo}
    _L1_xattn_all = _L1_xattn_setup()
    _L1_xattn_in = {k: v for k, v in _L1_xattn_all.items() if k in ('Wq', 'Wk', 'Wv', 'Wo', 'bo')}
    del _L1_xattn_all

    def _L1_ffn_setup():
        import jax, jax.numpy as jnp
        import numpy as np
        E = 8
        K = 2
        CAP_FACTOR = 1.0
        key = jax.random.key(seed)
        ks = jax.random.split(key, 5)
        B, T, C, H = (4, 512, 256, 1024)
        x = jax.random.normal(ks[0], (B, T, C), dtype=jnp.float32)
        Wr = jax.random.normal(ks[1], (C, E), dtype=jnp.float32) * 0.02
        br = jnp.zeros((E,), jnp.float32)
        W1 = jax.random.normal(ks[2], (E, C, H), dtype=jnp.float32) * 0.02
        b1 = jnp.zeros((E, H), jnp.float32)
        W2 = jax.random.normal(ks[3], (E, H, C), dtype=jnp.float32) * 0.02
        b2 = jnp.zeros((E, C), jnp.float32)
        return {'x': x, 'Wr': Wr, 'br': br, 'W1': W1, 'b1': b1, 'W2': W2, 'b2': b2}
    _L1_ffn_all = _L1_ffn_setup()
    _L1_ffn_in = {k: v for k, v in _L1_ffn_all.items() if k in ('Wr', 'br', 'W1', 'b1', 'W2', 'b2')}
    del _L1_ffn_all
    return {'x': x, 'ctx_768': ctx_768, 'L0_attn_Wq': _L0_attn_in['Wq'], 'L0_attn_bq': _L0_attn_in['bq'], 'L0_attn_Wk': _L0_attn_in['Wk'], 'L0_attn_bk': _L0_attn_in['bk'], 'L0_attn_Wv': _L0_attn_in['Wv'], 'L0_attn_bv': _L0_attn_in['bv'], 'L0_attn_Wo': _L0_attn_in['Wo'], 'L0_attn_bo': _L0_attn_in['bo'], 'L0_attn_W1': _L0_attn_in['W1'], 'L0_attn_b1': _L0_attn_in['b1'], 'L0_attn_W2': _L0_attn_in['W2'], 'L0_attn_b2': _L0_attn_in['b2'], 'L0_attn_g1': _L0_attn_in['g1'], 'L0_attn_be1': _L0_attn_in['be1'], 'L0_attn_g2': _L0_attn_in['g2'], 'L0_attn_be2': _L0_attn_in['be2'], 'L0_attn_gf': _L0_attn_in['gf'], 'L0_attn_bef': _L0_attn_in['bef'], 'L0_xattn_Wv': _L0_xattn_in['Wv'], 'L0_xattn_bv': _L0_xattn_in['bv'], 'L0_xattn_Wt': _L0_xattn_in['Wt'], 'L0_xattn_bt': _L0_xattn_in['bt'], 'L0_ffn_gate_w': _L0_ffn_in['gate_w'], 'L0_ffn_w0': _L0_ffn_in['w0'], 'L0_ffn_b0': _L0_ffn_in['b0'], 'L0_ffn_w1': _L0_ffn_in['w1'], 'L0_ffn_b1': _L0_ffn_in['b1'], 'L1_attn_in_proj_w': _L1_attn_in['in_proj_w'], 'L1_attn_in_proj_b': _L1_attn_in['in_proj_b'], 'L1_attn_conv_w': _L1_attn_in['conv_w'], 'L1_attn_conv_b': _L1_attn_in['conv_b'], 'L1_attn_x_proj_w': _L1_attn_in['x_proj_w'], 'L1_attn_dt_proj_w': _L1_attn_in['dt_proj_w'], 'L1_attn_dt_proj_b': _L1_attn_in['dt_proj_b'], 'L1_attn_out_proj_w': _L1_attn_in['out_proj_w'], 'L1_attn_out_proj_b': _L1_attn_in['out_proj_b'], 'L1_attn_A_log': _L1_attn_in['A_log'], 'L1_attn_D': _L1_attn_in['D'], 'L1_xattn_Wq': _L1_xattn_in['Wq'], 'L1_xattn_Wk': _L1_xattn_in['Wk'], 'L1_xattn_Wv': _L1_xattn_in['Wv'], 'L1_xattn_Wo': _L1_xattn_in['Wo'], 'L1_xattn_bo': _L1_xattn_in['bo'], 'L1_ffn_Wr': _L1_ffn_in['Wr'], 'L1_ffn_br': _L1_ffn_in['br'], 'L1_ffn_W1': _L1_ffn_in['W1'], 'L1_ffn_b1': _L1_ffn_in['b1'], 'L1_ffn_W2': _L1_ffn_in['W2'], 'L1_ffn_b2': _L1_ffn_in['b2']}

def reference(x, ctx_768, L0_attn_Wq, L0_attn_bq, L0_attn_Wk, L0_attn_bk, L0_attn_Wv, L0_attn_bv, L0_attn_Wo, L0_attn_bo, L0_attn_W1, L0_attn_b1, L0_attn_W2, L0_attn_b2, L0_attn_g1, L0_attn_be1, L0_attn_g2, L0_attn_be2, L0_attn_gf, L0_attn_bef, L0_xattn_Wv, L0_xattn_bv, L0_xattn_Wt, L0_xattn_bt, L0_ffn_gate_w, L0_ffn_w0, L0_ffn_b0, L0_ffn_w1, L0_ffn_b1, L1_attn_in_proj_w, L1_attn_in_proj_b, L1_attn_conv_w, L1_attn_conv_b, L1_attn_x_proj_w, L1_attn_dt_proj_w, L1_attn_dt_proj_b, L1_attn_out_proj_w, L1_attn_out_proj_b, L1_attn_A_log, L1_attn_D, L1_xattn_Wq, L1_xattn_Wk, L1_xattn_Wv, L1_xattn_Wo, L1_xattn_bo, L1_ffn_Wr, L1_ffn_br, L1_ffn_W1, L1_ffn_b1, L1_ffn_W2, L1_ffn_b2):
    import jax
    import jax.numpy as jnp

    def _L0_attn_ref(x, Wq, bq, Wk, bk, Wv, bv, Wo, bo, W1, b1, W2, b2, g1, be1, g2, be2, gf, bef):
        import jax, jax.numpy as jnp
        import numpy as np
        L, H, D_MODEL, D_FF = (4, 16, 256, 1024)
        HD = D_MODEL // H
        LN_EPS = 1e-05
        ATT_EPS = 1e-06
        CHUNK = 128

        def _ln(x, g, b):
            m = jnp.mean(x, axis=-1, keepdims=True)
            v = jnp.var(x, axis=-1, keepdims=True)
            return (x - m) * jax.lax.rsqrt(v + LN_EPS) * g + b

        def _feature_map(x):
            return jax.nn.elu(x) + 1.0

        def _causal_linear_attention(q, k, v):
            B, S, Hn, D = q.shape
            nC = S // CHUNK
            q = q.reshape(B, nC, CHUNK, Hn, D)
            k = k.reshape(B, nC, CHUNK, Hn, D)
            v = v.reshape(B, nC, CHUNK, Hn, D)
            KV = jnp.einsum('bnchd,bnche->bnhde', k, v)
            Ks = jnp.sum(k, axis=2)
            KVcum = jnp.cumsum(KV, axis=1) - KV
            Kcum = jnp.cumsum(Ks, axis=1) - Ks
            inter = jnp.einsum('bnchd,bnhde->bnche', q, KVcum)
            den_inter = jnp.einsum('bnchd,bnhd->bnch', q, Kcum)
            scores = jnp.einsum('bnchd,bnkhd->bnhck', q, k)
            mask = jnp.tril(jnp.ones((CHUNK, CHUNK), dtype=bool))
            scores = jnp.where(mask, scores, 0.0)
            intra = jnp.einsum('bnhck,bnkhe->bnche', scores, v)
            den_intra = jnp.transpose(jnp.sum(scores, axis=-1), (0, 1, 3, 2))
            out = (inter + intra) / (den_inter + den_intra + ATT_EPS)[..., None]
            return out.reshape(B, S, Hn, D)

        def _forward(x, Wq, bq, Wk, bk, Wv, bv, Wo, bo, W1, b1, W2, b2, g1, be1, g2, be2, gf, bef):
            B, S, Dm = x.shape
            for l in range(L):
                q = (x @ Wq[l] + bq[l]).reshape(B, S, H, HD)
                k = (x @ Wk[l] + bk[l]).reshape(B, S, H, HD)
                v = (x @ Wv[l] + bv[l]).reshape(B, S, H, HD)
                att = _causal_linear_attention(_feature_map(q), _feature_map(k), v)
                x = x + att.reshape(B, S, Dm) @ Wo[l] + bo[l]
                y = x = _ln(x, g1[l], be1[l])
                y = jax.nn.gelu(y @ W1[l] + b1[l], approximate=False)
                y = y @ W2[l] + b2[l]
                x = _ln(x + y, g2[l], be2[l])
            return _ln(x, gf, bef)
        return _forward(x, Wq, bq, Wk, bk, Wv, bv, Wo, bo, W1, b1, W2, b2, g1, be1, g2, be2, gf, bef)

    def _L0_xattn_ref(visual_features, text_features, Wv, bv, Wt, bt):
        import jax, jax.numpy as jnp
        import numpy as np
        EPS = 1e-08
        v = jnp.einsum('bsd,hd->bsh', visual_features, Wv) + bv
        t = jnp.einsum('bsd,hd->bsh', text_features, Wt) + bt
        dots = jnp.einsum('bih,bjh->bij', v, t)
        vn = jnp.linalg.norm(v, axis=-1)
        tn = jnp.linalg.norm(t, axis=-1)
        denom = jnp.maximum(vn[:, :, None] * tn[:, None, :], EPS)
        return dots / denom

    def _L0_ffn_ref(tokens, gate_w, w0, b0, w1, b1):
        import jax, jax.numpy as jnp
        import numpy as np
        B, S, D, E = (4, 1024, 256, 8)
        b, s, d = tokens.shape
        logits = jnp.einsum('bsd,de->bse', tokens, gate_w)
        weights = jax.nn.softmax(logits, axis=-1)
        topk_w, topk_idx = jax.lax.top_k(weights, 2)
        x = tokens.reshape(b * s, d)
        fw = topk_w.reshape(b * s, 2)
        fidx = topk_idx.reshape(b * s, 2)
        e0 = jax.nn.silu(x @ w0.T + b0)
        e1 = jax.nn.silu(x @ w1.T + b1)
        m0 = (fidx[:, 0:1] == 0).astype(x.dtype)
        m1 = (fidx[:, 1:2] == 1).astype(x.dtype)
        out = e0 * fw[:, 0:1] * m0 + e1 * fw[:, 1:2] * m1
        return out.reshape(b, s, d)

    def _L1_attn_ref(hidden_states, in_proj_w, in_proj_b, conv_w, conv_b, x_proj_w, dt_proj_w, dt_proj_b, out_proj_w, out_proj_b, A_log, D):
        import jax, jax.numpy as jnp
        import numpy as np
        from jax import lax
        D_MODEL = 256
        D_INNER = 512
        N_STATE = 16
        DT_RANK = 64
        K_CONV = 4
        SCALE_BITS = 15

        def _dyadic_scan(u_flat, decay_flat):
            B, L, F = u_flat.shape

            def step(h, xs):
                d_t, u_t = xs
                h = d_t * h + u_t
                return (h, h)
            h0 = jnp.zeros((B, F), dtype=u_flat.dtype)
            _, hs = lax.scan(step, h0, (decay_flat.transpose(1, 0, 2), u_flat.transpose(1, 0, 2)))
            return hs.transpose(1, 0, 2)
        Bsz, L, _ = hidden_states.shape
        projected = hidden_states @ in_proj_w.T + in_proj_b
        x, z = jnp.split(projected, 2, axis=-1)
        x_t = x.transpose(0, 2, 1)
        x_t = lax.conv_general_dilated(x_t, conv_w, window_strides=(1,), padding=[(K_CONV - 1, 0)], feature_group_count=D_INNER, dimension_numbers=('NCH', 'OIH', 'NCH'))
        x = (x_t + conv_b[None, :, None]).transpose(0, 2, 1)
        x = jax.nn.silu(x)
        x_dbl = x @ x_proj_w.T
        dt, Bc, Cc = jnp.split(x_dbl, [DT_RANK, DT_RANK + N_STATE], axis=-1)
        dt = jax.nn.softplus(dt @ dt_proj_w.T + dt_proj_b)
        A = -jnp.exp(A_log.astype(jnp.float32))
        dA = jnp.exp(jnp.einsum('bld,dn->bldn', dt, A))
        u = jnp.einsum('bld,bln->bldn', x, Bc) * dt[..., None]
        F = D_INNER * N_STATE
        u_flat = u.reshape(Bsz, L, F)
        dA_flat = dA.reshape(Bsz, L, F)
        scale = float(2 ** SCALE_BITS)
        decay_nums = jnp.clip(jnp.floor(dA_flat * scale), 0.0, 32767.0)
        decay = decay_nums / scale
        h_flat = _dyadic_scan(u_flat, decay)
        h = h_flat.reshape(Bsz, L, D_INNER, N_STATE)
        y = jnp.einsum('bldn,bln->bld', h, Cc)
        y = y + x * D
        y = y * jax.nn.silu(z)
        return y @ out_proj_w.T + out_proj_b

    def _L1_xattn_ref(x, context, Wq, Wk, Wv, Wo, bo):
        import jax, jax.numpy as jnp
        import numpy as np
        HEADS = 8
        DIM_HEAD = 64
        QUERY_DIM = 256
        CONTEXT_DIM = 192
        INNER = HEADS * DIM_HEAD
        B, Sq, _ = x.shape
        h, d = (HEADS, DIM_HEAD)
        scale = d ** (-0.5)
        q = (x @ Wq).reshape(B, Sq, h, d).transpose(0, 2, 1, 3)
        k = (context @ Wk).reshape(B, -1, h, d).transpose(0, 2, 1, 3)
        v = (context @ Wv).reshape(B, -1, h, d).transpose(0, 2, 1, 3)
        scores = jnp.einsum('bhid,bhjd->bhij', q, k) * scale
        attn = jax.nn.softmax(scores, axis=-1)
        out = jnp.einsum('bhij,bhjd->bhid', attn, v)
        out = out.transpose(0, 2, 1, 3).reshape(B, Sq, h * d)
        return out @ Wo + bo

    def _L1_ffn_ref(x, Wr, br, W1, b1, W2, b2):
        import jax, jax.numpy as jnp
        import numpy as np
        E = 8
        K = 2
        CAP_FACTOR = 1.0
        B, T, C = x.shape
        N = B * T
        xf = x.reshape(N, C)
        logits = xf @ Wr + br
        topv, topi = jax.lax.top_k(logits, K)
        gates = jax.nn.softmax(topv, axis=-1)
        rw = jnp.zeros((N, E), xf.dtype).at[jnp.arange(N)[:, None], topi].set(gates)
        cap = int(N * K / E * CAP_FACTOR)
        sel = jax.nn.one_hot(topi, E, dtype=jnp.int32).sum(1)
        rank = jnp.cumsum(sel, axis=0) - sel
        keep = (sel > 0) & (rank < cap)
        tok = jnp.broadcast_to(jnp.arange(N, dtype=jnp.int32)[:, None], (N, E))
        eid = jnp.broadcast_to(jnp.arange(E, dtype=jnp.int32)[None, :], (N, E))
        rank_c = jnp.where(keep, rank, cap)
        buf = jnp.full((E, cap), N, dtype=jnp.int32)
        buf = buf.at[eid, rank_c].set(tok, mode='drop')
        xpad = jnp.concatenate([xf, jnp.zeros((1, C), xf.dtype)], axis=0)
        xg = xpad[buf]
        h = jax.nn.gelu(jnp.einsum('ecd,edh->ech', xg, W1) + b1[:, None, :], approximate=False)
        out = jnp.einsum('ech,ehd->ecd', h, W2) + b2[:, None, :]
        rw_pad = jnp.concatenate([rw, jnp.zeros((1, E), rw.dtype)], axis=0)
        w = rw_pad[buf, jnp.arange(E, dtype=jnp.int32)[:, None]]
        weighted = out * w[..., None]
        final = jnp.zeros((N + 1, C), xf.dtype).at[buf.reshape(-1)].add(weighted.reshape(-1, C))
        return final[:N].reshape(B, T, C)
    x = x + _L0_attn_ref(_layernorm(x, axis=-1), L0_attn_Wq, L0_attn_bq, L0_attn_Wk, L0_attn_bk, L0_attn_Wv, L0_attn_bv, L0_attn_Wo, L0_attn_bo, L0_attn_W1, L0_attn_b1, L0_attn_W2, L0_attn_b2, L0_attn_g1, L0_attn_be1, L0_attn_g2, L0_attn_be2, L0_attn_gf, L0_attn_bef)
    x = x + _L0_xattn_ref(_layernorm(x, axis=-1), ctx_768, L0_xattn_Wv, L0_xattn_bv, L0_xattn_Wt, L0_xattn_bt)
    x = x + _L0_ffn_ref(_layernorm(x, axis=-1), L0_ffn_gate_w, L0_ffn_w0, L0_ffn_b0, L0_ffn_w1, L0_ffn_b1)
    x = x + _L1_attn_ref(_layernorm(x, axis=-1), L1_attn_in_proj_w, L1_attn_in_proj_b, L1_attn_conv_w, L1_attn_conv_b, L1_attn_x_proj_w, L1_attn_dt_proj_w, L1_attn_dt_proj_b, L1_attn_out_proj_w, L1_attn_out_proj_b, L1_attn_A_log, L1_attn_D)
    x = x + _L1_xattn_ref(_layernorm(x, axis=-1), ctx_768, L1_xattn_Wq, L1_xattn_Wk, L1_xattn_Wv, L1_xattn_Wo, L1_xattn_bo)
    x = x + _L1_ffn_ref(_layernorm(x, axis=-1), L1_ffn_Wr, L1_ffn_br, L1_ffn_W1, L1_ffn_b1, L1_ffn_W2, L1_ffn_b2)
    return x

_drawn_inputs = setup_inputs


def setup_inputs(seed=0):
    import zlib

    import numpy as np

    out = dict(_drawn_inputs(seed))
    spreads = {'L0_attn_bq': (0.0, 2.0),
     'L0_attn_bk': (0.0, 2.0),
     'L0_attn_bv': (0.0, 0.1),
     'L0_attn_bo': (0.0, 0.1),
     'L0_attn_b1': (0.0, 0.1),
     'L0_attn_b2': (0.0, 0.1),
     'L0_attn_g1': (1.0, 0.2),
     'L0_attn_be1': (0.0, 0.1),
     'L0_attn_g2': (1.0, 0.2),
     'L0_attn_be2': (0.0, 0.1),
     'L0_attn_gf': (1.0, 0.2),
     'L0_attn_bef': (0.0, 0.1),
     'L1_attn_D': (1.0, 0.6),
     'L1_ffn_br': (0.0, 2.0),
     'L1_ffn_b1': (0.0, 2.0),
     'L1_ffn_b2': (0.0, 0.8)}
    factors = {'L0_attn_Wq': 64.0,
     'L0_attn_Wk': 43.772,
     'L0_xattn_bv': 37.167,
     'L0_xattn_bt': 59.228,
     'L0_ffn_b0': 64.0,
     'L0_ffn_w1': 2.696,
     'L0_ffn_b1': 64.0,
     'L1_attn_in_proj_b': 8.0,
     'L1_attn_conv_w': 2.725,
     'L1_attn_conv_b': 3.311,
     'L1_attn_x_proj_w': 8.0,
     'L1_attn_dt_proj_w': 8.0,
     'L1_attn_dt_proj_b': 8.0,
     'L1_attn_out_proj_b': 31.416,
     'L1_attn_A_log': 8.0,
     'L1_xattn_bo': 64.0,
     'L1_xattn_Wq': 8.0,
     'L1_xattn_Wk': 8.0,
     'L1_xattn_Wv': 8.0,
     'L1_xattn_Wo': 8.0,
     'L1_ffn_Wr': 8.0,
     'L1_ffn_W1': 8.0,
     'L1_ffn_W2': 8.0}
    for name, (base, spread) in spreads.items():
        noise = np.random.default_rng([zlib.crc32(name.encode()), seed]).standard_normal(out[name].shape)
        drawn = base * np.exp(spread * noise) if base else spread * noise
        out[name] = jnp.asarray(drawn.astype(out[name].dtype))
    for name, factor in factors.items():
        out[name] = (out[name] * factor).astype(out[name].dtype)
    return out
```

```python
import numpy as np
import concourse.bass as bass
from concourse import mybir
from contextlib import ExitStack

F32 = mybir.dt.float32
I32 = mybir.dt.int32
ALU = mybir.AluOpType
ACT = mybir.ActivationFunctionType
AX = mybir.AxisListType.X

P = 128
B, S, D = 8, 256, 256
N = B * S
NT = N // P
KC = D // P
PAIRS = B // 2
TT = 4
W = TT * P
L, H, HD, FF = 4, 16, 16, 1024
FM = FF // P
VA = HD + 1
LN_EPS, ATT_EPS = 1e-5, 1e-6

HX, CT, E0 = 128, 192, 8
DI, NS, DTR, KCONV = 512, 16, 64, 4
IC = DI // P
NG = 4
QH, QD = 8, 64
QI = QH * QD
QC = QI // P
NE, EF, CAP = 8, 1024, N * 2 // 8
SIM_EPS = 1e-8
DECAY_TOP = 1.0 - 2.0 ** -24
DECAY_HALF = -2.0 ** -16
DECAY_GRID = 384.0
LEAST = 2.0 ** -24
SCALE = QD ** -0.5

DVE_STEPS, ACT_STEPS = 117, 1

C_ID, C_TRI, C_STRICT, C_ONES, C_BD = 0, 128, 256, 384, 512
C_EVEN = C_BD + KC * H * VA
C_ODD, C_MHALF, C_SLOT = C_EVEN + 1, C_EVEN + 2, C_EVEN + 6
C_ALL = C_SLOT + 8


def shape_constants():
    c = np.zeros((P, C_ALL), np.float32)
    i = np.arange(P)
    c[:, C_ID:C_ID + P] = np.eye(P)
    c[:, C_TRI:C_TRI + P] = i[None, :] >= i[:, None]
    c[:, C_STRICT:C_STRICT + P] = i[None, :] > i[:, None]
    c[:, C_ONES:C_ONES + P] = 1.0
    for m in range(KC):
        head = (m * P + i) // HD
        same = head[:, None] == (np.arange(H * VA) // VA)[None, :]
        c[:, C_BD + m * H * VA:C_BD + (m + 1) * H * VA] = same
    c[:, C_EVEN] = (i // HD) % 2 == 0
    c[:, C_ODD] = (i // HD) % 2 == 1
    c[:, C_MHALF:C_MHALF + 4] = -0.5
    c[:, C_SLOT:C_SLOT + 8] = 512.0 * np.arange(8)
    return c


class Steps:

    def __init__(self, eng, sem):
        self.eng, self.sem, self.base, self.n = eng, sem, 0, 0

    def loop(self, it, per):
        self.start, self.per, self.n = self.base + self.n, per, 0
        self.base = self.start + it * per

    def end_loop(self, times):
        assert self.n == self.per, (self.n, self.per)
        self.base, self.n = self.start + times * self.per, 0

    def after(self, ins):
        self.n += 1
        ins.then_inc(self.sem, 1)
        self.eng.wait_ge(self.sem, self.base + self.n)

    def apart(self, ins):
        self.n += 1
        ins.then_inc(self.sem, 1)
        hold(self.eng, self.sem, self.base + self.n)


def hold(eng, sem, value):
    eng.wait_ge(sem, value)
    eng.sem_inc(HELD[0], 1)


HELD = [None]


class Arena:

    def __init__(self, tile, at):
        self.tile, self.at, self.top = tile, at, at

    def __call__(self, *shape, rows=P):
        n = int(np.prod(shape))
        part = self.tile[0:rows, self.at:self.at + n]
        self.at += n
        if len(shape) == 2:
            part = part.rearrange("p (a b) -> p a b", a=shape[0])
        elif len(shape) == 3:
            part = part.rearrange("p (a b c) -> p a b c", a=shape[0], b=shape[1])
        return part


def decoder(nc, t, out):
    ctx = ExitStack()

    def sem(name):
        return ctx.enter_context(nc.semaphore(name))

    ts = bass.ts

    ARENA = 51 * 1024
    arena = ctx.enter_context(nc.sbuf_tensor("arena", [P, ARENA], F32))
    keep = Arena(arena, 0)
    xst = keep(NT, D)
    hst = keep(NT, D)
    const = keep(C_ALL)
    stats, mv, ve, rstd = keep(TT, 6), keep(TT, 2), keep(TT), keep(TT)
    lgall = keep(NT, 8)
    vecs = keep(7, D)
    ident, tri = const[:, C_ID:C_ID + P], const[:, C_TRI:C_TRI + P]
    strict, ones = const[:, C_STRICT:C_STRICT + P], const[:, C_ONES:C_ONES + P]
    mhalf, slot0 = const[:, C_MHALF:C_MHALF + TT], const[:, C_SLOT:C_SLOT + 8]

    def head_mask(m):
        return const[:, C_BD + m * H * VA:C_BD + (m + 1) * H * VA]

    PHASE = keep.at

    a = Arena(arena, PHASE)
    wq, wk, wv, wo = a(KC, D), a(KC, D), a(KC, D), a(KC, D)
    w1, w2 = a(KC, FF), a(FM, D)
    qkb, qkb1 = a(2 * KC), a(2 * KC)
    b1 = a(FM)
    hbuf, hT = a(TT, D), a(KC, W)
    expq = a(2 * KC, W)
    qf, kf, kE, kO = a(KC, W), a(KC, W), a(KC, W), a(KC, W)
    vaug, ktok = a(TT, H, VA), a(2, D)
    kvm = a(2, KC, H * VA)
    scm = a(8, TT, P)
    den = a(TT, H)
    att, attT = a(TT, D), a(KC, W)
    xb, r1, y, yb = a(TT, D), a(TT, D), a(TT, D), a(TT, D)
    yT, gT = a(KC, W), a(FM, W)
    zero = a(2048)
    assert a.at <= ARENA, a.at

    a = Arena(arena, PHASE)
    w_sv, w_st = a(KC, HX), a(2, HX)
    w_gate, w_pair = a(KC, E0), a(KC, 2 * D)
    w_in, w_xp, w_dt, w_out = a(KC, 2 * DI), a(IC, DTR + 2 * NS), a(DI, rows=DTR), a(IC, D)
    w_q, w_k, w_v, w_o = a(KC, QI), a(2, QI), a(2, QI), a(QC, D)
    w_r = a(KC, NE)
    cols = a(2 + 2 * IC + IC * KCONV + 3 * IC)
    sim_b, in_b = cols[:, 0:2], cols[:, 2:2 + 2 * IC]
    cw = cols[:, 10:10 + IC * KCONV].rearrange("p (c k) -> p c k", c=IC)
    conv_b, dt_b, skip = cols[:, 26:30], cols[:, 30:34], cols[:, 34:38]
    rows2 = a(4 * D + 2 * D + NE)
    r_gf, r_bef, r_out, r_xo = (rows2[:, i * D:(i + 1) * D] for i in range(4))
    r_pair, r_r = rows2[:, 4 * D:6 * D], rows2[:, 6 * D:6 * D + NE]
    acol = a(IC, NS)
    xc, xn, xnT = a(TT, D), a(TT, D), a(KC, W)
    ctxT = a(2, W)
    STAGE = a.at
    vT, tT, vsq, tsq, tn, vn, dn = a(W), a(W), a(W), a(W), a(W), a(TT), a(TT, D)
    a = Arena(arena, STAGE)
    lg, gmax, gsum, cmp8, cnt2, coef = a(TT, E0), a(TT), a(TT), a(TT, E0), a(2, TT), a(2, TT)
    eb = a(TT, 2 * D)
    a = Arena(arena, STAGE)
    zs, xs, dt, dtx = a(IC, W), a(IC, W), a(IC, W), a(IC, W)
    dtr, bc = a(W, rows=DTR), a(W, rows=2 * NS)
    Bs, Cs = [a(NG, W) for _ in range(2)], [a(NG, W) for _ in range(2)]
    dA = [a(NG, W) for _ in range(2)]
    uh = [a(NG, W) for _ in range(2)]
    dA_all = arena[:, a.at - 4 * NG * W:a.at - 2 * NG * W]
    xpad = dA_all[:, 0:IC * 2 * (S + 3)].rearrange("p (c s t) -> p c s t", c=IC, s=2)
    assert IC * 2 * (S + 3) <= 2 * NG * W
    soft_e, soft_l, soft_d = dA[0], dA[1], uh[0]
    assert a.at <= ARENA, a.at
    a = Arena(arena, STAGE)
    qT, kT, vv = a(QC, W), a(QC, W), a(TT, QI)
    mx, nm, sm = a(4, 2), a(4, 2), a(TT, QH)
    pexp, pT = [a(2, S) for _ in range(2)], [a(4, P) for _ in range(2)]
    at2, at2T = [a(QI) for _ in range(2)], [a(QC, P) for _ in range(2)]

    a = Arena(arena, STAGE)
    cmp3, cnt, sel, top = a(NT, NE), a(NT, NE), a(NT, NE), [a(NT, NE) for _ in range(2)]
    picked, before, rank = a(NT, NE), a(NT, NE), a(NT, NE)
    lt, gate, rk, base, over, place = ([a(NT) for _ in range(2)] for _ in range(6))
    gexp = a(NT)
    into = [a(NT).bitcast(I32) for _ in range(2)]
    outof = [a(NT).bitcast(I32) for _ in range(2)]
    weights_at = a.at
    w1e, w2e = [a(KC, EF) for _ in range(2)], [a(EF // P, D) for _ in range(2)]
    b1e, b2e = [a(EF // P) for _ in range(2)], [a(D) for _ in range(2)]
    xg, xgT, gTe, ye = [a(TT, D) for _ in range(2)], a(KC, W), a(EF // P, W), [a(TT, D) for _ in range(2)]
    back = arena[:, weights_at:weights_at + 2 * NT * D].rearrange("p (i d) -> p i d", d=D)
    assert a.at <= ARENA, a.at
    rows_to = nc.dram_tensor("rows_to_experts", (NE * CAP, D), F32, kind="Internal").ap()
    rows_back = nc.dram_tensor("rows_from_experts", (NE * CAP, D), F32, kind="Internal").ap()

    pa = [ctx.enter_context(nc.psum_tensor(f"pa{i}", [P, 512], F32)) for i in range(4)]
    pt = [ctx.enter_context(nc.psum_tensor(f"pt{i}", [P, 512], F32)) for i in range(2)]
    po = [ctx.enter_context(nc.psum_tensor(f"po{i}", [P, 512], F32)) for i in range(2)]

    const_in, x_in = sem("const_in"), [sem(f"x_in{p}") for p in range(PAIRS)]
    attn_w_in, ffn_w_in, rows_in = sem("attn_w_in"), sem("ffn_w_in"), sem("rows_in")
    dve_step, pool_step, act_step = sem("dve_step"), sem("pool_step"), sem("act_step")
    var_ready, rstd_ready = sem("var_ready"), sem("rstd_ready")
    h_ready, hbuf_ready, xb_ready = sem("h_ready"), sem("hbuf_ready"), sem("xb_ready")
    tr_done, tr_out = sem("tr_done"), sem("tr_out")
    qk_done, min_ready, exp_ready = sem("qk_done"), sem("min_ready"), sem("exp_ready")
    qf_ready, kf_ready, keo_ready = sem("qf_ready"), sem("kf_ready"), sem("keo_ready")
    v_done, vaug_ready = sem("v_done"), sem("vaug_ready")
    kv_done, kvm_ready = sem("kv_done"), sem("kvm_ready")
    sc_done, scm_ready, av_done, att_ready = sem("sc_done"), sem("scm_ready"), sem("av_done"), sem("att_ready")
    wo_done, r1_ready, y_ready, yb_ready = sem("wo_done"), sem("r1_ready"), sem("y_ready"), sem("yb_ready")
    up_done, gelu_ready, down_done = sem("up_done"), sem("gelu_ready"), sem("down_done")
    zero_ready, zeroed = sem("zero_ready"), sem("zeroed")
    out_done = sem("out_done")
    w_in_2, ctx_in, a_exp, a_ready = sem("w_in_2"), sem("ctx_in"), sem("a_exp"), sem("a_ready")
    xn_ready, xc_ready, x_kept, xf_kept = sem("xn_ready"), sem("xc_ready"), sem("x_kept"), sem("xf_kept")
    tr2_done, tr2_out = sem("tr2_done"), sem("tr2_out")
    vt_done, vt_ready, nrm_done, nrm_ready, dots_done = (sem(n) for n in ("vt_done", "vt_ready", "nrm_done", "nrm_ready", "dots_done"))
    gate_done, gl_ready, ge_ready, pair_done, eb_ready, sil_ready = (
        sem(n) for n in ("gate_done", "gl_ready", "ge_ready", "pair_done", "eb_ready", "sil_ready"))
    in_done, in_out, conv_ready, xs_ready, xp_done, xp_out = (
        sem(n) for n in ("in_done", "in_out", "conv_ready", "xs_ready", "xp_done", "xp_out"))
    dtp_done, soft_ready, dt_ready, bc_done, bc_out = (sem(n) for n in ("dtp_done", "soft_ready", "dt_ready", "bc_done", "bc_out"))
    da_ready, scan_done, hc_ready, ysum_done, yg_ready, proj_done = (
        sem(n) for n in ("da_ready", "scan_done", "hc_ready", "ysum_done", "yg_ready", "proj_done"))
    qkv_done, qkv_out, s2_done, nm_ready, pexp_ready = (sem(n) for n in ("qkv_done", "qkv_out", "s2_done", "nm_ready", "pexp_ready"))
    pT_done, pT_out, av2_done, at2_ready, wo2_done = (sem(n) for n in ("pT_done", "pT_out", "av2_done", "at2_ready", "wo2_done"))
    route_done, wo2_out = sem("route_done"), sem("wo2_out")
    soft_e_ready, soft_u_ready = sem("soft_e_ready"), sem("soft_u_ready")

    logits_ready, sel_ready, rank_done, lt_ready, gexp_ready, places_ready = (
        sem(n) for n in ("logits_ready", "sel_ready", "rank_done", "lt_ready", "gexp_ready", "places_ready"))
    scattered, tr3_done, tr3_out, up3_done, gelu3_ready = (sem(n) for n in ("scattered", "tr3_done", "tr3_out", "up3_done", "gelu3_ready"))
    we_in, xg_in, down3_done, ye_ready, ye_kept = ([sem(f"{n}{j}") for j in range(2)] for n in ("we_in", "xg_in", "down3_done", "ye_ready", "ye_kept"))
    back_in, final_ready = [sem(f"back_in{p}") for p in range(PAIRS)], sem("final_ready")
    HELD[0] = sem("held")
    V_BV, V_BO, V_G1, V_BE1, V_B2, V_G2, V_BE2 = range(7)
    LAYERS_DONE = 2 * PAIRS * (L + 1)
    W2_IN = 16 * (9 + 6 + 4)
    GROUPS = 2 * PAIRS + 4 * L * PAIRS
    TR2, XN = 14, 5

    def row(i, n):
        return vecs[:, i, :].unsqueeze(1).broadcast_to([P, n, D])

    def two(tile, s):
        return tile[:, 2 * s:2 * s + 2, :]

    block = ctx.enter_context(nc.Block())

    @block.sync
    def _(sp):
        sp.dma_start(const, t["consts"]).then_inc(const_in, 16)
        for p in range(PAIRS):
            sp.dma_start(xst[:, TT * p:TT * p + TT, :],
                         t["x"][p * W:(p + 1) * W, :].rearrange("(t p) d -> p t d", p=P)).then_inc(x_in[p], 16)
        sp.wait_ge(zero_ready, 1)
        for q in range(4):
            sp.dma_start(rows_to.rearrange("(q p r) d -> q p (r d)", q=4, p=P)[q], zero).then_inc(zeroed, 16)
        with sp.Fori(0, L) as l:
            sp.wait_ge(wo_done, l * (2 * PAIRS))
            for tile, name in ((wq, "L0_attn_Wq"), (wk, "L0_attn_Wk"), (wv, "L0_attn_Wv"), (wo, "L0_attn_Wo")):
                sp.dma_start(tile, t[name][l].rearrange("(k p) n -> p k n", p=P)).then_inc(attn_w_in, 16)
            sp.dma_start(qkb, t["qk_bias"][l]).then_inc(attn_w_in, 16)
            sp.wait_ge(h_ready, 2 * PAIRS + l * (2 * PAIRS))
            sp.dma_start(vecs, t["rows"][l].partition_broadcast(P)).then_inc(rows_in, 16)
            sp.wait_ge(down_done, l * (2 * PAIRS))
            sp.dma_start(w1, t["L0_attn_W1"][l].rearrange("(k p) n -> p k n", p=P)).then_inc(ffn_w_in, 16)
            sp.dma_start(b1, t["b1_cols"][l]).then_inc(ffn_w_in, 16)
            sp.dma_start(w2, t["L0_attn_W2"][l].rearrange("(m p) n -> p m n", p=P)).then_inc(ffn_w_in, 16)
        sp.wait_ge(h_ready, LAYERS_DONE)
        n_w2 = 0
        for dst, name in ((w_sv, "sim_wv"), (w_gate, "gate"), (w_pair, "pair_w"), (w_in, "ssm_in"), (w_xp, "ssm_xp"),
                          (w_out, "ssm_out"), (w_q, "L1_xattn_Wq"), (w_o, "L1_xattn_Wo"), (w_r, "L1_ffn_Wr")):
            sp.dma_start(dst, t[name].rearrange("(k p) n -> p k n", p=P)).then_inc(w_in_2, 16)
            n_w2 += 16
        for dst, name in ((w_st, "sim_wt"), (w_k, "L1_xattn_Wk"), (w_v, "L1_xattn_Wv")):
            sp.dma_start(dst[:, 0, :], t[name][0:P, :]).then_inc(w_in_2, 16)
            sp.dma_start(dst[0:CT - P, 1, :], t[name][P:CT, :]).then_inc(w_in_2, 16)
            n_w2 += 32
        sp.dma_start(w_dt, t["ssm_dt"]).then_inc(w_in_2, 16)
        sp.dma_start(cols, t["cols"]).then_inc(w_in_2, 16)
        sp.dma_start(rows2, t["rows2"].partition_broadcast(P)).then_inc(w_in_2, 16)
        sp.dma_start(acol, t["a_log"]).then_inc(w_in_2, 16)
        assert n_w2 + 64 == W2_IN
        with sp.Fori(0, PAIRS) as p:
            sp.wait_ge(qkv_done, 12 * p)
            sp.dma_start(ctxT[:, 0, :], t["ctxT"][0:P, ts(p, W)]).then_inc(ctx_in, 16)
            sp.dma_start(ctxT[0:CT - P, 1, :], t["ctxT"][P:CT, ts(p, W)]).then_inc(ctx_in, 16)
        sp.wait_ge(logits_ready, PAIRS)
        for first in (True, False):
            if first:
                loads = ExitStack()
                q = 0
            else:
                loads = sp.Fori(1, NE // 2)
            with loads as at:
                q = 0 if first else at
                for j in range(2):
                    if not first:
                        sp.wait_ge(ye_ready[j], 2 * q)
                    e = 2 * q + j
                    sp.dma_start(w1e[j], t["L1_ffn_W1"][e].rearrange("(k p) n -> p k n", p=P)).then_inc(we_in[j], 16)
                    sp.dma_start(b1e[j], t["b1e_cols"][e]).then_inc(we_in[j], 16)
                    sp.dma_start(w2e[j], t["L1_ffn_W2"][e].rearrange("(m p) n -> p m n", p=P)).then_inc(we_in[j], 16)
                    sp.dma_start(b2e[j], t["L1_ffn_b2"][e].partition_broadcast(P)).then_inc(we_in[j], 16)
                    if first and j == 0:
                        sp.wait_ge(scattered, 16 * 2 * NT)
                    sp.dma_start(xg[j], rows_to[ts(e, CAP), :].rearrange("(t p) d -> p t d", p=P)).then_inc(xg_in[j], 16)
        for p in range(PAIRS):
            sp.wait_ge(final_ready, TT * p + TT)
            sp.dma_start(out[p * W:(p + 1) * W, :].rearrange("(t p) d -> p t d", p=P), xst[:, TT * p:TT * p + TT, :]).then_inc(out_done, 16)
        sp.wait_ge(out_done, 16 * PAIRS)
    @block.gpsimd
    def _(pool):
        step = Steps(pool, pool_step)

        def deviations(n, c, k):
            hold(pool, var_ready, n)
            step.apart(nc.gpsimd.tensor_scalar(ve[:, c:c + k], mv[:, c:c + k, 1], LN_EPS, None, ALU.add))
            nc.gpsimd.tensor_tensor(rstd[:, c:c + k], ve[:, c:c + k], mhalf[:, 0:k], ALU.pow).then_inc(rstd_ready, 1)

        nc.gpsimd.memset(zero, 0.0).then_inc(zero_ready, 1)
        hold(pool, const_in, 16)
        with pool.Fori(0, PAIRS) as p:
            step.loop(p, 2)
            for s in range(2):
                deviations(2 * p + s + 1, 2 * s, 2)
            step.end_loop(PAIRS)
        with pool.Fori(0, L) as l:
            with pool.Fori(0, PAIRS) as p:
                it = l * PAIRS + p
                step.loop(it, 4)
                hold(pool, h_ready, 2 * it + 2)
                hold(pool, tr_done, 8 * it)
                nc.gpsimd.tensor_copy(hbuf, hst[:, ts(p, TT), :]).then_inc(hbuf_ready, 1)
                hold(pool, rows_in, 16 * l + 16)
                hold(pool, r1_ready, 2 * it)
                nc.gpsimd.tensor_tensor(xb, hst[:, ts(p, TT), :], row(V_BO, TT), ALU.add).then_inc(xb_ready, 1)
                for s in range(2):
                    deviations(2 * PAIRS + 4 * it + s + 1, 2 * s, 2)
                for s in range(2):
                    hold(pool, y_ready, 2 * it + s + 1)
                    nc.gpsimd.tensor_tensor(two(yb, s), two(y, s), row(V_B2, 2), ALU.add).then_inc(yb_ready, 1)
                for s in range(2):
                    deviations(2 * PAIRS + 4 * it + 2 + s + 1, 2 * s, 2)
                step.end_loop(L * PAIRS)
        with pool.Fori(0, PAIRS) as p:
            step.loop(p, 6)
            for k in range(5):
                deviations(GROUPS + 6 * p + k + 1, 0, TT)
            hold(pool, xc_ready, p + 1)
            nc.gpsimd.tensor_copy(xst[:, ts(p, TT), :], xc).then_inc(x_kept, 1)
            deviations(GROUPS + 6 * p + 6, 0, TT)
            hold(pool, xn_ready, XN * p + XN)
            nc.gpsimd.tensor_copy(hst[:, ts(p, TT), :], xn).then_inc(xf_kept, 1)
            step.end_loop(PAIRS)
        pool.wait_ge(zeroed, 16 * 4)
        pool.wait_ge(places_ready, 1)
        pool.wait_ge(xf_kept, PAIRS)
        for i in range(NT):
            for k in range(2):
                nc.gpsimd.indirect_dma_start(
                    out=rows_to, out_offset=bass.IndirectOffsetOnAxis(ap=into[k][:, i:i + 1], axis=0), in_=hst[:, i, :], in_offset=None,
                    bounds_check=NE * CAP - 1, oob_is_err=False).then_inc(scattered, 16)
        with pool.Fori(0, NE // 2) as q:
            for j in range(2):
                hold(pool, ye_ready[j], 2 * q + 2)
                nc.gpsimd.dma_start(rows_back[ts(2 * q + j, CAP), :].rearrange("(t p) d -> p t d", p=P), ye[j]).then_inc(ye_kept[j], 16)
        for j in range(2):
            pool.wait_ge(ye_kept[j], 16 * (NE // 2))
        for i in range(NT):
            for k in range(2):
                nc.gpsimd.indirect_dma_start(
                    out=back[:, 2 * i + k, :], out_offset=None, in_=rows_back,
                    in_offset=bass.IndirectOffsetOnAxis(ap=outof[k][:, i:i + 1], axis=0),
                    bounds_check=NE * CAP - 1, oob_is_err=False).then_inc(back_in[i // TT], 16)

    @block.scalar
    def _(act):
        def evacuate(n, dst, src):
            act.wait_ge(tr_done, n)
            nc.scalar.copy(dst, src).then_inc(tr_out, 1)

        with act.Fori(0, L) as l:
            with act.Fori(0, PAIRS) as p:
                it = l * PAIRS + p
                for k in range(KC):
                    evacuate(8 * it + k + 1, hT[:, k, :], pt[k][:, :])
                for j in range(2 * KC):
                    act.wait_ge(min_ready, 4 * it + j + 1)
                    nc.scalar.activation(expq[:, j, :], expq[:, j, :], ACT.Exp).then_inc(exp_ready, 1)
                for s in range(2):
                    evacuate(8 * it + 2 + s + 1, ktok[:, s, :], pt[s][:, 0:D])
                for s in range(2):
                    evacuate(8 * it + 4 + s + 1, attT[:, :, s * S:(s + 1) * S],
                             pt[s][:, :].rearrange("p (k t) -> p k t", k=KC))
                for s in range(2):
                    evacuate(8 * it + 6 + s + 1, yT[:, :, s * S:(s + 1) * S],
                             pt[s][:, :].rearrange("p (k t) -> p k t", k=KC))
                act.wait_ge(ffn_w_in, 48 * l + 48)
                for m in range(FM):
                    act.wait_ge(up_done, FM * it + m + 1)
                    nc.scalar.activation(gT[:, m, :], pa[m % 4][:, :], ACT.Gelu, bias=b1[:, m:m + 1]).then_inc(gelu_ready, 1)
        a_ = nc.scalar.activation
        step = Steps(act, act_step)
        act.wait_ge(w_in_2, W2_IN)
        a_(acol, acol, ACT.Exp).then_inc(a_exp, 1)
        with act.Fori(0, PAIRS) as p:
            step.loop(p, ACT_STEPS)

            def input_transposed(k):
                for s in range(2):
                    act.wait_ge(tr2_done, TR2 * p + k + s + 1)
                    nc.scalar.copy(xnT[:, :, s * S:(s + 1) * S], pt[s][:, :].rearrange("p (k t) -> p k t", k=KC)).then_inc(tr2_out, 1)

            input_transposed(0)
            for i, (full, square) in enumerate(((vT, vsq), (tT, tsq))):
                act.wait_ge(vt_done, 2 * p + i + 1)
                a_(full, pa[i][:, :], ACT.Identity, bias=sim_b[:, i:i + 1]).then_inc(vt_ready, 1)
                a_(square, pa[i][:, :], ACT.Square, bias=sim_b[:, i:i + 1]).then_inc(vt_ready, 1)
            act.wait_ge(nrm_done, p + 1)
            a_(vn, pa[2][:, 0:TT], ACT.Sqrt).then_inc(nrm_ready, 1)
            a_(tn, pa[3][:, :], ACT.Sqrt).then_inc(nrm_ready, 1)

            input_transposed(2)
            act.wait_ge(gl_ready, p + 1)
            a_(lg, lg, ACT.Exp).then_inc(ge_ready, 1)
            for i in range(TT):
                act.wait_ge(eb_ready, TT * p + i + 1)
                a_(eb[:, i, :], eb[:, i, :], ACT.Silu).then_inc(sil_ready, 1)

            input_transposed(4)
            for m in range(2 * IC):
                act.wait_ge(in_done, 8 * p + m + 1)
                if m < IC:
                    a_(xpad[:, m, :, 3:3 + S], pa[m % 4][:, :].rearrange("p (s t) -> p s t", s=2), ACT.Identity,
                       bias=in_b[:, m:m + 1]).then_inc(in_out, 1)
                else:
                    a_(zs[:, m - IC, :], pa[m % 4][:, :], ACT.Silu, bias=in_b[:, m:m + 1]).then_inc(in_out, 1)
            for c in range(IC):
                act.wait_ge(conv_ready, IC * p + c + 1)
                a_(xs[:, c, :], xs[:, c, :], ACT.Silu).then_inc(xs_ready, 1)
            act.wait_ge(xp_done, 2 * p + 2)
            nc.scalar.copy(dtr, pa[0][0:DTR, :]).then_inc(xp_out, 1)
            nc.scalar.copy(bc, pa[1][0:2 * NS, :]).then_inc(xp_out, 1)
            for c in range(IC):
                act.wait_ge(dtp_done, IC * p + c + 1)
                a_(soft_e[:, c, :], pa[c][:, :], ACT.Abs, bias=dt_b[:, c:c + 1])
                last = a_(dt[:, c, :], pa[c][:, :], ACT.Relu, bias=dt_b[:, c:c + 1])
            step.after(last)
            a_(soft_e, soft_e, ACT.Exp, scale=-1.0).then_inc(soft_e_ready, 1)
            act.wait_ge(soft_u_ready, p + 1)
            a_(soft_l, soft_d, ACT.Ln).then_inc(soft_ready, 1)

            def rows_spread(g):
                for n in range(NG):
                    for which, (src, dst) in enumerate(((pt, Bs), (po, Cs))):
                        act.wait_ge(bc_done, 32 * p + 8 * g + 2 * n + which + 1)
                        if n == 0 and which == 0 and g >= 2:
                            act.wait_ge(hc_ready, 16 * p + 4 * (g - 1))
                        nc.scalar.copy(dst[g % 2][:, n, :], src[n % 2][:, :]).then_inc(bc_out, 1)

            rows_spread(0)
            act.wait_ge(dt_ready, p + 1)
            for i in range(4 * IC):
                g, c = i // IC, i % IC
                if c == 2 and g + 1 < NS // NG:
                    rows_spread(g + 1)
                if i >= 2:
                    act.wait_ge(scan_done, 16 * p + i - 1)
                for n in range(NG):
                    last = a_(dA[i % 2][:, n, :], dt[:, c, :], ACT.Exp, scale=acol[:, c, NG * g + n:NG * g + n + 1])
                last.then_inc(da_ready, 1)

            input_transposed(6)
            for r in range(12):
                act.wait_ge(qkv_done, 12 * p + r + 1)
                nc.scalar.copy((qT, kT, vv)[r // 4][:, r % 4, :], pa[r % 4][:, :]).then_inc(qkv_out, 1)
            for u in range(16 + 4):
                if u < 16:
                    tile, h0 = u // 4, 4 * (u % 4 // 2) + u % 2
                    act.wait_ge(nm_ready, 16 * p + u + 1)
                    if u >= 2:
                        act.wait_ge(pT_done, 16 * p + u - 1)
                    for b in range(2):
                        last = a_(pexp[u % 2][:, b, :], pa[u % 2][:, b * S:(b + 1) * S], ACT.Exp, bias=nm[:, u % 4, b:b + 1], scale=SCALE,
                                  accum_out=sm[:, tile, h0 + 2 * b:h0 + 2 * b + 1])
                    last.then_inc(pexp_ready, 1)
                if u >= 7 and (u - 7) % 4 == 0:
                    tile = (u - 7) // 4
                    act.wait_ge(tr2_done, TR2 * p + 8 + tile + 1)
                    nc.scalar.copy(at2T[tile % 2], pt[tile % 2][:, :].rearrange("p (k t) -> p k t", k=QC)).then_inc(tr2_out, 1)
            input_transposed(12)
            step.end_loop(PAIRS)
        act.wait_ge(lt_ready, 1)
        a_(gexp, gexp, ACT.Exp).then_inc(gexp_ready, 1)
        with act.Fori(0, NE // 2) as q:
            for j in range(2):
                for s in range(2):
                    act.wait_ge(tr3_done, 4 * q + 2 * j + s + 1)
                    nc.scalar.copy(xgT[:, :, s * S:(s + 1) * S], pt[s][:, :].rearrange("p (k t) -> p k t", k=KC)).then_inc(tr3_out, 1)
                act.wait_ge(we_in[j], 64 * q + 64)
                for m in range(EF // P):
                    act.wait_ge(up3_done, 16 * q + 8 * j + m + 1)
                    a_(gTe[:, m, :], pa[m % 4][:, :], ACT.Gelu, bias=b1e[j][:, m:m + 1]).then_inc(gelu3_ready, 1)

    @block.vector
    def _(dve):
        step = Steps(dve, dve_step)
        v = nc.vector

        def normalise(n, c, src, dst):
            for i, one in enumerate(src):
                last = v.bn_stats(out=stats[:, c + i, :], in_=one)
            step.apart(last)
            for i in range(len(src)):
                last = v.bn_aggr(out=mv[:, c + i, :], in_=stats[:, c + i, :])
            last.then_inc(var_ready, 1)
            dve.wait_ge(rstd_ready, n)
            for i, one in enumerate(src):
                last = v.tensor_scalar(dst[i], one, mv[:, c + i, 0:1], rstd[:, c + i:c + i + 1], ALU.subtract, ALU.mult)
            return last

        last = v.memset(vaug, 1.0)
        step.after(last)
        dve.wait_ge(const_in, 16)
        for p in range(PAIRS):
            dve.wait_ge(x_in[p], 16)
        with dve.Fori(0, PAIRS) as p:
            step.loop(p, 2)
            for s in range(2):
                at = [bass.ds(p * TT + 2 * s + i, 1) for i in range(2)]
                normalise(2 * p + s + 1, 2 * s, [xst[:, j, :].rearrange("p a d -> p (a d)") for j in at],
                          [hst[:, j, :].rearrange("p a d -> p (a d)") for j in at]).then_inc(h_ready, 1)
            step.end_loop(PAIRS)
        with dve.Fori(0, L) as l:
            with dve.Fori(0, PAIRS) as p:
                it = l * PAIRS + p
                step.loop(it, 23)
                dve.wait_ge(attn_w_in, 80 * l + 80)
                step.after(v.tensor_scalar(qkb1, qkb, 1.0, None, ALU.add))
                for j in range(2 * KC):
                    dve.wait_ge(qk_done, 4 * it + j + 1)
                    v.tensor_scalar(expq[:, j, :], pa[j][:, :], qkb[:, j:j + 1], 0.0, ALU.add, ALU.min).then_inc(min_ready, 1)
                for j in range(2 * KC):
                    dve.wait_ge(exp_ready, 4 * it + j + 1)
                    dst = (qf if j < KC else kf)[:, j % KC, :]
                    v.scalar_tensor_tensor(dst, pa[j][:, :], qkb1[:, j:j + 1], expq[:, j, :], ALU.add, ALU.max)\
                        .then_inc(qf_ready if j < KC else kf_ready, 1)
                dve.wait_ge(kf_ready, KC * it + KC)
                v.tensor_scalar(kE, kf, const[:, C_EVEN:C_EVEN + 1], None, ALU.mult).then_inc(keo_ready, 1)
                v.tensor_scalar(kO, kf, const[:, C_ODD:C_ODD + 1], None, ALU.mult).then_inc(keo_ready, 1)
                dve.wait_ge(rows_in, 16 * l + 16)
                for s in range(2):
                    dve.wait_ge(v_done, 2 * it + s + 1)
                    for i in range(2):
                        last = v.tensor_tensor(vaug[:, 2 * s + i, :, 0:HD],
                                               po[s][:, ts(i, D)].rearrange("p (h e) -> p h e", h=H),
                                               vecs[:, V_BV, :].rearrange("p (h e) -> p h e", h=H), ALU.add)
                    last.then_inc(vaug_ready, 1)
                for i in range(2 * KC):
                    dve.wait_ge(kv_done, 4 * it + i + 1)
                    v.tensor_tensor(kvm[:, i // KC, i % KC, :], pa[i][:, 0:H * VA], head_mask(i % KC), ALU.mult)\
                        .then_inc(kvm_ready, 1)

                def mask_scores(tile):
                    if tile >= 2:
                        dve.wait_ge(av_done, 4 * it + tile - 1)
                    for g in range(4):
                        i = 4 * tile + g
                        dve.wait_ge(sc_done, 16 * it + i + 1)
                        v.tensor_tensor(scm[:, i % 8, :, :], pa[g][:, :].rearrange("p (h q) -> p h q", h=4),
                                        tri.unsqueeze(1).broadcast_to([P, 4, P]), ALU.mult).then_inc(scm_ready, 1)

                def divide(tile):
                    dve.wait_ge(av_done, 4 * it + tile + 1)
                    num = po[tile % 2][:, 0:H * VA].rearrange("p (h e) -> p h e", h=H)
                    step.after(v.tensor_scalar(den[:, tile, :], num[:, :, HD], ATT_EPS, None, ALU.add))
                    step.after(v.reciprocal(den[:, tile, :], den[:, tile, :]))
                    v.tensor_tensor(att[:, tile, :].rearrange("p (h e) -> p h e", h=H), num[:, :, 0:HD],
                                    den[:, tile, :].unsqueeze(2).broadcast_to([P, H, HD]), ALU.mult).then_inc(att_ready, 1)

                mask_scores(0)
                mask_scores(1)
                divide(0)
                mask_scores(2)
                divide(1)
                mask_scores(3)
                divide(2)
                divide(3)
                dve.wait_ge(xb_ready, it + 1)
                for s in range(2):
                    dve.wait_ge(wo_done, 2 * it + s + 1)
                    v.tensor_tensor(two(r1, s), pa[s][:, :].rearrange("p (t d) -> p t d", t=2), two(xb, s), ALU.add)\
                        .then_inc(r1_ready, 1)
                    dve.wait_ge(r1_ready, 2 * it + s + 1)
                    tiles = [2 * s, 2 * s + 1]
                    step.after(normalise(2 * PAIRS + 4 * it + s + 1, 2 * s, [r1[:, i, :] for i in tiles], [y[:, i, :] for i in tiles]))
                    step.after(v.tensor_tensor(two(y, s), two(y, s), row(V_G1, 2), ALU.mult))
                    v.tensor_tensor(two(y, s), two(y, s), row(V_BE1, 2), ALU.add).then_inc(y_ready, 1)
                for s in range(2):
                    dve.wait_ge(down_done, 2 * it + s + 1)
                    dve.wait_ge(yb_ready, 2 * it + s + 1)
                    step.after(v.tensor_tensor(two(r1, s), po[s][:, :].rearrange("p (t d) -> p t d", t=2), two(yb, s), ALU.add))
                    tiles = [2 * s, 2 * s + 1]
                    step.after(normalise(2 * PAIRS + 4 * it + 2 + s + 1, 2 * s, [r1[:, i, :] for i in tiles], [r1[:, i, :] for i in tiles]))
                    step.after(v.tensor_tensor(two(r1, s), two(r1, s), row(V_G2, 2), ALU.mult))
                    v.tensor_tensor(hst[:, bass.ds(p * TT + 2 * s, 2), :], two(r1, s), row(V_BE2, 2), ALU.add).then_inc(h_ready, 1)
                step.end_loop(L * PAIRS)
        dve.wait_ge(w_in_2, W2_IN)
        dve.wait_ge(a_exp, 1)
        dve.wait_ge(h_ready, LAYERS_DONE)
        v.tensor_scalar(acol, acol, -1.0, None, ALU.mult).then_inc(a_ready, 1)
        dve.wait_ge(a_ready, 1)
        with dve.Fori(0, PAIRS) as p:
            step.loop(p, DVE_STEPS)
            xct, xnt = [xc[:, i, :] for i in range(TT)], [xn[:, i, :] for i in range(TT)]

            def wide(r, n):
                return r.unsqueeze(1).broadcast_to([P, n, r.shape[1]])

            def normalised(k):
                normalise(GROUPS + 6 * p + k + 1, 0, xct, xnt).then_inc(xn_ready, 1)

            dve.wait_ge(x_kept, p)
            at = [bass.ds(p * TT + i, 1) for i in range(TT)]
            step.after(normalise(GROUPS + 6 * p + 1, 0, [hst[:, j, :].rearrange("p a d -> p (a d)") for j in at], xct))
            step.after(v.tensor_tensor(xc, xc, wide(r_gf, TT), ALU.mult))
            step.after(v.tensor_tensor(xc, xc, wide(r_bef, TT), ALU.add))
            step.after(v.tensor_tensor(xc, xc, xst[:, ts(p, TT), :], ALU.add))

            dve.wait_ge(xf_kept, p)
            normalised(1)
            dve.wait_ge(nrm_ready, 2 * p + 2)
            for i in range(TT):
                last = v.tensor_scalar(dn[:, i, :], tn[:, (i // 2) * S:(i // 2 + 1) * S], vn[:, i:i + 1], SIM_EPS, ALU.mult, ALU.max)
            step.after(last)
            step.after(v.reciprocal(dn, dn))
            for s in range(2):
                dve.wait_ge(dots_done, 2 * p + s + 1)
                last = v.tensor_tensor(two(dn, s), po[s][:, :].rearrange("p (t d) -> p t d", t=2), two(dn, s), ALU.mult)
            step.after(last)
            step.after(v.tensor_tensor(xc, xc, dn, ALU.add))

            normalised(2)
            dve.wait_ge(gate_done, p + 1)
            gates = pa[0][:, 0:TT * E0].rearrange("p (t e) -> p t e", t=TT)
            step.after(v.tensor_reduce(gmax, gates, AX, ALU.max))
            v.tensor_tensor(lg, gates, gmax.unsqueeze(2).broadcast_to([P, TT, E0]), ALU.subtract).then_inc(gl_ready, 1)
            for i in range(TT):
                dve.wait_ge(pair_done, TT * p + i + 1)
                v.tensor_tensor(eb[:, i, :], (po[0], pa[1], pa[2], pa[3])[i][:, :], r_pair, ALU.add).then_inc(eb_ready, 1)
            dve.wait_ge(ge_ready, p + 1)
            step.after(v.tensor_reduce(gsum, lg, AX, ALU.add))
            step.after(v.reciprocal(gsum, gsum))
            step.after(v.tensor_tensor(lg, lg, gsum.unsqueeze(2).broadcast_to([P, TT, E0]), ALU.mult))
            for e in range(2):
                step.after(v.tensor_tensor(cmp8, lg, lg[:, :, e:e + 1].broadcast_to([P, TT, E0]), ALU.is_gt))
                if e:
                    step.after(v.tensor_tensor(cmp8[:, :, 0:e], lg[:, :, 0:e], lg[:, :, e:e + 1].broadcast_to([P, TT, e]), ALU.is_ge))
                step.after(v.tensor_reduce(cnt2[:, e, :], cmp8, AX, ALU.add))
                step.after(v.scalar_tensor_tensor(coef[:, e, :], cnt2[:, e, :], float(e), lg[:, :, e], ALU.is_equal, ALU.mult))
            for i in range(TT):
                dve.wait_ge(sil_ready, TT * p + i + 1)
                for e in range(2):
                    step.after(v.scalar_tensor_tensor(xct[i], eb[:, i, e * D:(e + 1) * D], coef[:, e, i:i + 1], xct[i], ALU.mult, ALU.add))

            normalised(3)
            step.after(v.memset(xpad[:, :, :, 0:3], 0.0))
            for tap in range(KCONV):
                for c in range(IC):
                    if tap == 0:
                        dve.wait_ge(in_out, 8 * p + c + 1)
                    at = KCONV - 1 - tap
                    dst = xs[:, c, :].rearrange("p (s t) -> p s t", s=2)
                    src, w_tap = xpad[:, c, :, at:at + S], cw[:, c, at:at + 1]
                    if tap == 0:
                        last = v.tensor_scalar(dst, src, w_tap, conv_b[:, c:c + 1], ALU.mult, ALU.add)
                    else:
                        last = v.scalar_tensor_tensor(dst, src, w_tap, dst, ALU.mult, ALU.add)
                    if tap == KCONV - 1:
                        last.then_inc(conv_ready, 1)
                if tap < KCONV - 1:
                    step.after(last)
            dve.wait_ge(soft_e_ready, p + 1)
            v.tensor_scalar(soft_d, soft_e, 1.0, None, ALU.add).then_inc(soft_u_ready, 1)
            dve.wait_ge(soft_ready, p + 1)
            step.after(v.tensor_scalar(soft_d, soft_d, 1.0, LEAST, ALU.subtract, ALU.max))
            step.after(v.reciprocal(soft_d, soft_d))
            step.after(v.scalar_tensor_tensor(soft_d, soft_l, LEAST, soft_d, ALU.max, ALU.mult))
            step.after(v.tensor_tensor(soft_d, soft_d, soft_e, ALU.mult))
            v.tensor_tensor(dt, dt, soft_d, ALU.add).then_inc(dt_ready, 1)
            dve.wait_ge(dt_ready, p + 1)
            step.after(v.tensor_tensor(dtx, dt, xs, ALU.mult))
            for i in range(4 * IC):
                g, c = i // IC, i % IC
                decay, h = dA[i % 2], uh[i % 2]
                flat = "p n t -> p (n t)"
                dve.wait_ge(da_ready, 16 * p + i + 1)
                step.after(v.tensor_scalar(decay, decay, DECAY_TOP, DECAY_HALF, ALU.min, ALU.add))
                if i >= 2:
                    dve.wait_ge(ysum_done, 16 * p + i - 1)
                dve.wait_ge(bc_out, 32 * p + 8 * g + 8)
                v.tensor_tensor(h, dtx[:, c, :].unsqueeze(1).broadcast_to([P, NG, W]), Bs[g % 2], ALU.mult)
                step.after(v.tensor_scalar(decay, decay, DECAY_GRID, DECAY_GRID, ALU.add, ALU.subtract))
                step.after(v.memset(decay.rearrange("p n (s t) -> p (n s) t", s=2)[:, :, 0], 0.0))
                v.tensor_tensor_scan(h.rearrange(flat), decay.rearrange(flat), h.rearrange(flat), 0.0, ALU.mult, ALU.add).then_inc(scan_done, 1)
                dve.wait_ge(scan_done, 16 * p + i + 1)
                v.tensor_tensor(h, h, Cs[g % 2], ALU.mult).then_inc(hc_ready, 1)
            for c in range(IC):
                dve.wait_ge(ysum_done, 16 * p + 12 + c + 1)
                step.after(v.scalar_tensor_tensor(dtx[:, c, :], xs[:, c, :], skip[:, c:c + 1], pa[c][:, :], ALU.mult, ALU.add))
                v.tensor_tensor(dtx[:, c, :], dtx[:, c, :], zs[:, c, :], ALU.mult).then_inc(yg_ready, 1)
            for s in range(2):
                dve.wait_ge(proj_done, 2 * p + s + 1)
                step.after(v.tensor_tensor(two(xc, s), po[s][:, :].rearrange("p (t d) -> p t d", t=2), two(xc, s), ALU.add))
            step.after(v.tensor_tensor(xc, xc, wide(r_out, TT), ALU.add))

            normalised(4)
            for u in range(16 + 5):
                if u < 16:
                    dve.wait_ge(s2_done, 16 * p + u + 1)
                    step.after(v.tensor_reduce(mx[:, u % 4, :], pa[u % 2][:, :].rearrange("p (b j) -> p b j", b=2), AX, ALU.max))
                    v.tensor_scalar(nm[:, u % 4, :], mx[:, u % 4, :], -SCALE, None, ALU.mult).then_inc(nm_ready, 1)
                if 1 <= u < 17:
                    w = u - 1
                    dve.wait_ge(pT_done, 16 * p + w + 1)
                    if w >= 2:
                        dve.wait_ge(av2_done, 16 * p + w - 1)
                    v.tensor_copy(pT[w % 2], pa[2 + w % 2][:, :].rearrange("p (b i) -> p b i", b=4)).then_inc(pT_out, 1)
                if u >= 6 and (u - 6) % 4 == 0 and u <= 18:
                    tile = (u - 6) // 4
                    dve.wait_ge(av2_done, 16 * p + 4 * tile + 4)
                    step.after(v.reciprocal(sm[:, tile, :], sm[:, tile, :]))
                    v.tensor_tensor(at2[tile % 2].rearrange("p (h d) -> p h d", h=QH), po[tile % 2][:, :].rearrange("p (h d) -> p h d", h=QH),
                                    sm[:, tile, :].unsqueeze(2).broadcast_to([P, QH, QD]), ALU.mult).then_inc(at2_ready, 1)
                if u >= 8 and (u - 8) % 4 == 0:
                    tile = (u - 8) // 4
                    dve.wait_ge(wo2_done, 4 * p + tile + 1)
                    v.tensor_tensor(xct[tile], po[tile % 2][:, 0:D], xct[tile], ALU.add).then_inc(wo2_out, 1)
            dve.wait_ge(wo2_out, 4 * p + 4)
            v.tensor_tensor(xc, xc, wide(r_xo, TT), ALU.add).then_inc(xc_ready, 1)
            dve.wait_ge(xc_ready, p + 1)
            normalised(5)
            dve.wait_ge(route_done, p + 1)
            v.tensor_tensor(lgall[:, ts(p, TT), :], pa[0][:, 0:TT * NE].rearrange("p (t e) -> p t e", t=TT), wide(r_r, TT), ALU.add)\
                .then_inc(logits_ready, 1)
            step.end_loop(PAIRS)
        def each(row):
            return row.unsqueeze(2).broadcast_to([P, NT, NE])

        dve.wait_ge(logits_ready, PAIRS)
        for e in range(NE):
            if e:
                v.tensor_tensor(cmp3[:, :, 0:e], lgall[:, :, 0:e], lgall[:, :, e:e + 1].broadcast_to([P, NT, e]), ALU.is_ge)
            step.after(v.tensor_tensor(cmp3[:, :, e:NE], lgall[:, :, e:NE], lgall[:, :, e:e + 1].broadcast_to([P, NT, NE - e]), ALU.is_gt))
            step.after(v.tensor_reduce(cnt[:, :, e], cmp3, AX, ALU.add))
        v.tensor_scalar(sel, cnt, 2.0, None, ALU.is_lt).then_inc(sel_ready, 1)
        for k in range(2):
            last = v.tensor_scalar(top[k], cnt, float(k), None, ALU.is_equal)
        step.after(last)
        for k in range(2):
            step.after(v.tensor_tensor(picked, top[k], lgall, ALU.mult))
            step.after(v.tensor_reduce(lt[k], picked, AX, ALU.add))
        v.tensor_tensor(gexp, lt[1], lt[0], ALU.subtract).then_inc(lt_ready, 1)
        dve.wait_ge(rank_done, 1)
        total = pa[1][:, 0:NT * NE].rearrange("p (t e) -> p t e", t=NT)
        step.after(v.memset(before[:, 0, :], 0.0))
        for i in range(1, NT):
            step.after(v.tensor_tensor(before[:, i, :], total[:, i - 1, :], before[:, i - 1, :], ALU.add))
        step.after(v.tensor_tensor(rank, pa[0][:, 0:NT * NE].rearrange("p (t e) -> p t e", t=NT), before, ALU.add))
        dve.wait_ge(gexp_ready, 1)
        step.after(v.tensor_scalar(gate[0], gexp, 1.0, None, ALU.add))
        step.after(v.reciprocal(gate[0], gate[0]))
        step.after(v.tensor_tensor(gate[1], gate[0], gexp, ALU.mult))
        for k in range(2):
            step.after(v.tensor_tensor(picked, top[k], rank, ALU.mult))
            step.after(v.tensor_reduce(rk[k], picked, AX, ALU.add))
            step.after(v.tensor_tensor(picked, top[k], slot0.unsqueeze(1).broadcast_to([P, NT, NE]), ALU.mult))
            step.after(v.tensor_reduce(base[k], picked, AX, ALU.add))
            step.after(v.tensor_scalar(over[k], rk[k], float(CAP), float(NE * CAP), ALU.is_ge, ALU.mult))
            step.after(v.tensor_tensor(over[k], over[k], rk[k], ALU.add))
            step.after(v.tensor_tensor(into[k], over[k], base[k], ALU.add))
            step.after(v.scalar_tensor_tensor(gate[k], rk[k], float(CAP), gate[k], ALU.is_lt, ALU.mult))
            step.after(v.scalar_tensor_tensor(outof[k], rk[k], CAP - 1.0, base[k], ALU.min, ALU.add))
        v.memset(picked, 0.0).then_inc(places_ready, 1)

        with dve.Fori(0, NE // 2) as q:
            for j in range(2):
                dve.wait_ge(we_in[j], 64 * q + 64)
                dve.wait_ge(ye_kept[j], 16 * q)
                for s in range(2):
                    dve.wait_ge(down3_done[j], 2 * q + s + 1)
                    v.tensor_tensor(two(ye[j], s), po[s][:, :].rearrange("p (t d) -> p t d", t=2),
                                    b2e[j].unsqueeze(1).broadcast_to([P, 2, D]), ALU.add).then_inc(ye_ready[j], 1)
        dve.wait_ge(x_kept, PAIRS)
        for i in range(NT):
            if i % TT == 0:
                dve.wait_ge(back_in[i // TT], 16 * 2 * TT)
            step.after(v.scalar_tensor_tensor(xst[:, i, :], back[:, 2 * i, :], gate[0][:, i:i + 1], xst[:, i, :], ALU.mult, ALU.add))
            v.scalar_tensor_tensor(xst[:, i, :], back[:, 2 * i + 1, :], gate[1][:, i:i + 1], xst[:, i, :], ALU.mult, ALU.add).then_inc(final_ready, 1)

    @block.tensor
    def _(pe):
        mm = nc.tensor.matmul

        def transposed(dst, src):
            return nc.tensor.transpose(dst, src, ident)

        pe.wait_ge(const_in, 16)
        with pe.Fori(0, L) as l:
            with pe.Fori(0, PAIRS) as p:
                it = l * PAIRS + p
                pe.wait_ge(hbuf_ready, it + 1)
                for k in range(KC):
                    for i in range(TT):
                        last = transposed(pt[k][:, ts(i, P)], hbuf[:, i, ts(k, P)])
                    last.then_inc(tr_done, 1)
                pe.wait_ge(attn_w_in, 80 * l + 80)
                pe.wait_ge(tr_out, 8 * it + 2)
                pe.wait_ge(gelu_ready, FM * it)
                for j in range(2 * KC):
                    for k in range(KC):
                        last = mm(pa[j][:, :], (wq if j < KC else wk)[:, k, ts(j % KC, P)], hT[:, k, :], start=k == 0, stop=k == KC - 1)
                    last.then_inc(qk_done, 1)
                pe.wait_ge(h_ready, 2 * PAIRS + 2 * it)
                for s in range(2):
                    for i in range(2):
                        for k in range(KC):
                            last = mm(po[s][:, ts(i, D)], hT[:, k, ts(2 * s + i, P)], wv[:, k, :], start=k == 0, stop=k == KC - 1)
                    last.then_inc(v_done, 1)
                pe.wait_ge(kf_ready, KC * it + KC)
                for s in range(2):
                    for m in range(KC):
                        last = transposed(pt[s][:, ts(m, P)], kf[:, m, ts(2 * s, P)])
                    last.then_inc(tr_done, 1)
                pe.wait_ge(vaug_ready, 2 * it + 2)
                pe.wait_ge(tr_out, 8 * it + 4)
                for i in range(2 * KC):
                    s = i // KC
                    mm(pa[i][:, 0:H * VA], ktok[:, s, ts(i % KC, P)], vaug[:, 2 * s, :, :].rearrange("p h e -> p (h e)"),
                       start=True, stop=True).then_inc(kv_done, 1)
                pe.wait_ge(keo_ready, 2 * it + 2)
                pe.wait_ge(kvm_ready, 4 * it + 4)

                def scores(tile):
                    for g in range(4):
                        i = 4 * tile + g
                        if tile:
                            pe.wait_ge(scm_ready, 16 * it + i - 3)
                        for c in range(KC):
                            for e in range(2):
                                keys = (kO if e else kE)[ts(g, 32), c, ts(tile, P)]
                                last = mm(pa[g][:, ts(2 * c + e, P)], keys, qf[ts(g, 32), c, ts(tile, P)], start=True, stop=True)
                        last.then_inc(sc_done, 1)

                def weigh(tile):
                    if tile >= 2:
                        pe.wait_ge(att_ready, 4 * it + tile - 1)
                    s, num = tile // 2, po[tile % 2]
                    if tile % 2:
                        for m in range(KC):
                            mm(num[:, 0:H * VA], qf[:, m, ts(tile, P)], kvm[:, s, m, :], start=m == 0, stop=m == KC - 1)
                    for g in range(4):
                        pe.wait_ge(scm_ready, 16 * it + 4 * tile + g + 1)
                        for n in range(4):
                            h = 8 * (n // 2) + 2 * g + n % 2
                            last = mm(num[:, ts(h, VA)], scm[:, (4 * tile + g) % 8, n, :], vaug[:, tile, h, :],
                                      start=tile % 2 == 0, stop=True, skip_group_check=True)
                    last.then_inc(av_done, 1)

                def attention_transposed(s):
                    pe.wait_ge(att_ready, 4 * it + 2 * s + 2)
                    for k in range(KC):
                        for i in range(2):
                            last = transposed(pt[s][:, ts(2 * k + i, P)], att[:, 2 * s + i, ts(k, P)])
                    last.then_inc(tr_done, 1)

                def project(s):
                    pe.wait_ge(tr_out, 8 * it + 4 + s + 1)
                    pe.wait_ge(scm_ready, 16 * it + 13 + s)
                    for i in range(2):
                        for k in range(KC):
                            last = mm(pa[s][:, ts(i, D)], attT[:, k, ts(2 * s + i, P)], wo[:, k, :], start=k == 0, stop=k == KC - 1)
                    last.then_inc(wo_done, 1)

                scores(0)
                scores(1)
                weigh(0)
                scores(2)
                weigh(1)
                scores(3)
                attention_transposed(0)
                weigh(2)
                project(0)
                weigh(3)
                attention_transposed(1)
                project(1)
                for s in range(2):
                    pe.wait_ge(y_ready, 2 * it + s + 1)
                    for k in range(KC):
                        for i in range(2):
                            last = transposed(pt[s][:, ts(2 * k + i, P)], y[:, 2 * s + i, ts(k, P)])
                    last.then_inc(tr_done, 1)
                pe.wait_ge(ffn_w_in, 48 * l + 48)
                pe.wait_ge(tr_out, 8 * it + 8)
                for m in range(FM):
                    if m >= 4:
                        pe.wait_ge(gelu_ready, FM * it + m - 3)
                    for k in range(KC):
                        last = mm(pa[m % 4][:, :], w1[:, k, ts(m, P)], yT[:, k, :], start=k == 0, stop=k == KC - 1)
                    last.then_inc(up_done, 1)
                for s in range(2):
                    for i in range(2):
                        for m in range(FM):
                            if s == 0 and i == 0:
                                pe.wait_ge(gelu_ready, FM * it + m + 1)
                            last = mm(po[s][:, ts(i, D)], gT[:, m, ts(2 * s + i, P)], w2[:, m, :], start=m == 0, stop=m == FM - 1)
                    last.then_inc(down_done, 1)
        pe.wait_ge(w_in_2, W2_IN)
        with pe.Fori(0, PAIRS) as p:
            def input_transposed(k, n):
                pe.wait_ge(xn_ready, XN * p + n)
                for s in range(2):
                    if k:
                        pe.wait_ge(tr2_out, TR2 * p + k + s - 1)
                    for c in range(KC):
                        for i in range(2):
                            last = transposed(pt[s][:, ts(2 * c + i, P)], xn[:, 2 * s + i, ts(c, P)])
                    last.then_inc(tr2_done, 1)
                pe.wait_ge(tr2_out, TR2 * p + k + 2)

            input_transposed(0, 1)
            for c in range(KC):
                last = mm(pa[0][:, :], w_sv[:, c, :], xnT[:, c, :], start=c == 0, stop=c == KC - 1)
            last.then_inc(vt_done, 1)
            pe.wait_ge(ctx_in, 32 * p + 32)
            mm(pa[1][:, :], w_st[:, 0, :], ctxT[:, 0, :], start=True, stop=False)
            mm(pa[1][:, :], w_st[0:CT - P, 1, :], ctxT[0:CT - P, 1, :], start=False, stop=True).then_inc(vt_done, 1)
            pe.wait_ge(vt_ready, 4 * p + 4)
            for i in range(TT):
                mm(pa[2][:, i:i + 1], vsq[:, ts(i, P)], ones[:, 0:1], start=True, stop=True)
            mm(pa[3][:, :], ones, tsq, start=True, stop=True).then_inc(nrm_done, 1)
            for s in range(2):
                for i in range(2):
                    last = mm(po[s][:, ts(i, S)], vT[:, ts(2 * s + i, P)], tT[:, s * S:(s + 1) * S], start=True, stop=True)
                last.then_inc(dots_done, 1)
            input_transposed(2, 2)
            for i in range(TT):
                for c in range(KC):
                    last = mm(pa[0][:, ts(i, E0)], xnT[:, c, ts(i, P)], w_gate[:, c, :], start=c == 0, stop=c == KC - 1)
            last.then_inc(gate_done, 1)
            for i in range(TT):
                for c in range(KC):
                    last = mm((po[0], pa[1], pa[2], pa[3])[i][:, :], xnT[:, c, ts(i, P)], w_pair[:, c, :], start=c == 0, stop=c == KC - 1)
                last.then_inc(pair_done, 1)
            input_transposed(4, 3)
            for m in range(2 * IC):
                if m >= 4:
                    pe.wait_ge(in_out, 8 * p + m - 3)
                for c in range(KC):
                    last = mm(pa[m % 4][:, :], w_in[:, c, ts(m, P)], xnT[:, c, :], start=c == 0, stop=c == KC - 1)
                last.then_inc(in_done, 1)
            pe.wait_ge(xs_ready, IC * p + IC)
            pe.wait_ge(in_out, 8 * p + 8)
            for c in range(IC):
                last = mm(pa[0][0:DTR, :], w_xp[:, c, 0:DTR], xs[:, c, :], start=c == 0, stop=c == IC - 1)
            last.then_inc(xp_done, 1)
            for c in range(IC):
                last = mm(pa[1][0:2 * NS, :], w_xp[:, c, DTR:DTR + 2 * NS], xs[:, c, :], start=c == 0, stop=c == IC - 1)
            last.then_inc(xp_done, 1)
            pe.wait_ge(xp_out, 2 * p + 2)
            for c in range(IC):
                mm(pa[c][:, :], w_dt[:, ts(c, P)], dtr, start=True, stop=True).then_inc(dtp_done, 1)

            def spread(g):
                for n in range(NG):
                    k = 8 * g + 2 * n
                    for which, bank in enumerate((pt, po)):
                        if k >= 4:
                            pe.wait_ge(bc_out, 32 * p + k + which - 3)
                        r = which * NS + g * NG + n
                        mm(bank[n % 2][:, :], ident[0:2 * NS, r:r + 1].broadcast_to([2 * NS, P]), bc,
                           start=True, stop=True).then_inc(bc_done, 1)

            spread(0)
            pe.wait_ge(soft_ready, p + 1)
            for i in range(4 * IC):
                g, c = i // IC, i % IC
                if c == 2 and g + 1 < NS // NG:
                    spread(g + 1)
                pe.wait_ge(hc_ready, 16 * p + i + 1)
                for n in range(NG):
                    last = mm(pa[c][:, :], ident, uh[i % 2][:, n, :], start=g == 0 and n == 0, stop=g == NS // NG - 1 and n == NG - 1)
                last.then_inc(ysum_done, 1)
            pe.wait_ge(yg_ready, IC * p + IC)
            for s in range(2):
                for i in range(2):
                    for c in range(IC):
                        last = mm(po[s][:, ts(i, D)], dtx[:, c, ts(2 * s + i, P)], w_out[:, c, :], start=c == 0, stop=c == IC - 1)
                last.then_inc(proj_done, 1)
            input_transposed(6, 4)
            for r in range(12):
                if r >= 4:
                    pe.wait_ge(qkv_out, 12 * p + r - 3)
                m, bank = r % 4, pa[r % 4][:, :]
                if r < 4:
                    for c in range(KC):
                        last = mm(bank, w_q[:, c, ts(m, P)], xnT[:, c, :], start=c == 0, stop=c == KC - 1)
                elif r < 8:
                    mm(bank, w_k[:, 0, ts(m, P)], ctxT[:, 0, :], start=True, stop=False)
                    last = mm(bank, w_k[0:CT - P, 1, ts(m, P)], ctxT[0:CT - P, 1, :], start=False, stop=True)
                else:
                    mm(bank, ctxT[:, 0, ts(m, P)], w_v[:, 0, :], start=True, stop=False)
                    last = mm(bank, ctxT[0:CT - P, 1, ts(m, P)], w_v[0:CT - P, 1, :], start=False, stop=True)
                last.then_inc(qkv_done, 1)
            pe.wait_ge(qkv_out, 12 * p + 12)

            def scores2(u):
                tile, j, e = u // 4, u % 4 // 2, u % 2
                if u >= 2:
                    pe.wait_ge(pexp_ready, 16 * p + u - 1)
                for b in range(2):
                    last = mm(pa[e][:, b * S:(b + 1) * S], qT[ts(e, QD), 2 * j + b, ts(tile, P)],
                              kT[ts(e, QD), 2 * j + b, (tile // 2) * S:(tile // 2 + 1) * S], start=True, stop=True)
                last.then_inc(s2_done, 1)

            def weights_transposed(u):
                pe.wait_ge(pexp_ready, 16 * p + u + 1)
                if u >= 2:
                    pe.wait_ge(pT_out, 16 * p + u - 1)
                for b in range(2):
                    for k in range(2):
                        last = transposed(pa[2 + u % 2][:, ts(2 * b + k, P)], pexp[u % 2][:, b, ts(k, P)])
                last.then_inc(pT_done, 1)

            def weigh2(u):
                tile, h0 = u // 4, 4 * (u % 4 // 2) + u % 2
                pe.wait_ge(pT_out, 16 * p + u + 1)
                if u % 4 == 0 and tile >= 2:
                    pe.wait_ge(wo2_out, 4 * p + tile - 1)
                for b in range(2):
                    for k in range(2):
                        last = mm(po[tile % 2][:, ts(h0 + 2 * b, QD)], pT[u % 2][:, 2 * b + k, :],
                                  vv[:, 2 * (tile // 2) + k, ts(h0 + 2 * b, QD)], start=k == 0, stop=k == 1)
                last.then_inc(av2_done, 1)

            def project2(tile):
                pe.wait_ge(at2_ready, 4 * p + tile + 1)
                pe.wait_ge(tr2_out, TR2 * p + 8 + tile - 1)
                for c in range(QC):
                    last = transposed(pt[tile % 2][:, ts(c, P)], at2[tile % 2][:, ts(c, P)])
                last.then_inc(tr2_done, 1)
                pe.wait_ge(tr2_out, TR2 * p + 8 + tile + 1)
                for c in range(QC):
                    last = mm(po[tile % 2][:, 0:D], at2T[tile % 2][:, c, :], w_o[:, c, :], start=c == 0, stop=c == QC - 1)
                last.then_inc(wo2_done, 1)

            for u in range(16 + 4):
                if u < 16:
                    scores2(u)
                if 1 <= u < 17:
                    weights_transposed(u - 1)
                if 2 <= u < 18:
                    weigh2(u - 2)
                if u >= 7 and (u - 7) % 4 == 0:
                    project2((u - 7) // 4)
            input_transposed(12, 5)
            for i in range(TT):
                for c in range(KC):
                    last = mm(pa[0][:, ts(i, NE)], xnT[:, c, ts(i, P)], w_r[:, c, :], start=c == 0, stop=c == KC - 1)
            last.then_inc(route_done, 1)
        pe.wait_ge(sel_ready, 1)
        flat_sel = sel.rearrange("p t e -> p (t e)")
        mm(pa[0][:, 0:NT * NE], strict, flat_sel, start=True, stop=True)
        mm(pa[1][:, 0:NT * NE], ones, flat_sel, start=True, stop=True).then_inc(rank_done, 1)
        with pe.Fori(0, NE // 2) as q:
            for j in range(2):
                pe.wait_ge(xg_in[j], 16 * q + 16)
                for s in range(2):
                    if j:
                        pe.wait_ge(tr3_out, 4 * q + s + 1)
                    for c in range(KC):
                        for i in range(2):
                            last = transposed(pt[s][:, ts(2 * c + i, P)], xg[j][:, 2 * s + i, ts(c, P)])
                    last.then_inc(tr3_done, 1)
                pe.wait_ge(we_in[j], 64 * q + 64)
                pe.wait_ge(tr3_out, 4 * q + 2 * j + 2)
                for m in range(EF // P):
                    if m >= 4:
                        pe.wait_ge(gelu3_ready, 16 * q + 8 * j + m - 3)
                    for c in range(KC):
                        last = mm(pa[m % 4][:, :], w1e[j][:, c, ts(m, P)], xgT[:, c, :], start=c == 0, stop=c == KC - 1)
                    last.then_inc(up3_done, 1)
                pe.wait_ge(ye_ready[1 - j], 2 * q + 2 * j)
                for s in range(2):
                    for i in range(2):
                        for m in range(EF // P):
                            if s == 0 and i == 0:
                                pe.wait_ge(gelu3_ready, 16 * q + 8 * j + m + 1)
                            last = mm(po[s][:, ts(i, D)], gTe[:, m, ts(2 * s + i, P)], w2e[j][:, m, :], start=m == 0, stop=m == EF // P - 1)
                    last.then_inc(down3_done[j], 1)

    ctx.close()


def host_arrays(inputs):
    f = {k: np.asarray(a) for k, a in inputs.items()}
    c = np.ascontiguousarray
    rows = [f["L0_attn_" + n] for n in ("bv", "bo", "g1", "be1", "b2", "g2", "be2")]
    cols = lambda a: a.reshape(L, -1, P).transpose(0, 2, 1)
    arrays = {
        "consts": shape_constants(),
        "x": f["x"].reshape(N, D),
        "rows": np.stack(rows, 1).reshape(L, 7 * D),
        "qk_bias": np.concatenate([cols(f["L0_attn_bq"]), cols(f["L0_attn_bk"])], 2),
        "b1_cols": cols(f["L0_attn_b1"]),
    }
    arrays["b1e_cols"] = f["L1_ffn_b1"].reshape(NE, EF // P, P).transpose(0, 2, 1)
    for n in ("W1", "W2", "b2"):
        arrays["L1_ffn_" + n] = f["L1_ffn_" + n]
    for n in ("Wq", "Wk", "Wv", "Wo", "W1", "W2"):
        arrays["L0_attn_" + n] = f["L0_attn_" + n]
    chunks = lambda a: a.reshape(-1, P).T
    arrays |= {
        "ctxT": f["ctx_768"].reshape(N, CT).T,
        "sim_wv": f["L0_xattn_Wv"].T, "sim_wt": f["L0_xattn_Wt"].T,
        "gate": f["L0_ffn_gate_w"], "pair_w": np.concatenate([f["L0_ffn_w0"].T, f["L0_ffn_w1"].T], 1),
        "ssm_in": f["L1_attn_in_proj_w"].T, "ssm_xp": f["L1_attn_x_proj_w"].T, "ssm_dt": f["L1_attn_dt_proj_w"].T,
        "ssm_out": f["L1_attn_out_proj_w"].T,
        "a_log": f["L1_attn_A_log"].reshape(IC, P, NS).transpose(1, 0, 2),
        "cols": np.concatenate([
            chunks(f["L0_xattn_bv"]), chunks(f["L0_xattn_bt"]), chunks(f["L1_attn_in_proj_b"]),
            f["L1_attn_conv_w"].reshape(IC, P, KCONV).transpose(1, 0, 2).reshape(P, -1),
            chunks(f["L1_attn_conv_b"]), chunks(f["L1_attn_dt_proj_b"]), chunks(f["L1_attn_D"])], 1),
        "rows2": np.concatenate([f["L0_attn_gf"], f["L0_attn_bef"], f["L1_attn_out_proj_b"], f["L1_xattn_bo"],
                                 f["L0_ffn_b0"], f["L0_ffn_b1"], f["L1_ffn_br"]]),
    }
    for n in ("L1_xattn_Wq", "L1_xattn_Wk", "L1_xattn_Wv", "L1_xattn_Wo", "L1_ffn_Wr"):
        arrays[n] = f[n]
    return {k: c(a) for k, a in arrays.items()}


def kernel(**inputs):
    import concourse.bacc as bacc
    from concourse.bass_utils import run_bass_kernel_spmd as run
    arrays = host_arrays(inputs)
    nc = bacc.Bacc("TRN2", target_bir_lowering=False, num_devices=1)
    aps = {k: nc.dram_tensor("in_" + k, a.shape, F32, kind="ExternalInput").ap() for k, a in arrays.items()}
    out = nc.dram_tensor("out", (N, D), F32, kind="ExternalOutput").ap()
    decoder(nc, aps, out)
    r = run(nc, [{"in_" + k: a for k, a in arrays.items()}], core_ids=[0])
    return r.results[0]["out"].reshape(B, S, D)
```

```python
import numpy as np
import concourse.bass as bass
from concourse import mybir
from contextlib import ExitStack

F32 = mybir.dt.float32
I32 = mybir.dt.int32
ALU = mybir.AluOpType
ACT = mybir.ActivationFunctionType
AX = mybir.AxisListType.X

P = 128
B, S, D = 8, 256, 256
N = B * S
NT = N // P
KC = D // P
PAIRS = B // 2
TT = 4
W = TT * P
L, H, HD, FF = 4, 16, 16, 1024
FM = FF // P
VA = 32
HB = P // VA
LN_EPS, ATT_EPS = 1e-5, 1e-6

HX, CT, E0 = 128, 192, 8
DI, NS, DTR, KCONV = 512, 16, 64, 4
IC = DI // P
NG = 4
QH, QD = 8, 64
QI = QH * QD
QC = QI // P
NE, EF, CAP = 8, 1024, N * 2 // 8
SIM_EPS = 1e-8
DECAY_TOP = 1.0 - 2.0 ** -24
DECAY_HALF = -2.0 ** -16
DECAY_GRID = 384.0
SCALE = QD ** -0.5

ATTN_STEPS, FFN_STEPS = 9, 12
DVE_STEPS, ACT_STEPS = 116, 2

C_ID, C_TRI, C_STRICT, C_ONES, C_BD = 0, 128, 256, 384, 512
C_EVEN = C_BD + KC * P
C_ODD, C_MHALF, C_SLOT = C_EVEN + 1, C_EVEN + 2, C_EVEN + 6
C_ALL = C_SLOT + 8


def shape_constants():
    c = np.zeros((P, C_ALL), np.float32)
    i = np.arange(P)
    c[:, C_ID:C_ID + P] = np.eye(P)
    c[:, C_TRI:C_TRI + P] = i[None, :] >= i[:, None]
    c[:, C_STRICT:C_STRICT + P] = i[None, :] > i[:, None]
    c[:, C_ONES:C_ONES + P] = 1.0
    c[:, C_BD:C_BD + KC * P] = (i // HD)[:, None] == (np.arange(KC * P) // VA)[None, :]
    c[:, C_EVEN] = (i // HD) % 2 == 0
    c[:, C_ODD] = (i // HD) % 2 == 1
    c[:, C_MHALF:C_MHALF + 4] = -0.5
    c[:, C_SLOT:C_SLOT + 8] = 512.0 * np.arange(8)
    return c


class Steps:

    def __init__(self, eng, sem):
        self.eng, self.sem, self.base, self.n = eng, sem, 0, 0

    def loop(self, it, per):
        self.enter()
        self.per = per
        self.at(it * per)

    def enter(self):
        self.start = self.base + self.n

    def at(self, done):
        self.base, self.n = self.start + done, 0

    def end_loop(self, times):
        assert self.n == self.per, (self.n, self.per)
        self.base, self.n = self.start + times * self.per, 0

    def after(self, ins):
        self.n += 1
        ins.then_inc(self.sem, 1)
        self.eng.wait_ge(self.sem, self.base + self.n)

    def apart(self, ins):
        self.n += 1
        ins.then_inc(self.sem, 1)
        hold(self.eng, self.sem, self.base + self.n)


def hold(eng, sem, value):
    eng.wait_ge(sem, value)
    eng.sem_inc(HELD[0], 1)


HELD = [None]


def attention_and_ffn(eng, body):
    body(0, (0, 0), None)
    with eng.Fori(0, L - 1) as l:
        with eng.Fori(0, PAIRS - 1) as p:
            body(l * PAIRS + p + 1, (l, p + 1), (l, p))
        body(l * PAIRS + PAIRS, (l + 1, 0), (l, PAIRS - 1))
    with eng.Fori(0, PAIRS - 1) as p:
        body((L - 1) * PAIRS + p + 1, (L - 1, p + 1), (L - 1, p))
    body(L * PAIRS, None, (L - 1, PAIRS - 1))


class Arena:

    def __init__(self, tile, at):
        self.tile, self.at, self.top = tile, at, at

    def __call__(self, *shape, rows=P):
        n = int(np.prod(shape))
        part = self.tile[0:rows, self.at:self.at + n]
        self.at += n
        if len(shape) == 2:
            part = part.rearrange("p (a b) -> p a b", a=shape[0])
        elif len(shape) == 3:
            part = part.rearrange("p (a b c) -> p a b c", a=shape[0], b=shape[1])
        return part


def decoder(nc, t, out):
    ctx = ExitStack()

    def sem(name):
        return ctx.enter_context(nc.semaphore(name))

    ts = bass.ts

    ARENA = 51 * 1024
    arena = ctx.enter_context(nc.sbuf_tensor("arena", [P, ARENA], F32))
    keep = Arena(arena, 0)
    xst = keep(NT, D)
    hst = keep(NT, D)
    const = keep(C_ALL)
    stats, mv, ve, rstd = keep(TT, 6), keep(TT, 2), keep(TT), keep(TT)
    lgall = keep(NT, 8)
    vecs = keep(7, D)
    ident, tri = const[:, C_ID:C_ID + P], const[:, C_TRI:C_TRI + P]
    strict, ones = const[:, C_STRICT:C_STRICT + P], const[:, C_ONES:C_ONES + P]
    mhalf, slot0 = const[:, C_MHALF:C_MHALF + TT], const[:, C_SLOT:C_SLOT + 8]

    head_mask = const[:, C_BD:C_BD + KC * P]

    PHASE = keep.at

    a = Arena(arena, PHASE)
    wq, wk, wv, wo = a(KC, D), a(KC, D), a(KC, D), a(KC, D)
    w1, w2 = a(KC, FF), a(FM, D)
    qkb, qkb1 = a(2 * KC), a(2 * KC)
    b1 = a(FM)
    hbuf, hT = a(TT, D), a(KC, W)
    expq = a(2 * KC, W)
    qf, kf, kE, kO = a(KC, W), a(KC, W), a(KC, W), a(KC, W)
    vaug, ktok = a(TT, H, VA), a(2, D)
    kvm = a(2, KC, KC * P)
    num = [a(H // HB, P) for _ in range(2)]
    scm = a(8, TT, P)
    den = a(TT, H)
    att, attT = a(TT, D), a(KC, W)
    xb, r1, y, yb = a(TT, D), a(TT, D), a(TT, D), a(TT, D)
    yT, gT = a(KC, W), a(FM, W)
    zero = gT[:, 0:4, :].rearrange("p m t -> p (m t)")
    assert a.at <= ARENA, a.at

    a = Arena(arena, PHASE)
    w_sv, w_st = a(KC, HX), a(2, HX)
    w_gate, w_pair = a(KC, E0), a(KC, 2 * D)
    w_in, w_xp, w_dt, w_out = a(KC, 2 * DI), a(IC, DTR + 2 * NS), a(DI, rows=DTR), a(IC, D)
    w_q, w_k, w_v, w_o = a(KC, QI), a(2, QI), a(2, QI), a(QC, D)
    w_r = a(KC, NE)
    cols = a(2 + 2 * IC + IC * KCONV + 3 * IC)
    sim_b, in_b = cols[:, 0:2], cols[:, 2:2 + 2 * IC]
    cw = cols[:, 10:10 + IC * KCONV].rearrange("p (c k) -> p c k", c=IC)
    conv_b, dt_b, skip = cols[:, 26:30], cols[:, 30:34], cols[:, 34:38]
    rows2 = a(4 * D + 2 * D + NE)
    r_gf, r_bef, r_out, r_xo = (rows2[:, i * D:(i + 1) * D] for i in range(4))
    r_pair, r_r = rows2[:, 4 * D:6 * D], rows2[:, 6 * D:6 * D + NE]
    acol = a(IC, NS)
    xc, xn, xnT = a(TT, D), a(TT, D), a(KC, W)
    ctxT = a(2, W)
    STAGE = a.at
    vT, tT, vsq, tsq, tn, vn, dn = a(W), a(W), a(W), a(W), a(W), a(TT), a(TT, D)
    a = Arena(arena, STAGE)
    lg, gmax, gsum, cmp8, cnt2, coef = a(TT, E0), a(TT), a(TT), a(TT, E0), a(2, TT), a(2, TT)
    eb = a(TT, 2 * D)
    a = Arena(arena, STAGE)
    zs, xs, dt, dtx = a(IC, W), a(IC, W), a(IC, W), a(IC, W)
    dtr, bc = a(W, rows=DTR), a(W, rows=2 * NS)
    Bs, Cs = [a(NG, W) for _ in range(2)], [a(NG, W) for _ in range(2)]
    dA = [a(NG, W) for _ in range(2)]
    uh = [a(NG, W) for _ in range(2)]
    dA_all = arena[:, a.at - 4 * NG * W:a.at - 2 * NG * W]
    xpad = dA_all[:, 0:IC * 2 * (S + 3)].rearrange("p (c s t) -> p c s t", c=IC, s=2)
    assert IC * 2 * (S + 3) <= 2 * NG * W
    soft_e, soft_l, soft_d, soft_r = dA[0], dA[1], uh[0], uh[1]
    assert a.at <= ARENA, a.at
    a = Arena(arena, STAGE)
    qT, kT, vv = a(QC, W), a(QC, W), a(TT, QI)
    mx, nm, sm = a(4, 2), a(4, 2), a(TT, QH)
    pexp, pT = [a(2, S) for _ in range(2)], [a(4, P) for _ in range(2)]
    at2, at2T = [a(QI) for _ in range(2)], [a(QC, P) for _ in range(2)]

    a = Arena(arena, STAGE)
    cmp3, cnt, sel, top = a(NT, NE), a(NT, NE), a(NT, NE), [a(NT, NE) for _ in range(2)]
    picked, before, rank = a(NT, NE), a(NT, NE), a(NT, NE)
    lt, gate, rk, base, over, place = ([a(NT) for _ in range(2)] for _ in range(6))
    gexp = a(NT)
    into = [a(NT).bitcast(I32) for _ in range(2)]
    outof = [a(NT).bitcast(I32) for _ in range(2)]
    weights_at = a.at
    w1e, w2e = [a(KC, EF) for _ in range(2)], [a(EF // P, D) for _ in range(2)]
    b1e, b2e = [a(EF // P) for _ in range(2)], [a(D) for _ in range(2)]
    xg, xgT, gTe, ye = [a(TT, D) for _ in range(2)], a(KC, W), a(EF // P, W), [a(TT, D) for _ in range(2)]
    back = arena[:, weights_at:weights_at + 2 * NT * D].rearrange("p (i d) -> p i d", d=D)
    assert a.at <= ARENA, a.at
    rows_to = nc.dram_tensor("rows_to_experts", (NE * CAP, D), F32, kind="Internal").ap()
    rows_back = nc.dram_tensor("rows_from_experts", (NE * CAP, D), F32, kind="Internal").ap()

    pa = [ctx.enter_context(nc.psum_tensor(f"pa{i}", [P, 512], F32)) for i in range(4)]
    pt = [ctx.enter_context(nc.psum_tensor(f"pt{i}", [P, 512], F32)) for i in range(2)]
    po = [ctx.enter_context(nc.psum_tensor(f"po{i}", [P, 512], F32)) for i in range(2)]

    const_in, x_in = sem("const_in"), [sem(f"x_in{p}") for p in range(PAIRS)]
    qkv_w_in, wo_in, w1_in, w2_in = sem("qkv_w_in"), sem("wo_in"), sem("w1_in"), sem("w2_in")
    bvo_in, ln1_in, ln2_in = sem("bvo_in"), sem("ln1_in"), sem("ln2_in")
    dve_step, pool_step, act_step = sem("dve_step"), sem("pool_step"), sem("act_step")
    var_ready, rstd_ready = sem("var_ready"), sem("rstd_ready")
    h_ready, hbuf_ready, xb_ready = sem("h_ready"), sem("hbuf_ready"), sem("xb_ready")
    tr_done, tr_out = sem("tr_done"), sem("tr_out")
    ytr_done, ytr_out = sem("ytr_done"), sem("ytr_out")
    qk_done, min_ready, exp_ready = sem("qk_done"), sem("min_ready"), sem("exp_ready")
    qf_ready, kf_ready, keo_ready = sem("qf_ready"), sem("kf_ready"), sem("keo_ready")
    v_done, vaug_ready = sem("v_done"), sem("vaug_ready")
    kv_done, kvm_ready = sem("kv_done"), sem("kvm_ready")
    sc_done, scm_ready, av_done, att_ready = sem("sc_done"), sem("scm_ready"), sem("av_done"), sem("att_ready")
    num_out, numT_done = sem("num_out"), sem("numT_done")
    wo_done, r1_ready, y_ready, yb_ready = sem("wo_done"), sem("r1_ready"), sem("y_ready"), sem("yb_ready")
    up_done, gelu_ready, down_done, down_out = sem("up_done"), sem("gelu_ready"), sem("down_done"), sem("down_out")
    zero_ready, zeroed = sem("zero_ready"), sem("zeroed")
    out_done = sem("out_done")
    w_in_2, ctx_in, a_exp, a_ready = sem("w_in_2"), sem("ctx_in"), sem("a_exp"), sem("a_ready")
    xn_ready, xc_ready, x_kept, xf_kept = sem("xn_ready"), sem("xc_ready"), sem("x_kept"), sem("xf_kept")
    tr2_done, tr2_out = sem("tr2_done"), sem("tr2_out")
    vt_done, vt_ready, nrm_done, nrm_ready, dots_done = (sem(n) for n in ("vt_done", "vt_ready", "nrm_done", "nrm_ready", "dots_done"))
    gate_done, gl_ready, ge_ready, pair_done, eb_ready, sil_ready = (
        sem(n) for n in ("gate_done", "gl_ready", "ge_ready", "pair_done", "eb_ready", "sil_ready"))
    in_done, in_out, conv_ready, xs_ready, xp_done, xp_out = (
        sem(n) for n in ("in_done", "in_out", "conv_ready", "xs_ready", "xp_done", "xp_out"))
    dtp_done, soft_ready, dt_ready, bc_done, bc_out = (sem(n) for n in ("dtp_done", "soft_ready", "dt_ready", "bc_done", "bc_out"))
    da_ready, scan_done, hc_ready, ysum_done, yg_ready, proj_done = (
        sem(n) for n in ("da_ready", "scan_done", "hc_ready", "ysum_done", "yg_ready", "proj_done"))
    qkv_done, qkv_out, s2_done, nm_ready, pexp_ready = (sem(n) for n in ("qkv_done", "qkv_out", "s2_done", "nm_ready", "pexp_ready"))
    pT_done, pT_out, av2_done, at2_ready, wo2_done = (sem(n) for n in ("pT_done", "pT_out", "av2_done", "at2_ready", "wo2_done"))
    route_done, wo2_out = sem("route_done"), sem("wo2_out")
    soft_e_ready, soft_u_ready = sem("soft_e_ready"), sem("soft_u_ready")

    logits_ready, sel_ready, rank_done, lt_ready, gexp_ready, places_ready = (
        sem(n) for n in ("logits_ready", "sel_ready", "rank_done", "lt_ready", "gexp_ready", "places_ready"))
    scattered, tr3_done, tr3_out, up3_done, gelu3_ready = (sem(n) for n in ("scattered", "tr3_done", "tr3_out", "up3_done", "gelu3_ready"))
    we_in, xg_in, down3_done, ye_ready, ye_kept = ([sem(f"{n}{j}") for j in range(2)] for n in ("we_in", "xg_in", "down3_done", "ye_ready", "ye_kept"))
    back_in, final_ready = [sem(f"back_in{p}") for p in range(PAIRS)], sem("final_ready")
    HELD[0] = sem("held")
    V_BV, V_BO, V_G1, V_BE1, V_B2, V_G2, V_BE2 = range(7)
    LAYERS_DONE = 2 * PAIRS * (L + 1)
    W2_IN = 16 * (9 + 6 + 4)
    GROUPS = 2 * PAIRS + 4 * L * PAIRS
    TR2, XN = 14, 5

    def row(i, n):
        return vecs[:, i, :].unsqueeze(1).broadcast_to([P, n, D])

    def two(tile, s):
        return tile[:, 2 * s:2 * s + 2, :]

    block = ctx.enter_context(nc.Block())

    @block.sync
    def _(sp):
        sp.dma_start(const, t["consts"]).then_inc(const_in, 16)
        for p in range(PAIRS):
            sp.dma_start(xst[:, TT * p:TT * p + TT, :],
                         t["x"][p * W:(p + 1) * W, :].rearrange("(t p) d -> p t d", p=P)).then_inc(x_in[p], 16)
        def layer_weights(l, first):
            def after(sem, per_pair):
                if not first:
                    sp.wait_ge(sem, l * PAIRS * per_pair)

            after(v_done, 2)
            for tile, name in ((wq, "L0_attn_Wq"), (wk, "L0_attn_Wk"), (wv, "L0_attn_Wv")):
                sp.dma_start(tile, t[name][l].rearrange("(k p) n -> p k n", p=P)).then_inc(qkv_w_in, 16)
            after(kf_ready, KC)
            sp.dma_start(qkb, t["qk_bias"][l]).then_inc(qkv_w_in, 16)
            after(vaug_ready, 2)
            after(xb_ready, 1)
            sp.dma_start(vecs[:, V_BV:V_G1, :], t["rows"][l, V_BV:V_G1].partition_broadcast(P)).then_inc(bvo_in, 16)
            after(wo_done, 2)
            sp.dma_start(wo, t["L0_attn_Wo"][l].rearrange("(k p) n -> p k n", p=P)).then_inc(wo_in, 16)
            after(y_ready, 2)
            sp.dma_start(vecs[:, V_G1:V_B2, :], t["rows"][l, V_G1:V_B2].partition_broadcast(P)).then_inc(ln1_in, 16)
            after(gelu_ready, FM)
            sp.dma_start(w1, t["L0_attn_W1"][l].rearrange("(k p) n -> p k n", p=P)).then_inc(w1_in, 16)
            sp.dma_start(b1, t["b1_cols"][l]).then_inc(w1_in, 16)
            after(down_done, 2)
            sp.dma_start(w2, t["L0_attn_W2"][l].rearrange("(m p) n -> p m n", p=P)).then_inc(w2_in, 16)
            if not first:
                sp.wait_ge(h_ready, 2 * PAIRS + 2 * l * PAIRS)
            sp.dma_start(vecs[:, V_B2:, :], t["rows"][l, V_B2:].partition_broadcast(P)).then_inc(ln2_in, 16)

        layer_weights(0, True)
        sp.wait_ge(zero_ready, 1)
        for q in range(4):
            sp.dma_start(rows_to.rearrange("(q p r) d -> q p (r d)", q=4, p=P)[q], zero).then_inc(zeroed, 16)
        with sp.Fori(1, L) as l:
            layer_weights(l, False)
        sp.wait_ge(h_ready, LAYERS_DONE)
        n_w2 = 0
        for dst, name in ((w_sv, "sim_wv"), (w_gate, "gate"), (w_pair, "pair_w"), (w_in, "ssm_in"), (w_xp, "ssm_xp"),
                          (w_out, "ssm_out"), (w_q, "L1_xattn_Wq"), (w_o, "L1_xattn_Wo"), (w_r, "L1_ffn_Wr")):
            sp.dma_start(dst, t[name].rearrange("(k p) n -> p k n", p=P)).then_inc(w_in_2, 16)
            n_w2 += 16
        for dst, name in ((w_st, "sim_wt"), (w_k, "L1_xattn_Wk"), (w_v, "L1_xattn_Wv")):
            sp.dma_start(dst[:, 0, :], t[name][0:P, :]).then_inc(w_in_2, 16)
            sp.dma_start(dst[0:CT - P, 1, :], t[name][P:CT, :]).then_inc(w_in_2, 16)
            n_w2 += 32
        sp.dma_start(w_dt, t["ssm_dt"]).then_inc(w_in_2, 16)
        sp.dma_start(cols, t["cols"]).then_inc(w_in_2, 16)
        sp.dma_start(rows2, t["rows2"].partition_broadcast(P)).then_inc(w_in_2, 16)
        sp.dma_start(acol, t["a_log"]).then_inc(w_in_2, 16)
        assert n_w2 + 64 == W2_IN
        def context(p):
            sp.dma_start(ctxT[:, 0, :], t["ctxT"][0:P, ts(p, W)]).then_inc(ctx_in, 16)
            sp.dma_start(ctxT[0:CT - P, 1, :], t["ctxT"][P:CT, ts(p, W)]).then_inc(ctx_in, 16)

        context(0)
        with sp.Fori(1, PAIRS) as p:
            sp.wait_ge(qkv_done, 12 * p)
            context(p)
        sp.wait_ge(logits_ready, PAIRS)
        for first in (True, False):
            if first:
                loads = ExitStack()
                q = 0
            else:
                loads = sp.Fori(1, NE // 2)
            with loads as at:
                q = 0 if first else at
                for j in range(2):
                    if not first:
                        sp.wait_ge(ye_ready[j], 2 * q)
                    e = 2 * q + j
                    sp.dma_start(w1e[j], t["L1_ffn_W1"][e].rearrange("(k p) n -> p k n", p=P)).then_inc(we_in[j], 16)
                    sp.dma_start(b1e[j], t["b1e_cols"][e]).then_inc(we_in[j], 16)
                    sp.dma_start(w2e[j], t["L1_ffn_W2"][e].rearrange("(m p) n -> p m n", p=P)).then_inc(we_in[j], 16)
                    sp.dma_start(b2e[j], t["L1_ffn_b2"][e].partition_broadcast(P)).then_inc(we_in[j], 16)
                    if first and j == 0:
                        sp.wait_ge(scattered, 16 * 2 * NT)
                    sp.dma_start(xg[j], rows_to[ts(e, CAP), :].rearrange("(t p) d -> p t d", p=P)).then_inc(xg_in[j], 16)
        for p in range(PAIRS):
            sp.wait_ge(final_ready, TT * p + TT)
            sp.dma_start(out[p * W:(p + 1) * W, :].rearrange("(t p) d -> p t d", p=P), xst[:, TT * p:TT * p + TT, :]).then_inc(out_done, 16)
        sp.wait_ge(out_done, 16 * PAIRS)
    @block.gpsimd
    def _(pool):
        step = Steps(pool, pool_step)

        def deviations(n, c, k):
            hold(pool, var_ready, n)
            step.apart(nc.gpsimd.tensor_scalar(ve[:, c:c + k], mv[:, c:c + k, 1], LN_EPS, None, ALU.add))
            nc.gpsimd.tensor_tensor(rstd[:, c:c + k], ve[:, c:c + k], mhalf[:, 0:k], ALU.pow).then_inc(rstd_ready, 1)

        nc.gpsimd.memset(zero, 0.0).then_inc(zero_ready, 1)
        hold(pool, const_in, 16)
        with pool.Fori(0, PAIRS) as p:
            step.loop(p, 2)
            for s in range(2):
                deviations(2 * p + s + 1, 2 * s, 2)
            step.end_loop(PAIRS)
        step.enter()

        def layer(n, attn, ffn):
            m = n - 1
            if attn:
                la, p = attn
                hold(pool, h_ready, 2 * n + 2)
                if ffn:
                    hold(pool, tr_done, 6 * m + 2)
                nc.gpsimd.tensor_copy(hbuf, hst[:, ts(p, TT), :]).then_inc(hbuf_ready, 1)
            if ffn:
                step.at(m * 4)
                lf = ffn[0]
                for s in range(2):
                    deviations(2 * PAIRS + 4 * m + s + 1, 2 * s, 2)
            if attn:
                hold(pool, bvo_in, 16 * la + 16)
                if ffn:
                    hold(pool, r1_ready, 2 * m + 2)
                nc.gpsimd.tensor_tensor(xb, hst[:, ts(p, TT), :], row(V_BO, TT), ALU.add).then_inc(xb_ready, 1)
            if ffn:
                hold(pool, ln2_in, 16 * lf + 16)
                for s in range(2):
                    hold(pool, y_ready, 2 * m + s + 1)
                    nc.gpsimd.tensor_tensor(two(yb, s), two(y, s), row(V_B2, 2), ALU.add).then_inc(yb_ready, 1)
                for s in range(2):
                    deviations(2 * PAIRS + 4 * m + 2 + s + 1, 2 * s, 2)

        attention_and_ffn(pool, layer)
        step.at(L * PAIRS * 4)
        pool.sem_inc(x_kept, 1)
        pool.sem_inc(xf_kept, 1)
        with pool.Fori(0, PAIRS) as p:
            step.loop(p, 6)
            for k in range(5):
                deviations(GROUPS + 6 * p + k + 1, 0, TT)
            hold(pool, xc_ready, p + 1)
            nc.gpsimd.tensor_copy(xst[:, ts(p, TT), :], xc).then_inc(x_kept, 1)
            deviations(GROUPS + 6 * p + 6, 0, TT)
            hold(pool, xn_ready, XN * p + XN)
            nc.gpsimd.tensor_copy(hst[:, ts(p, TT), :], xn).then_inc(xf_kept, 1)
            step.end_loop(PAIRS)
        pool.wait_ge(zeroed, 16 * 4)
        pool.wait_ge(places_ready, 1)
        pool.wait_ge(xf_kept, PAIRS + 1)
        for i in range(NT):
            for k in range(2):
                nc.gpsimd.indirect_dma_start(
                    out=rows_to, out_offset=bass.IndirectOffsetOnAxis(ap=into[k][:, i:i + 1], axis=0), in_=hst[:, i, :], in_offset=None,
                    bounds_check=NE * CAP - 1, oob_is_err=False).then_inc(scattered, 16)
        with pool.Fori(0, NE // 2) as q:
            for j in range(2):
                hold(pool, ye_ready[j], 2 * q + 2)
                nc.gpsimd.dma_start(rows_back[ts(2 * q + j, CAP), :].rearrange("(t p) d -> p t d", p=P), ye[j]).then_inc(ye_kept[j], 16)
        for j in range(2):
            pool.wait_ge(ye_kept[j], 16 * (NE // 2))
        for i in range(NT):
            for k in range(2):
                nc.gpsimd.indirect_dma_start(
                    out=back[:, 2 * i + k, :], out_offset=None, in_=rows_back,
                    in_offset=bass.IndirectOffsetOnAxis(ap=outof[k][:, i:i + 1], axis=0),
                    bounds_check=NE * CAP - 1, oob_is_err=False).then_inc(back_in[i // TT], 16)

    @block.scalar
    def _(act):
        def layer(n, attn, ffn):
            m = n - 1

            def evacuate(k, dst, src):
                act.wait_ge(tr_done, 6 * n + k + 1)
                nc.scalar.copy(dst, src).then_inc(tr_out, 1)

            if attn:
                for k in range(KC):
                    evacuate(k, hT[:, k, :], pt[k][:, :])
                for j in range(2 * KC):
                    act.wait_ge(min_ready, 4 * n + j + 1)
                    nc.scalar.activation(expq[:, j, :], expq[:, j, :], ACT.Exp).then_inc(exp_ready, 1)
            if ffn:
                for s in range(2):
                    act.wait_ge(ytr_done, 2 * m + s + 1)
                    nc.scalar.copy(yT[:, :, s * S:(s + 1) * S], pt[s][:, :].rearrange("p (k t) -> p k t", k=KC)).then_inc(ytr_out, 1)
                act.wait_ge(w1_in, 32 * ffn[0] + 32)
            for half in range(2):
                if ffn:
                    for i in range(FM // 2 * half, FM // 2 * (half + 1)):
                        act.wait_ge(up_done, FM * m + i + 1)
                        nc.scalar.activation(gT[:, i, :], pa[i % 4][:, :], ACT.Gelu, bias=b1[:, i:i + 1]).then_inc(gelu_ready, 1)
                if attn and half == 0:
                    for s in range(2):
                        evacuate(2 + s, ktok[:, s, :], pt[s][:, 0:D])
            def weighed(tile):
                act.wait_ge(av_done, 4 * n + tile + 1)
                nc.scalar.copy(num[tile % 2], po[tile % 2][:, :].rearrange("p (b q) -> p b q", b=H // HB)).then_inc(num_out, 1)

            def attention_evacuated(s):
                evacuate(4 + s, attT[:, :, s * S:(s + 1) * S], pt[s][:, :].rearrange("p (k t) -> p k t", k=KC))

            if not ffn:
                act.wait_ge(zeroed, 16 * 4)
            if attn:
                weighed(0)
                weighed(1)
                act.wait_ge(numT_done, 4 * n + 1)
                weighed(2)
                attention_evacuated(0)
                act.wait_ge(numT_done, 4 * n + 2)
                weighed(3)
                attention_evacuated(1)

        attention_and_ffn(act, layer)
        a_ = nc.scalar.activation
        step = Steps(act, act_step)
        act.wait_ge(w_in_2, W2_IN)
        a_(acol, acol, ACT.Exp).then_inc(a_exp, 1)
        with act.Fori(0, PAIRS) as p:
            step.loop(p, ACT_STEPS)

            def input_transposed(k):
                for s in range(2):
                    act.wait_ge(tr2_done, TR2 * p + k + s + 1)
                    nc.scalar.copy(xnT[:, :, s * S:(s + 1) * S], pt[s][:, :].rearrange("p (k t) -> p k t", k=KC)).then_inc(tr2_out, 1)

            input_transposed(0)
            for i, (full, square) in enumerate(((vT, vsq), (tT, tsq))):
                act.wait_ge(vt_done, 2 * p + i + 1)
                a_(full, pa[i][:, :], ACT.Identity, bias=sim_b[:, i:i + 1]).then_inc(vt_ready, 1)
                a_(square, pa[i][:, :], ACT.Square, bias=sim_b[:, i:i + 1]).then_inc(vt_ready, 1)
            act.wait_ge(nrm_done, p + 1)
            a_(vn, pa[2][:, 0:TT], ACT.Sqrt).then_inc(nrm_ready, 1)
            a_(tn, pa[3][:, :], ACT.Sqrt).then_inc(nrm_ready, 1)

            input_transposed(2)
            act.wait_ge(gl_ready, p + 1)
            a_(lg, lg, ACT.Exp).then_inc(ge_ready, 1)
            for i in range(TT):
                act.wait_ge(eb_ready, TT * p + i + 1)
                a_(eb[:, i, :], eb[:, i, :], ACT.Silu).then_inc(sil_ready, 1)

            input_transposed(4)
            for m in range(2 * IC):
                act.wait_ge(in_done, 8 * p + m + 1)
                if m < IC:
                    a_(xpad[:, m, :, 3:3 + S], pa[m % 4][:, :].rearrange("p (s t) -> p s t", s=2), ACT.Identity,
                       bias=in_b[:, m:m + 1]).then_inc(in_out, 1)
                else:
                    a_(zs[:, m - IC, :], pa[m % 4][:, :], ACT.Silu, bias=in_b[:, m:m + 1]).then_inc(in_out, 1)
            for c in range(IC):
                act.wait_ge(conv_ready, IC * p + c + 1)
                a_(xs[:, c, :], xs[:, c, :], ACT.Silu).then_inc(xs_ready, 1)
            act.wait_ge(xp_done, 2 * p + 2)
            nc.scalar.copy(dtr, pa[0][0:DTR, :]).then_inc(xp_out, 1)
            nc.scalar.copy(bc, pa[1][0:2 * NS, :]).then_inc(xp_out, 1)
            for c in range(IC):
                act.wait_ge(dtp_done, IC * p + c + 1)
                a_(soft_e[:, c, :], pa[c][:, :], ACT.Abs, bias=dt_b[:, c:c + 1])
                last = a_(dt[:, c, :], pa[c][:, :], ACT.Relu, bias=dt_b[:, c:c + 1])
            step.after(last)
            a_(soft_e, soft_e, ACT.Exp, scale=-1.0).then_inc(soft_e_ready, 1)

            def row_spread(g, n):
                for which, (src, dst) in enumerate(((pt, Bs), (po, Cs))):
                    act.wait_ge(bc_done, 32 * p + 8 * g + 2 * n + which + 1)
                    if n == 0 and which == 0 and g >= 2:
                        act.wait_ge(hc_ready, 16 * p + 4 * (g - 1))
                    nc.scalar.copy(dst[g % 2][:, n, :], src[n % 2][:, :]).then_inc(bc_out, 1)

            act.wait_ge(soft_u_ready, p + 1)
            step.after(a_(soft_l, soft_d, ACT.Ln))
            a_(soft_r, soft_l, ACT.Exp, scale=-1.0).then_inc(soft_ready, 1)
            for n in range(NG):
                row_spread(0, n)
            act.wait_ge(dt_ready, p + 1)
            for i in range(4 * IC):
                g, c = i // IC, i % IC
                if i >= 2:
                    act.wait_ge(scan_done, 16 * p + i - 1)
                for n in range(NG):
                    last = a_(dA[i % 2][:, n, :], dt[:, c, :], ACT.Exp, scale=acol[:, c, NG * g + n:NG * g + n + 1])
                last.then_inc(da_ready, 1)
                if g + 1 < NS // NG:
                    row_spread(g + 1, c)

            input_transposed(6)
            for r in range(12):
                act.wait_ge(qkv_done, 12 * p + r + 1)
                nc.scalar.copy((qT, kT, vv)[r // 4][:, r % 4, :], pa[r % 4][:, :]).then_inc(qkv_out, 1)
            for u in range(16 + 4):
                if u < 16:
                    tile, h0 = u // 4, 4 * (u % 4 // 2) + u % 2
                    act.wait_ge(nm_ready, 16 * p + u + 1)
                    if u >= 2:
                        act.wait_ge(pT_done, 16 * p + u - 1)
                    for b in range(2):
                        last = a_(pexp[u % 2][:, b, :], pa[u % 2][:, b * S:(b + 1) * S], ACT.Exp, bias=nm[:, u % 4, b:b + 1], scale=SCALE,
                                  accum_out=sm[:, tile, h0 + 2 * b:h0 + 2 * b + 1])
                    last.then_inc(pexp_ready, 1)
                if u >= 7 and (u - 7) % 4 == 0:
                    tile = (u - 7) // 4
                    act.wait_ge(tr2_done, TR2 * p + 8 + tile + 1)
                    nc.scalar.copy(at2T[tile % 2], pt[tile % 2][:, :].rearrange("p (k t) -> p k t", k=QC)).then_inc(tr2_out, 1)
            input_transposed(12)
            step.end_loop(PAIRS)
        act.wait_ge(lt_ready, 1)
        a_(gexp, gexp, ACT.Exp).then_inc(gexp_ready, 1)
        with act.Fori(0, NE // 2) as q:
            for j in range(2):
                for s in range(2):
                    act.wait_ge(tr3_done, 4 * q + 2 * j + s + 1)
                    nc.scalar.copy(xgT[:, :, s * S:(s + 1) * S], pt[s][:, :].rearrange("p (k t) -> p k t", k=KC)).then_inc(tr3_out, 1)
                act.wait_ge(we_in[j], 64 * q + 64)
                for m in range(EF // P):
                    act.wait_ge(up3_done, 16 * q + 8 * j + m + 1)
                    a_(gTe[:, m, :], pa[m % 4][:, :], ACT.Gelu, bias=b1e[j][:, m:m + 1]).then_inc(gelu3_ready, 1)

    @block.vector
    def _(dve):
        step = Steps(dve, dve_step)
        v = nc.vector

        def normalise(n, c, src, dst):
            for i, one in enumerate(src):
                last = v.bn_stats(out=stats[:, c + i, :], in_=one)
            step.apart(last)
            for i in range(len(src)):
                last = v.bn_aggr(out=mv[:, c + i, :], in_=stats[:, c + i, :])
            last.then_inc(var_ready, 1)
            dve.wait_ge(rstd_ready, n)
            for i, one in enumerate(src):
                last = v.tensor_scalar(dst[i], one, mv[:, c + i, 0:1], rstd[:, c + i:c + i + 1], ALU.subtract, ALU.mult)
            return last

        step.after(v.memset(vaug, 0.0))
        step.after(v.memset(vaug[:, :, :, HD], 1.0))
        dve.wait_ge(const_in, 16)
        for p in range(PAIRS):
            dve.wait_ge(x_in[p], 16)
        with dve.Fori(0, PAIRS) as p:
            step.loop(p, 2)
            for s in range(2):
                at = [bass.ds(p * TT + 2 * s + i, 1) for i in range(2)]
                normalise(2 * p + s + 1, 2 * s, [xst[:, j, :].rearrange("p a d -> p (a d)") for j in at],
                          [hst[:, j, :].rearrange("p a d -> p (a d)") for j in at]).then_inc(h_ready, 1)
            step.end_loop(PAIRS)
        step.enter()

        def layer(n, attn, ffn):
            m = n - 1
            step.at(n * ATTN_STEPS + m * FFN_STEPS if ffn else 0)

            def statistics(s, rows):
                for i in (2 * s, 2 * s + 1):
                    last = v.bn_stats(out=stats[:, i, :], in_=rows[:, i, :])
                step.apart(last)
                for i in (2 * s, 2 * s + 1):
                    last = v.bn_aggr(out=mv[:, i, :], in_=stats[:, i, :])
                last.then_inc(var_ready, 1)

            def scaled(group, s, rows, dst, gamma):
                dve.wait_ge(rstd_ready, 2 * PAIRS + 4 * m + group + 1)
                for i in (2 * s, 2 * s + 1):
                    last = v.tensor_scalar(dst[:, i, :], rows[:, i, :], mv[:, i, 0:1], rstd[:, i:i + 1], ALU.subtract, ALU.mult)
                step.after(last)
                step.after(v.tensor_tensor(two(dst, s), two(dst, s), row(gamma, 2), ALU.mult))

            if ffn:
                lf, pf = ffn
                dve.wait_ge(xb_ready, m + 1)
                for s in range(2):
                    dve.wait_ge(wo_done, 2 * m + s + 1)
                    v.tensor_tensor(two(r1, s), pa[s][:, :].rearrange("p (t d) -> p t d", t=2), two(xb, s), ALU.add)\
                        .then_inc(r1_ready, 1)
                for s in range(2):
                    dve.wait_ge(r1_ready, 2 * m + s + 1)
                    statistics(s, r1)
                dve.wait_ge(ln1_in, 16 * lf + 16)
                for s in range(2):
                    scaled(s, s, r1, y, V_G1)
                    v.tensor_tensor(two(y, s), two(y, s), row(V_BE1, 2), ALU.add).then_inc(y_ready, 1)
            if attn:
                la = attn[0]
                dve.wait_ge(qkv_w_in, 64 * la + 64)
                step.after(v.tensor_scalar(qkb1, qkb, 1.0, None, ALU.add))
                for j in range(2 * KC):
                    dve.wait_ge(qk_done, 4 * n + j + 1)
                    v.tensor_scalar(expq[:, j, :], pa[j][:, :], qkb[:, j:j + 1], 0.0, ALU.add, ALU.min).then_inc(min_ready, 1)
                for j in range(2 * KC):
                    dve.wait_ge(exp_ready, 4 * n + j + 1)
                    dst = (qf if j < KC else kf)[:, j % KC, :]
                    v.scalar_tensor_tensor(dst, pa[j][:, :], qkb1[:, j:j + 1], expq[:, j, :], ALU.add, ALU.max)\
                        .then_inc(qf_ready if j < KC else kf_ready, 1)
                dve.wait_ge(kf_ready, KC * n + KC)
                v.tensor_scalar(kE, kf, const[:, C_EVEN:C_EVEN + 1], None, ALU.mult).then_inc(keo_ready, 1)
                v.tensor_scalar(kO, kf, const[:, C_ODD:C_ODD + 1], None, ALU.mult).then_inc(keo_ready, 1)
                dve.wait_ge(bvo_in, 16 * la + 16)
                for s in range(2):
                    dve.wait_ge(v_done, 2 * n + s + 1)
                    for i in range(2):
                        last = v.tensor_tensor(vaug[:, 2 * s + i, :, 0:HD],
                                               po[s][:, ts(i, D)].rearrange("p (h e) -> p h e", h=H),
                                               vecs[:, V_BV, :].rearrange("p (h e) -> p h e", h=H), ALU.add)
                    last.then_inc(vaug_ready, 1)
                for i in range(2 * KC):
                    dve.wait_ge(kv_done, 4 * n + i + 1)
                    v.tensor_tensor(kvm[:, i // KC, i % KC, :], pa[i][:, 0:KC * P], head_mask, ALU.mult)\
                        .then_inc(kvm_ready, 1)

            def mask_scores(tile):
                if tile >= 2:
                    dve.wait_ge(av_done, 4 * n + tile - 1)
                for g in range(4):
                    i = 4 * tile + g
                    dve.wait_ge(sc_done, 16 * n + i + 1)
                    v.tensor_tensor(scm[:, i % 8, :, :], pa[g][:, :].rearrange("p (h q) -> p h q", h=4),
                                    tri.unsqueeze(1).broadcast_to([P, 4, P]), ALU.mult).then_inc(scm_ready, 1)

            def divide(tile):
                dve.wait_ge(numT_done, 4 * n + tile + 1)
                num = pt[tile % 2][:, :].rearrange("p (h e) -> p h e", h=H)
                step.after(v.tensor_scalar(den[:, tile, :], num[:, :, HD], ATT_EPS, None, ALU.add))
                step.after(v.reciprocal(den[:, tile, :], den[:, tile, :]))
                v.tensor_tensor(att[:, tile, :].rearrange("p (h e) -> p h e", h=H), num[:, :, 0:HD],
                                den[:, tile, :].unsqueeze(2).broadcast_to([P, H, HD]), ALU.mult).then_inc(att_ready, 1)

            def ffn_residual(s):
                dve.wait_ge(down_done, 2 * m + s + 1)
                dve.wait_ge(yb_ready, 2 * m + s + 1)
                v.tensor_tensor(two(r1, s), po[s][:, :].rearrange("p (t d) -> p t d", t=2), two(yb, s), ALU.add).then_inc(down_out, 1)
                dve.wait_ge(down_out, 2 * m + s + 1)
                statistics(s, r1)

            def ffn_normalised(s):
                scaled(2 + s, s, r1, r1, V_G2)
                v.tensor_tensor(hst[:, bass.ds(pf * TT + 2 * s, 2), :], two(r1, s), row(V_BE2, 2), ALU.add).then_inc(h_ready, 1)

            if attn:
                mask_scores(0)
            if ffn:
                ffn_residual(0)
            if attn:
                mask_scores(1)
            if ffn:
                ffn_residual(1)
            if attn:
                divide(0)
                mask_scores(2)
                divide(1)
            if ffn:
                ffn_normalised(0)
            if attn:
                mask_scores(3)
                divide(2)
            if ffn:
                ffn_normalised(1)
            if attn:
                divide(3)
            assert step.n == (ATTN_STEPS if attn else 0) + (FFN_STEPS if ffn else 0)

        attention_and_ffn(dve, layer)
        step.at(L * PAIRS * (ATTN_STEPS + FFN_STEPS))
        dve.wait_ge(w_in_2, W2_IN)
        dve.wait_ge(a_exp, 1)
        dve.wait_ge(h_ready, LAYERS_DONE)
        v.tensor_scalar(acol, acol, -1.0, None, ALU.mult).then_inc(a_ready, 1)
        dve.wait_ge(a_ready, 1)
        with dve.Fori(0, PAIRS) as p:
            step.loop(p, DVE_STEPS)
            xct, xnt = [xc[:, i, :] for i in range(TT)], [xn[:, i, :] for i in range(TT)]

            def wide(r, n):
                return r.unsqueeze(1).broadcast_to([P, n, r.shape[1]])

            def normalised(k):
                normalise(GROUPS + 6 * p + k + 1, 0, xct, xnt).then_inc(xn_ready, 1)

            dve.wait_ge(x_kept, p + 1)
            at = [bass.ds(p * TT + i, 1) for i in range(TT)]
            step.after(normalise(GROUPS + 6 * p + 1, 0, [hst[:, j, :].rearrange("p a d -> p (a d)") for j in at], xct))
            step.after(v.tensor_tensor(xc, xc, wide(r_gf, TT), ALU.mult))
            step.after(v.tensor_tensor(xc, xc, wide(r_bef, TT), ALU.add))
            step.after(v.tensor_tensor(xc, xc, xst[:, ts(p, TT), :], ALU.add))

            dve.wait_ge(xf_kept, p + 1)
            normalised(1)
            dve.wait_ge(nrm_ready, 2 * p + 2)
            for i in range(TT):
                last = v.tensor_scalar(dn[:, i, :], tn[:, (i // 2) * S:(i // 2 + 1) * S], vn[:, i:i + 1], SIM_EPS, ALU.mult, ALU.max)
            step.after(last)
            step.after(v.reciprocal(dn, dn))
            for s in range(2):
                dve.wait_ge(dots_done, 2 * p + s + 1)
                last = v.tensor_tensor(two(dn, s), po[s][:, :].rearrange("p (t d) -> p t d", t=2), two(dn, s), ALU.mult)
            step.after(last)
            step.after(v.tensor_tensor(xc, xc, dn, ALU.add))

            normalised(2)
            dve.wait_ge(gate_done, p + 1)
            gates = pa[0][:, 0:TT * E0].rearrange("p (t e) -> p t e", t=TT)
            step.after(v.tensor_reduce(gmax, gates, AX, ALU.max))
            v.tensor_tensor(lg, gates, gmax.unsqueeze(2).broadcast_to([P, TT, E0]), ALU.subtract).then_inc(gl_ready, 1)
            for i in range(TT):
                dve.wait_ge(pair_done, TT * p + i + 1)
                v.tensor_tensor(eb[:, i, :], (po[0], pa[1], pa[2], pa[3])[i][:, :], r_pair, ALU.add).then_inc(eb_ready, 1)
            dve.wait_ge(ge_ready, p + 1)
            step.after(v.tensor_reduce(gsum, lg, AX, ALU.add))
            step.after(v.reciprocal(gsum, gsum))
            step.after(v.tensor_tensor(lg, lg, gsum.unsqueeze(2).broadcast_to([P, TT, E0]), ALU.mult))
            for e in range(2):
                step.after(v.tensor_tensor(cmp8, lg, lg[:, :, e:e + 1].broadcast_to([P, TT, E0]), ALU.is_gt))
                if e:
                    step.after(v.tensor_tensor(cmp8[:, :, 0:e], lg[:, :, 0:e], lg[:, :, e:e + 1].broadcast_to([P, TT, e]), ALU.is_ge))
                step.after(v.tensor_reduce(cnt2[:, e, :], cmp8, AX, ALU.add))
                step.after(v.scalar_tensor_tensor(coef[:, e, :], cnt2[:, e, :], float(e), lg[:, :, e], ALU.is_equal, ALU.mult))
            for i in range(TT):
                dve.wait_ge(sil_ready, TT * p + i + 1)
                for e in range(2):
                    step.after(v.scalar_tensor_tensor(xct[i], eb[:, i, e * D:(e + 1) * D], coef[:, e, i:i + 1], xct[i], ALU.mult, ALU.add))

            normalised(3)
            step.after(v.memset(xpad[:, :, :, 0:3], 0.0))
            for tap in range(KCONV):
                for c in range(IC):
                    if tap == 0:
                        dve.wait_ge(in_out, 8 * p + c + 1)
                    at = KCONV - 1 - tap
                    dst = xs[:, c, :].rearrange("p (s t) -> p s t", s=2)
                    src, w_tap = xpad[:, c, :, at:at + S], cw[:, c, at:at + 1]
                    if tap == 0:
                        last = v.tensor_scalar(dst, src, w_tap, conv_b[:, c:c + 1], ALU.mult, ALU.add)
                    else:
                        last = v.scalar_tensor_tensor(dst, src, w_tap, dst, ALU.mult, ALU.add)
                    if tap == KCONV - 1:
                        last.then_inc(conv_ready, 1)
                if tap < KCONV - 1:
                    step.after(last)
            dve.wait_ge(soft_e_ready, p + 1)
            v.tensor_scalar(soft_d, soft_e, 1.0, None, ALU.add).then_inc(soft_u_ready, 1)
            dve.wait_ge(soft_u_ready, p + 1)
            step.after(v.scalar_tensor_tensor(soft_e, soft_d, 1.0, soft_e, ALU.subtract, ALU.subtract))
            dve.wait_ge(soft_ready, p + 1)
            v.scalar_tensor_tensor(soft_l, soft_d, 1.0, soft_l, ALU.is_gt, ALU.mult)
            step.after(v.scalar_tensor_tensor(soft_e, soft_e, -1.0, soft_r, ALU.mult, ALU.mult))
            step.after(v.tensor_tensor(soft_l, soft_l, soft_e, ALU.add))
            v.tensor_tensor(dt, dt, soft_l, ALU.add).then_inc(dt_ready, 1)
            dve.wait_ge(dt_ready, p + 1)
            step.after(v.tensor_tensor(dtx, dt, xs, ALU.mult))
            for i in range(4 * IC):
                g, c = i // IC, i % IC
                decay, h = dA[i % 2], uh[i % 2]
                flat = "p n t -> p (n t)"
                dve.wait_ge(da_ready, 16 * p + i + 1)
                step.after(v.tensor_scalar(decay, decay, DECAY_TOP, DECAY_HALF, ALU.min, ALU.add))
                if i >= 2:
                    dve.wait_ge(ysum_done, 16 * p + i - 1)
                dve.wait_ge(bc_out, 32 * p + 8 * g + 8)
                v.tensor_tensor(h, dtx[:, c, :].unsqueeze(1).broadcast_to([P, NG, W]), Bs[g % 2], ALU.mult)
                step.after(v.tensor_scalar(decay, decay, DECAY_GRID, DECAY_GRID, ALU.add, ALU.subtract))
                step.after(v.memset(decay.rearrange("p n (s t) -> p (n s) t", s=2)[:, :, 0], 0.0))
                v.tensor_tensor_scan(h.rearrange(flat), decay.rearrange(flat), h.rearrange(flat), 0.0, ALU.mult, ALU.add).then_inc(scan_done, 1)
                dve.wait_ge(scan_done, 16 * p + i + 1)
                v.tensor_tensor(h, h, Cs[g % 2], ALU.mult).then_inc(hc_ready, 1)
            for c in range(IC):
                dve.wait_ge(ysum_done, 16 * p + 12 + c + 1)
                step.after(v.scalar_tensor_tensor(dtx[:, c, :], xs[:, c, :], skip[:, c:c + 1], pa[c][:, :], ALU.mult, ALU.add))
                v.tensor_tensor(dtx[:, c, :], dtx[:, c, :], zs[:, c, :], ALU.mult).then_inc(yg_ready, 1)
            for s in range(2):
                dve.wait_ge(proj_done, 2 * p + s + 1)
                step.after(v.tensor_tensor(two(xc, s), po[s][:, :].rearrange("p (t d) -> p t d", t=2), two(xc, s), ALU.add))
            step.after(v.tensor_tensor(xc, xc, wide(r_out, TT), ALU.add))

            normalised(4)
            for u in range(16 + 5):
                if u < 16:
                    dve.wait_ge(s2_done, 16 * p + u + 1)
                    step.after(v.tensor_reduce(mx[:, u % 4, :], pa[u % 2][:, :].rearrange("p (b j) -> p b j", b=2), AX, ALU.max))
                    v.tensor_scalar(nm[:, u % 4, :], mx[:, u % 4, :], -SCALE, None, ALU.mult).then_inc(nm_ready, 1)
                if 1 <= u < 17:
                    w = u - 1
                    dve.wait_ge(pT_done, 16 * p + w + 1)
                    if w >= 2:
                        dve.wait_ge(av2_done, 16 * p + w - 1)
                    v.tensor_copy(pT[w % 2], pa[2 + w % 2][:, :].rearrange("p (b i) -> p b i", b=4)).then_inc(pT_out, 1)
                if u >= 6 and (u - 6) % 4 == 0 and u <= 18:
                    tile = (u - 6) // 4
                    dve.wait_ge(av2_done, 16 * p + 4 * tile + 4)
                    step.after(v.reciprocal(sm[:, tile, :], sm[:, tile, :]))
                    v.tensor_tensor(at2[tile % 2].rearrange("p (h d) -> p h d", h=QH), po[tile % 2][:, :].rearrange("p (h d) -> p h d", h=QH),
                                    sm[:, tile, :].unsqueeze(2).broadcast_to([P, QH, QD]), ALU.mult).then_inc(at2_ready, 1)
                if u >= 8 and (u - 8) % 4 == 0:
                    tile = (u - 8) // 4
                    dve.wait_ge(wo2_done, 4 * p + tile + 1)
                    v.tensor_tensor(xct[tile], po[tile % 2][:, 0:D], xct[tile], ALU.add).then_inc(wo2_out, 1)
            dve.wait_ge(wo2_out, 4 * p + 4)
            v.tensor_tensor(xc, xc, wide(r_xo, TT), ALU.add).then_inc(xc_ready, 1)
            dve.wait_ge(xc_ready, p + 1)
            normalised(5)
            dve.wait_ge(route_done, p + 1)
            v.tensor_tensor(lgall[:, ts(p, TT), :], pa[0][:, 0:TT * NE].rearrange("p (t e) -> p t e", t=TT), wide(r_r, TT), ALU.add)\
                .then_inc(logits_ready, 1)
            step.end_loop(PAIRS)
        def each(row):
            return row.unsqueeze(2).broadcast_to([P, NT, NE])

        dve.wait_ge(logits_ready, PAIRS)
        for e in range(NE):
            if e:
                v.tensor_tensor(cmp3[:, :, 0:e], lgall[:, :, 0:e], lgall[:, :, e:e + 1].broadcast_to([P, NT, e]), ALU.is_ge)
            step.after(v.tensor_tensor(cmp3[:, :, e:NE], lgall[:, :, e:NE], lgall[:, :, e:e + 1].broadcast_to([P, NT, NE - e]), ALU.is_gt))
            step.after(v.tensor_reduce(cnt[:, :, e], cmp3, AX, ALU.add))
        v.tensor_scalar(sel, cnt, 2.0, None, ALU.is_lt).then_inc(sel_ready, 1)
        for k in range(2):
            last = v.tensor_scalar(top[k], cnt, float(k), None, ALU.is_equal)
        step.after(last)
        for k in range(2):
            step.after(v.tensor_tensor(picked, top[k], lgall, ALU.mult))
            step.after(v.tensor_reduce(lt[k], picked, AX, ALU.add))
        v.tensor_tensor(gexp, lt[1], lt[0], ALU.subtract).then_inc(lt_ready, 1)
        dve.wait_ge(rank_done, 1)
        total = pa[1][:, 0:NT * NE].rearrange("p (t e) -> p t e", t=NT)
        step.after(v.memset(before[:, 0, :], 0.0))
        for i in range(1, NT):
            step.after(v.tensor_tensor(before[:, i, :], total[:, i - 1, :], before[:, i - 1, :], ALU.add))
        step.after(v.tensor_tensor(rank, pa[0][:, 0:NT * NE].rearrange("p (t e) -> p t e", t=NT), before, ALU.add))
        dve.wait_ge(gexp_ready, 1)
        step.after(v.tensor_scalar(gate[0], gexp, 1.0, None, ALU.add))
        step.after(v.reciprocal(gate[0], gate[0]))
        step.after(v.tensor_tensor(gate[1], gate[0], gexp, ALU.mult))
        for k in range(2):
            step.after(v.tensor_tensor(picked, top[k], rank, ALU.mult))
            step.after(v.tensor_reduce(rk[k], picked, AX, ALU.add))
            step.after(v.tensor_tensor(picked, top[k], slot0.unsqueeze(1).broadcast_to([P, NT, NE]), ALU.mult))
            step.after(v.tensor_reduce(base[k], picked, AX, ALU.add))
            step.after(v.tensor_scalar(over[k], rk[k], float(CAP), float(NE * CAP), ALU.is_ge, ALU.mult))
            step.after(v.tensor_tensor(over[k], over[k], rk[k], ALU.add))
            step.after(v.tensor_tensor(into[k], over[k], base[k], ALU.add))
            step.after(v.scalar_tensor_tensor(gate[k], rk[k], float(CAP), gate[k], ALU.is_lt, ALU.mult))
            step.after(v.scalar_tensor_tensor(outof[k], rk[k], CAP - 1.0, base[k], ALU.min, ALU.add))
        v.memset(picked, 0.0).then_inc(places_ready, 1)

        def experts_out(q, first):
            for j in range(2):
                dve.wait_ge(we_in[j], 64 * q + 64)
                if not first:
                    dve.wait_ge(ye_kept[j], 16 * q)
                for s in range(2):
                    dve.wait_ge(down3_done[j], 2 * q + s + 1)
                    v.tensor_tensor(two(ye[j], s), po[s][:, :].rearrange("p (t d) -> p t d", t=2),
                                    b2e[j].unsqueeze(1).broadcast_to([P, 2, D]), ALU.add).then_inc(ye_ready[j], 1)

        experts_out(0, True)
        with dve.Fori(1, NE // 2) as q:
            experts_out(q, False)
        dve.wait_ge(x_kept, PAIRS + 1)
        for i in range(NT):
            if i % TT == 0:
                dve.wait_ge(back_in[i // TT], 16 * 2 * TT)
            step.after(v.scalar_tensor_tensor(xst[:, i, :], back[:, 2 * i, :], gate[0][:, i:i + 1], xst[:, i, :], ALU.mult, ALU.add))
            v.scalar_tensor_tensor(xst[:, i, :], back[:, 2 * i + 1, :], gate[1][:, i:i + 1], xst[:, i, :], ALU.mult, ALU.add).then_inc(final_ready, 1)

    @block.tensor
    def _(pe):
        mm = nc.tensor.matmul

        def transposed(dst, src):
            return nc.tensor.transpose(dst, src, ident)

        pe.wait_ge(const_in, 16)
        def layer(n, attn, ffn):
            m = n - 1

            def scores(tile):
                for e in range(4):
                    for g in range(4):
                        if e == 0 and tile:
                            pe.wait_ge(scm_ready, 16 * n + 4 * tile + g - 3)
                        c = e // 2
                        keys = (kO if e % 2 else kE)[ts(g, 32), c, ts(tile, P)]
                        last = mm(pa[g][:, ts(e, P)], keys, qf[ts(g, 32), c, ts(tile, P)], start=True, stop=True)
                        if e == 3:
                            last.then_inc(sc_done, 1)

            def weigh(tile):
                if tile >= 2:
                    pe.wait_ge(num_out, 4 * n + tile - 1)
                elif ffn:
                    pe.wait_ge(down_out, 2 * m + tile + 1)
                s, bank = tile // 2, po[tile % 2]
                for b in range(H // HB):
                    c, half = b // 2, b % 2
                    if tile % 2:
                        mm(bank[:, ts(b, P)], kvm[:, s, c, ts(half, P)], qf[:, c, ts(tile, P)], start=True, stop=True)
                    for j in range(HB):
                        h = HB * b + j
                        g, e = 2 * half + j // 2, 2 * c + j % 2
                        if c == 0 and j % 2 == 0:
                            pe.wait_ge(scm_ready, 16 * n + 4 * tile + g + 1)
                        last = mm(bank[ts(j, VA), ts(b, P)], vaug[:, tile, h, :], scm[:, (4 * tile + g) % 8, e, :],
                                  start=tile % 2 == 0, stop=True, skip_group_check=True, tile_position=(0, VA * j))
                last.then_inc(av_done, 1)

            def weighed_transposed(tile):
                pe.wait_ge(num_out, 4 * n + tile + 1)
                if tile == 2:
                    pe.wait_ge(tr_out, 6 * n + 5)
                for b in range(H // HB):
                    last = transposed(pt[tile % 2][:, ts(b, P)], num[tile % 2][:, b, :])
                last.then_inc(numT_done, 1)

            def attention_transposed(s):
                pe.wait_ge(att_ready, 4 * n + 2 * s + 2)
                for k in range(KC):
                    for i in range(2):
                        last = transposed(pt[s][:, ts(2 * k + i, P)], att[:, 2 * s + i, ts(k, P)])
                last.then_inc(tr_done, 1)

            def project(s):
                pe.wait_ge(tr_out, 6 * n + 4 + s + 1)
                pe.wait_ge(scm_ready, 16 * n + 13 + s)
                for i in range(2):
                    for k in range(KC):
                        last = mm(pa[s][:, ts(i, D)], attT[:, k, ts(2 * s + i, P)], wo[:, k, :], start=k == 0, stop=k == KC - 1)
                last.then_inc(wo_done, 1)

            def up(half):
                for i in range(FM // 2 * half, FM // 2 * (half + 1)):
                    if half:
                        pe.wait_ge(gelu_ready, FM * m + i - 3)
                    elif attn:
                        pe.wait_ge((qf_ready, kf_ready)[i // KC], KC * n + i % KC + 1)
                    for k in range(KC):
                        last = mm(pa[i % 4][:, :], w1[:, k, ts(i, P)], yT[:, k, :], start=k == 0, stop=k == KC - 1)
                    last.then_inc(up_done, 1)

            def down(s):
                if attn:
                    pe.wait_ge(vaug_ready, 2 * n + s + 1)
                for i in range(2):
                    for c in range(FM):
                        if s == 0 and i == 0:
                            pe.wait_ge(gelu_ready, FM * m + c + 1)
                        last = mm(po[s][:, ts(i, D)], gT[:, c, ts(2 * s + i, P)], w2[:, c, :], start=c == 0, stop=c == FM - 1)
                last.then_inc(down_done, 1)

            if attn:
                la = attn[0]
                pe.wait_ge(hbuf_ready, n + 1)
                if ffn:
                    pe.wait_ge(tr_out, 6 * n)
                for k in range(KC):
                    for i in range(TT):
                        last = transposed(pt[k][:, ts(i, P)], hbuf[:, i, ts(k, P)])
                    last.then_inc(tr_done, 1)
                pe.wait_ge(qkv_w_in, 64 * la + 64)
                pe.wait_ge(tr_out, 6 * n + 2)
                if ffn:
                    pe.wait_ge(scm_ready, 16 * n)
                    pe.wait_ge(r1_ready, 2 * m + 2)
                for j in range(2 * KC):
                    for k in range(KC):
                        last = mm(pa[j][:, :], (wq if j < KC else wk)[:, k, ts(j % KC, P)], hT[:, k, :], start=k == 0, stop=k == KC - 1)
                    last.then_inc(qk_done, 1)
                if ffn:
                    pe.wait_ge(num_out, 4 * n)
                for s in range(2):
                    for i in range(2):
                        for k in range(KC):
                            last = mm(po[s][:, ts(i, D)], hT[:, k, ts(2 * s + i, P)], wv[:, k, :], start=k == 0, stop=k == KC - 1)
                    last.then_inc(v_done, 1)
            if ffn:
                lf = ffn[0]
                pe.wait_ge(tr_out, 6 * n + (2 if attn else 0))
                for s in range(2):
                    pe.wait_ge(y_ready, 2 * m + s + 1)
                    for k in range(KC):
                        for i in range(2):
                            last = transposed(pt[s][:, ts(2 * k + i, P)], y[:, 2 * s + i, ts(k, P)])
                    last.then_inc(ytr_done, 1)
                pe.wait_ge(w1_in, 32 * lf + 32)
                pe.wait_ge(ytr_out, 2 * m + 2)
                up(0)
            if attn:
                pe.wait_ge(kf_ready, KC * n + KC)
                for s in range(2):
                    for c in range(KC):
                        last = transposed(pt[s][:, ts(c, P)], kf[:, c, ts(2 * s, P)])
                    last.then_inc(tr_done, 1)
            if ffn:
                up(1)
            if attn:
                pe.wait_ge(vaug_ready, 2 * n + 2)
                pe.wait_ge(tr_out, 6 * n + 4)
                for i in range(2 * KC):
                    if ffn:
                        pe.wait_ge(gelu_ready, FM * m + i + 5)
                    mm(pa[i][:, 0:KC * P], ktok[:, i // KC, ts(i % KC, P)],
                       vaug[:, 2 * (i // KC), ts(i % KC, H // KC), :].rearrange("p h e -> p (h e)"), start=True, stop=True).then_inc(kv_done, 1)
                pe.wait_ge(keo_ready, 2 * n + 2)
                pe.wait_ge(kvm_ready, 4 * n + 4)
                scores(0)
            if ffn:
                pe.wait_ge(w2_in, 16 * lf + 16)
                down(0)
            if attn:
                scores(1)
            if ffn:
                down(1)
            if attn:
                pe.wait_ge(wo_in, 16 * la + 16)
                weigh(0)
                scores(2)
                weighed_transposed(0)
                weigh(1)
                scores(3)
                weighed_transposed(1)
                weigh(2)
                attention_transposed(0)
                weigh(3)
                weighed_transposed(2)
                project(0)
                weighed_transposed(3)
                attention_transposed(1)
                project(1)

        attention_and_ffn(pe, layer)
        pe.wait_ge(w_in_2, W2_IN)
        with pe.Fori(0, PAIRS) as p:
            def input_transposed(k, n):
                pe.wait_ge(xn_ready, XN * p + n)
                for s in range(2):
                    if k:
                        pe.wait_ge(tr2_out, TR2 * p + k + s - 1)
                    for c in range(KC):
                        for i in range(2):
                            last = transposed(pt[s][:, ts(2 * c + i, P)], xn[:, 2 * s + i, ts(c, P)])
                    last.then_inc(tr2_done, 1)
                pe.wait_ge(tr2_out, TR2 * p + k + 2)

            input_transposed(0, 1)
            for c in range(KC):
                last = mm(pa[0][:, :], w_sv[:, c, :], xnT[:, c, :], start=c == 0, stop=c == KC - 1)
            last.then_inc(vt_done, 1)
            pe.wait_ge(ctx_in, 32 * p + 32)
            mm(pa[1][:, :], w_st[:, 0, :], ctxT[:, 0, :], start=True, stop=False)
            mm(pa[1][:, :], w_st[0:CT - P, 1, :], ctxT[0:CT - P, 1, :], start=False, stop=True).then_inc(vt_done, 1)
            pe.wait_ge(vt_ready, 4 * p + 4)
            for i in range(TT):
                mm(pa[2][:, i:i + 1], vsq[:, ts(i, P)], ones[:, 0:1], start=True, stop=True)
            mm(pa[3][:, :], ones, tsq, start=True, stop=True).then_inc(nrm_done, 1)
            for s in range(2):
                for i in range(2):
                    last = mm(po[s][:, ts(i, S)], vT[:, ts(2 * s + i, P)], tT[:, s * S:(s + 1) * S], start=True, stop=True)
                last.then_inc(dots_done, 1)
            input_transposed(2, 2)
            for i in range(TT):
                for c in range(KC):
                    last = mm(pa[0][:, ts(i, E0)], xnT[:, c, ts(i, P)], w_gate[:, c, :], start=c == 0, stop=c == KC - 1)
            last.then_inc(gate_done, 1)
            for i in range(TT):
                for c in range(KC):
                    last = mm((po[0], pa[1], pa[2], pa[3])[i][:, :], xnT[:, c, ts(i, P)], w_pair[:, c, :], start=c == 0, stop=c == KC - 1)
                last.then_inc(pair_done, 1)
            input_transposed(4, 3)
            for m in range(2 * IC):
                if m >= 4:
                    pe.wait_ge(in_out, 8 * p + m - 3)
                for c in range(KC):
                    last = mm(pa[m % 4][:, :], w_in[:, c, ts(m, P)], xnT[:, c, :], start=c == 0, stop=c == KC - 1)
                last.then_inc(in_done, 1)
            pe.wait_ge(xs_ready, IC * p + IC)
            pe.wait_ge(in_out, 8 * p + 8)
            for c in range(IC):
                last = mm(pa[0][0:DTR, :], w_xp[:, c, 0:DTR], xs[:, c, :], start=c == 0, stop=c == IC - 1)
            last.then_inc(xp_done, 1)
            for c in range(IC):
                last = mm(pa[1][0:2 * NS, :], w_xp[:, c, DTR:DTR + 2 * NS], xs[:, c, :], start=c == 0, stop=c == IC - 1)
            last.then_inc(xp_done, 1)
            pe.wait_ge(xp_out, 2 * p + 2)
            for c in range(IC):
                mm(pa[c][:, :], w_dt[:, ts(c, P)], dtr, start=True, stop=True).then_inc(dtp_done, 1)

            def row_spread(g, n):
                k = 8 * g + 2 * n
                for which, bank in enumerate((pt, po)):
                    if k >= 4:
                        pe.wait_ge(bc_out, 32 * p + k + which - 3)
                    r = which * NS + g * NG + n
                    mm(bank[n % 2][:, :], ident[0:2 * NS, r:r + 1].broadcast_to([2 * NS, P]), bc,
                       start=True, stop=True).then_inc(bc_done, 1)

            for n in range(NG):
                row_spread(0, n)
            pe.wait_ge(soft_ready, p + 1)
            for i in range(4 * IC):
                g, c = i // IC, i % IC
                if g + 1 < NS // NG:
                    row_spread(g + 1, c)
                pe.wait_ge(hc_ready, 16 * p + i + 1)
                for n in range(NG):
                    last = mm(pa[c][:, :], ident, uh[i % 2][:, n, :], start=g == 0 and n == 0, stop=g == NS // NG - 1 and n == NG - 1)
                last.then_inc(ysum_done, 1)
            pe.wait_ge(yg_ready, IC * p + IC)
            for s in range(2):
                for i in range(2):
                    for c in range(IC):
                        last = mm(po[s][:, ts(i, D)], dtx[:, c, ts(2 * s + i, P)], w_out[:, c, :], start=c == 0, stop=c == IC - 1)
                last.then_inc(proj_done, 1)
            input_transposed(6, 4)
            for r in range(12):
                if r >= 4:
                    pe.wait_ge(qkv_out, 12 * p + r - 3)
                m, bank = r % 4, pa[r % 4][:, :]
                if r < 4:
                    for c in range(KC):
                        last = mm(bank, w_q[:, c, ts(m, P)], xnT[:, c, :], start=c == 0, stop=c == KC - 1)
                elif r < 8:
                    mm(bank, w_k[:, 0, ts(m, P)], ctxT[:, 0, :], start=True, stop=False)
                    last = mm(bank, w_k[0:CT - P, 1, ts(m, P)], ctxT[0:CT - P, 1, :], start=False, stop=True)
                else:
                    mm(bank, ctxT[:, 0, ts(m, P)], w_v[:, 0, :], start=True, stop=False)
                    last = mm(bank, ctxT[0:CT - P, 1, ts(m, P)], w_v[0:CT - P, 1, :], start=False, stop=True)
                last.then_inc(qkv_done, 1)
            pe.wait_ge(qkv_out, 12 * p + 12)

            def scores2(u):
                tile, j, e = u // 4, u % 4 // 2, u % 2
                if u >= 2:
                    pe.wait_ge(pexp_ready, 16 * p + u - 1)
                for b in range(2):
                    last = mm(pa[e][:, b * S:(b + 1) * S], qT[ts(e, QD), 2 * j + b, ts(tile, P)],
                              kT[ts(e, QD), 2 * j + b, (tile // 2) * S:(tile // 2 + 1) * S], start=True, stop=True)
                last.then_inc(s2_done, 1)

            def weights_transposed(u):
                pe.wait_ge(pexp_ready, 16 * p + u + 1)
                if u >= 2:
                    pe.wait_ge(pT_out, 16 * p + u - 1)
                for b in range(2):
                    for k in range(2):
                        last = transposed(pa[2 + u % 2][:, ts(2 * b + k, P)], pexp[u % 2][:, b, ts(k, P)])
                last.then_inc(pT_done, 1)

            def weigh2(u):
                tile, h0 = u // 4, 4 * (u % 4 // 2) + u % 2
                pe.wait_ge(pT_out, 16 * p + u + 1)
                if u % 4 == 0 and tile >= 2:
                    pe.wait_ge(wo2_out, 4 * p + tile - 1)
                for b in range(2):
                    for k in range(2):
                        last = mm(po[tile % 2][:, ts(h0 + 2 * b, QD)], pT[u % 2][:, 2 * b + k, :],
                                  vv[:, 2 * (tile // 2) + k, ts(h0 + 2 * b, QD)], start=k == 0, stop=k == 1)
                last.then_inc(av2_done, 1)

            def project2(tile):
                pe.wait_ge(at2_ready, 4 * p + tile + 1)
                pe.wait_ge(tr2_out, TR2 * p + 8 + tile - 1)
                for c in range(QC):
                    last = transposed(pt[tile % 2][:, ts(c, P)], at2[tile % 2][:, ts(c, P)])
                last.then_inc(tr2_done, 1)
                pe.wait_ge(tr2_out, TR2 * p + 8 + tile + 1)
                for c in range(QC):
                    last = mm(po[tile % 2][:, 0:D], at2T[tile % 2][:, c, :], w_o[:, c, :], start=c == 0, stop=c == QC - 1)
                last.then_inc(wo2_done, 1)

            for u in range(16 + 4):
                if u < 16:
                    scores2(u)
                if 1 <= u < 17:
                    weights_transposed(u - 1)
                if 2 <= u < 18:
                    weigh2(u - 2)
                if u >= 7 and (u - 7) % 4 == 0:
                    project2((u - 7) // 4)
            input_transposed(12, 5)
            for i in range(TT):
                for c in range(KC):
                    last = mm(pa[0][:, ts(i, NE)], xnT[:, c, ts(i, P)], w_r[:, c, :], start=c == 0, stop=c == KC - 1)
            last.then_inc(route_done, 1)
        pe.wait_ge(sel_ready, 1)
        flat_sel = sel.rearrange("p t e -> p (t e)")
        mm(pa[0][:, 0:NT * NE], strict, flat_sel, start=True, stop=True)
        mm(pa[1][:, 0:NT * NE], ones, flat_sel, start=True, stop=True).then_inc(rank_done, 1)
        def experts(q, first):
            for j in range(2):
                pe.wait_ge(xg_in[j], 16 * q + 16)
                for s in range(2):
                    if j:
                        pe.wait_ge(tr3_out, 4 * q + s + 1)
                    for c in range(KC):
                        for i in range(2):
                            last = transposed(pt[s][:, ts(2 * c + i, P)], xg[j][:, 2 * s + i, ts(c, P)])
                    last.then_inc(tr3_done, 1)
                pe.wait_ge(we_in[j], 64 * q + 64)
                pe.wait_ge(tr3_out, 4 * q + 2 * j + 2)
                for m in range(EF // P):
                    if m >= 4:
                        pe.wait_ge(gelu3_ready, 16 * q + 8 * j + m - 3)
                    for c in range(KC):
                        last = mm(pa[m % 4][:, :], w1e[j][:, c, ts(m, P)], xgT[:, c, :], start=c == 0, stop=c == KC - 1)
                    last.then_inc(up3_done, 1)
                if j or not first:
                    pe.wait_ge(ye_ready[1 - j], 2 * q + 2 * j)
                for s in range(2):
                    for i in range(2):
                        for m in range(EF // P):
                            if s == 0 and i == 0:
                                pe.wait_ge(gelu3_ready, 16 * q + 8 * j + m + 1)
                            last = mm(po[s][:, ts(i, D)], gTe[:, m, ts(2 * s + i, P)], w2e[j][:, m, :], start=m == 0, stop=m == EF // P - 1)
                    last.then_inc(down3_done[j], 1)

        experts(0, True)
        with pe.Fori(1, NE // 2) as q:
            experts(q, False)

    ctx.close()


def host_arrays(inputs):
    f = {k: np.asarray(a) for k, a in inputs.items()}
    c = np.ascontiguousarray
    rows = [f["L0_attn_" + n] for n in ("bv", "bo", "g1", "be1", "b2", "g2", "be2")]
    cols = lambda a: a.reshape(L, -1, P).transpose(0, 2, 1)
    arrays = {
        "consts": shape_constants(),
        "x": f["x"].reshape(N, D),
        "rows": np.stack(rows, 1),
        "qk_bias": np.concatenate([cols(f["L0_attn_bq"]), cols(f["L0_attn_bk"])], 2),
        "b1_cols": cols(f["L0_attn_b1"]),
    }
    arrays["b1e_cols"] = f["L1_ffn_b1"].reshape(NE, EF // P, P).transpose(0, 2, 1)
    for n in ("W1", "W2", "b2"):
        arrays["L1_ffn_" + n] = f["L1_ffn_" + n]
    for n in ("Wq", "Wk", "Wv", "Wo", "W1", "W2"):
        arrays["L0_attn_" + n] = f["L0_attn_" + n]
    chunks = lambda a: a.reshape(-1, P).T
    arrays |= {
        "ctxT": f["ctx_768"].reshape(N, CT).T,
        "sim_wv": f["L0_xattn_Wv"].T, "sim_wt": f["L0_xattn_Wt"].T,
        "gate": f["L0_ffn_gate_w"], "pair_w": np.concatenate([f["L0_ffn_w0"].T, f["L0_ffn_w1"].T], 1),
        "ssm_in": f["L1_attn_in_proj_w"].T, "ssm_xp": f["L1_attn_x_proj_w"].T, "ssm_dt": f["L1_attn_dt_proj_w"].T,
        "ssm_out": f["L1_attn_out_proj_w"].T,
        "a_log": f["L1_attn_A_log"].reshape(IC, P, NS).transpose(1, 0, 2),
        "cols": np.concatenate([
            chunks(f["L0_xattn_bv"]), chunks(f["L0_xattn_bt"]), chunks(f["L1_attn_in_proj_b"]),
            f["L1_attn_conv_w"].reshape(IC, P, KCONV).transpose(1, 0, 2).reshape(P, -1),
            chunks(f["L1_attn_conv_b"]), chunks(f["L1_attn_dt_proj_b"]), chunks(f["L1_attn_D"])], 1),
        "rows2": np.concatenate([f["L0_attn_gf"], f["L0_attn_bef"], f["L1_attn_out_proj_b"], f["L1_xattn_bo"],
                                 f["L0_ffn_b0"], f["L0_ffn_b1"], f["L1_ffn_br"]]),
    }
    for n in ("L1_xattn_Wq", "L1_xattn_Wk", "L1_xattn_Wv", "L1_xattn_Wo", "L1_ffn_Wr"):
        arrays[n] = f[n]
    return {k: c(a) for k, a in arrays.items()}


def kernel(**inputs):
    import concourse.bacc as bacc
    from concourse.bass_utils import run_bass_kernel_spmd as run
    arrays = host_arrays(inputs)
    nc = bacc.Bacc("TRN2", target_bir_lowering=False, num_devices=1)
    aps = {k: nc.dram_tensor("in_" + k, a.shape, F32, kind="ExternalInput").ap() for k, a in arrays.items()}
    out = nc.dram_tensor("out", (N, D), F32, kind="ExternalOutput").ap()
    decoder(nc, aps, out)
    r = run(nc, [{"in_" + k: a for k, a in arrays.items()}], core_ids=[0])
    return r.results[0]["out"].reshape(B, S, D)
```

```python
import numpy as np
import concourse.bass as bass
from concourse import mybir
from contextlib import ExitStack

F32 = mybir.dt.float32
BF16 = mybir.dt.bfloat16
I32 = mybir.dt.int32
ALU = mybir.AluOpType
ACT = mybir.ActivationFunctionType
AX = mybir.AxisListType.X

P = 128
B, S, D = 8, 256, 256
N = B * S
NT = N // P
KC = D // P
PAIRS = B // 2
TT = 4
W = TT * P
L, H, HD, FF = 4, 16, 16, 1024
FM = FF // P
VA = 32
HB = P // VA
LN_EPS, ATT_EPS = 1e-5, 1e-6

HX, CT, E0 = 128, 192, 8
DI, NS, DTR, KCONV = 512, 16, 64, 4
PARTS, BC = 3, 2 * NS
IC = DI // P
NG = 2
UNITS = NS // NG * IC
QH, QD = 8, 64
QI = QH * QD
QC = QI // P
NE, EF, CAP = 8, 1024, N * 2 // 8
SIM_EPS = 1e-8
NORM_MIN = 1e-30
DECAY_TOP = 1.0 - 2.0 ** -15
DECAY_MID = DECAY_TOP + 2.0 ** -16 - 2.0 ** -24
DECAY_GRID = 384.0
SCALE = QD ** -0.5

ATTN_STEPS, FFN_STEPS = 9, 12
END_STEPS = 5
SSM_STEPS, CROSS_STEPS = 91, 22
ACT_STEPS = UNITS
CROSS_SLOTS = 36


C_ID, C_TRI, C_STRICT, C_ONES, C_BD = 0, 128, 256, 384, 512
C_EVEN = C_BD + KC * P
C_ODD, C_MHALF, C_SLOT = C_EVEN + 1, C_EVEN + 2, C_EVEN + 6
C_ROW = C_SLOT + 8
C_MID = C_ROW + BC
C_ALL = C_MID + 1


def shape_constants():
    c = np.zeros((P, C_ALL), np.float32)
    i = np.arange(P)
    c[:, C_ID:C_ID + P] = np.eye(P)
    c[:, C_TRI:C_TRI + P] = i[None, :] >= i[:, None]
    c[:, C_STRICT:C_STRICT + P] = i[None, :] > i[:, None]
    c[:, C_ONES:C_ONES + P] = 1.0
    c[:, C_BD:C_BD + KC * P] = (i // HD)[:, None] == (np.arange(KC * P) // VA)[None, :]
    c[:, C_EVEN] = (i // HD) % 2 == 0
    c[:, C_MID] = DECAY_MID
    c[:, C_ODD] = (i // HD) % 2 == 1
    c[:, C_MHALF:C_MHALF + 4] = -0.5
    c[:, C_SLOT:C_SLOT + 8] = 512.0 * np.arange(8)
    c[:, C_ROW:C_ROW + BC] = (i % BC)[:, None] == np.arange(BC)[None, :]
    return c


class Steps:

    def __init__(self, eng, sem):
        self.eng, self.sem, self.base, self.n = eng, sem, 0, 0

    def loop(self, it, per):
        self.enter()
        self.per = per
        self.at(it * per)

    def enter(self):
        self.start = self.base + self.n

    def at(self, done):
        self.base, self.n = self.start + done, 0

    def end_loop(self, times):
        assert self.n == self.per, (self.n, self.per)
        self.base, self.n = self.start + times * self.per, 0

    def mark(self, ins):
        self.n += 1
        ins.then_inc(self.sem, 1)
        return self.base + self.n

    def passed(self, count):
        self.eng.wait_ge(self.sem, count)

    def after(self, ins):
        self.passed(self.mark(ins))

    def apart(self, ins):
        self.n += 1
        ins.then_inc(self.sem, 1)
        hold(self.eng, self.sem, self.base + self.n)


def hold(eng, sem, value):
    eng.wait_ge(sem, value)
    eng.sem_inc(HELD[0], 1)


HELD = [None]


def attention_and_ffn(eng, body):
    body(0, (0, 0), None)
    with eng.Fori(0, L - 1) as l:
        with eng.Fori(0, PAIRS - 1) as p:
            body(l * PAIRS + p + 1, (l, p + 1), (l, p))
        body(l * PAIRS + PAIRS, (l + 1, 0), (l, PAIRS - 1))
    with eng.Fori(0, PAIRS - 1) as p:
        body((L - 1) * PAIRS + p + 1, (L - 1, p + 1), (L - 1, p), p)
    body(L * PAIRS, None, (L - 1, PAIRS - 1), PAIRS - 1)


def ssm_and_cross(eng, body):
    body(0, None)
    with eng.Fori(0, PAIRS - 1) as q:
        body(q + 1, q)
    body(None, PAIRS - 1)


class Arena:

    def __init__(self, tile, at):
        self.tile, self.at, self.top = tile, at, at

    def __call__(self, *shape, rows=P):
        n = int(np.prod(shape))
        part = self.tile[0:rows, self.at:self.at + n]
        self.at += n
        if len(shape) == 2:
            part = part.rearrange("p (a b) -> p a b", a=shape[0])
        elif len(shape) == 3:
            part = part.rearrange("p (a b c) -> p a b c", a=shape[0], b=shape[1])
        return part


def decoder(nc, t, out):
    ctx = ExitStack()

    def sem(name):
        return ctx.enter_context(nc.semaphore(name))

    ts = bass.ts

    ARENA = 51 * 1024 + 576
    arena = ctx.enter_context(nc.sbuf_tensor("arena", [P, ARENA], F32))
    keep = Arena(arena, 0)
    xst = keep(NT, D)
    hst = keep(NT, D)
    const = keep(C_ALL)
    stats, mv, ve, rstd = keep(TT, 6), keep(TT, 2), keep(TT), keep(TT)
    lgall = keep(NT, 8)
    ident, tri = const[:, C_ID:C_ID + P], const[:, C_TRI:C_TRI + P]
    strict, ones = const[:, C_STRICT:C_STRICT + P], const[:, C_ONES:C_ONES + P]
    mhalf, slot0 = const[:, C_MHALF:C_MHALF + TT], const[:, C_SLOT:C_SLOT + 8]

    head_mask = const[:, C_BD:C_BD + KC * P]

    bc_parts = ctx.enter_context(nc.sbuf_tensor("bc_parts", [PARTS * BC, W], BF16))
    row_of_bc = ctx.enter_context(nc.sbuf_tensor("row_of_bc", [PARTS * BC, BC], BF16))
    PHASE = keep.at

    a = Arena(arena, PHASE)
    vecs = a(7, D)
    wq, wk, wv, wo = a(KC, D), a(KC, D), a(KC, D), a(KC, D)
    w1, w2 = a(KC, FF), a(FM, D)
    qkb, qkb1 = a(2 * KC), a(2 * KC)
    b1 = a(FM)
    hbuf, hT = a(TT, D), a(KC, W)
    expq = a(2 * KC, W)
    qf, kf, kE, kO = a(KC, W), a(KC, W), a(KC, W), a(KC, W)
    vaug, ktok = a(TT, H, VA), a(2, D)
    kvm = a(2, KC, KC * P)
    num = [a(H // HB, P) for _ in range(2)]
    scm = a(8, TT, P)
    den = a(TT, H)
    att, attT = a(TT, D), a(KC, W)
    xb, r1, y, yb = a(TT, D), a(TT, D), a(TT, D), a(TT, D)
    yT, gT = a(KC, W), a(FM, W)
    zero = gT[:, 0:4, :].rearrange("p m t -> p (m t)")
    layers_top = a.at

    EARLY = ARENA - (4 * HX + KC * E0 + KC * 2 * D + KC * 2 * DI + IC * (DTR + PARTS * BC) + DI + IC * D + KC * NE
                     + 2 + 2 * IC + IC * KCONV + 3 * IC + 6 * D + NE + IC * NS)
    a = Arena(arena, EARLY)
    w_sv, w_st = a(KC, HX), a(2, HX)
    w_gate, w_pair = a(KC, E0), a(KC, 2 * D)
    w_in, w_xp, w_dt, w_out = a(KC, 2 * DI), a(IC, DTR + PARTS * BC), a(DI, rows=DTR), a(IC, D)
    w_r = a(KC, NE)
    cols = a(2 + 2 * IC + IC * KCONV + 3 * IC)
    sim_b, in_b = cols[:, 0:2], cols[:, 2:2 + 2 * IC]
    cw = cols[:, 10:10 + IC * KCONV].rearrange("p (c k) -> p c k", c=IC)
    conv_b, dt_b, skip = cols[:, 26:30], cols[:, 30:34], cols[:, 34:38]
    rows2 = a(4 * D + 2 * D + NE)
    r_gf, r_bef, r_out, r_xo = (rows2[:, i * D:(i + 1) * D] for i in range(4))
    r_pair, r_r = rows2[:, 4 * D:6 * D], rows2[:, 6 * D:6 * D + NE]
    acol = a(IC, NS)
    assert a.at == ARENA and layers_top <= EARLY, (a.at, layers_top, EARLY)
    a = Arena(arena, PHASE)
    w_q, w_k, w_v, w_o = a(KC, QI), a(2, QI), a(2, QI), a(QC, D)
    xc, xn, xnT = a(TT, D), a(TT, D), a(KC, W)
    ctxT = a(2, W)
    STAGE = a.at
    vT, tT, vsq, tsq, tn, vn, dn = a(W), a(W), a(W), a(W), a(W), a(TT), a(TT, D)
    a = Arena(arena, STAGE)
    lg, gmax, gsum, cmp8, cnt2, coef = a(TT, E0), a(TT), a(TT), a(TT, E0), a(2, TT), a(2, TT)
    eb = a(TT, 2 * D)
    a = Arena(arena, STAGE)
    zs, xs, dt, dtx = a(IC, W), a(IC, W), a(IC, W), a(IC, W)
    dtr, bc = a(W, rows=DTR), a(W, rows=PARTS * BC)
    late = a.at
    Bs, Cs = zip(*((a(NG, W), a(NG, W)) for _ in range(2)))
    units_at = a.at
    dA, uh = [a(NG, W) for _ in range(2)], [a(NG, W) for _ in range(2)]

    uh.append(xn.rearrange("p t d -> p (t d)").rearrange("p (n t) -> p n t", n=NG))

    def chunks_at(at):
        return arena[:, at:at + IC * W].rearrange("p (c t) -> p c t", c=IC)

    xpad = arena[:, units_at:units_at + IC * 2 * (S + KCONV - 1)].rearrange("p (c s t) -> p c s t", c=IC, s=2)
    soft_e, soft_l, soft_d, soft_r = chunks_at(units_at), chunks_at(units_at + IC * W), dtx, chunks_at(late + 2 * NG * W)
    xr, xrT = uh[0].rearrange("p n (t d) -> p (n t) d", d=D), dA[0]
    qT, kT, vv = a(QC, W), a(QC, W), a(TT, QI)
    mx, nm, sm = a(4, 2), a(4, 2), a(TT, QH)
    pexp, pT = [a(2, S) for _ in range(2)], [a(4, P) for _ in range(2)]
    at2, at2T = a(QI), a(QC, P)
    assert a.at <= EARLY, (a.at, EARLY)

    a = Arena(arena, STAGE)
    cmp3, cnt, sel, top = a(NT, NE), a(NT, NE), a(NT, NE), [a(NT, NE) for _ in range(2)]
    picked, before, rank = a(NT, NE), a(NT, NE), a(NT, NE)
    lt, gate, rk, base, over, place = ([a(NT) for _ in range(2)] for _ in range(6))
    gexp = a(NT)
    into = [a(NT).bitcast(I32) for _ in range(2)]
    outof = [a(NT).bitcast(I32) for _ in range(2)]
    weights_at = a.at
    w1e, w2e = [a(KC, EF) for _ in range(2)], [a(EF // P, D) for _ in range(2)]
    b1e, b2e = [a(EF // P) for _ in range(2)], [a(D) for _ in range(2)]
    xg, xgT, gTe, ye = [a(TT, D) for _ in range(2)], a(KC, W), a(EF // P, W), [a(TT, D) for _ in range(2)]
    back = arena[:, weights_at:weights_at + 2 * NT * D].rearrange("p (i d) -> p i d", d=D)
    assert a.at <= ARENA, a.at
    rows_to = nc.dram_tensor("rows_to_experts", (NE * CAP, D), F32, kind="Internal").ap()
    rows_back = nc.dram_tensor("rows_from_experts", (NE * CAP, D), F32, kind="Internal").ap()

    pa = [ctx.enter_context(nc.psum_tensor(f"pa{i}", [P, 512], F32)) for i in range(4)]
    pt = [ctx.enter_context(nc.psum_tensor(f"pt{i}", [P, 512], F32)) for i in range(2)]
    po = [ctx.enter_context(nc.psum_tensor(f"po{i}", [P, 512], F32)) for i in range(2)]
    bank_row, bank_score, bank_tr, bank_av = pt[0], pt[1], po[0], po[1]
    gate_banks = (po[0], po[1], pa[1], po[0])

    const_in, x_in = sem("const_in"), [sem(f"x_in{p}") for p in range(PAIRS)]
    qkv_w_in, wo_in, w1_in, w2_in = sem("qkv_w_in"), sem("wo_in"), sem("w1_in"), sem("w2_in")
    bvo_in, ln1_in, ln2_in = sem("bvo_in"), sem("ln1_in"), sem("ln2_in")
    dve_step, pool_step, act_step = sem("dve_step"), sem("pool_step"), sem("act_step")
    var_ready, rstd_ready = sem("var_ready"), sem("rstd_ready")
    h_ready, hbuf_ready, xb_ready = sem("h_ready"), sem("hbuf_ready"), sem("xb_ready")
    tr_done, tr_out = sem("tr_done"), sem("tr_out")
    ytr_done, ytr_out = sem("ytr_done"), sem("ytr_out")
    qk_done, min_ready, exp_ready = sem("qk_done"), sem("min_ready"), sem("exp_ready")
    qf_ready, kf_ready, keo_ready = sem("qf_ready"), sem("kf_ready"), sem("keo_ready")
    v_done, vaug_ready = sem("v_done"), sem("vaug_ready")
    kv_done, kvm_ready = sem("kv_done"), sem("kvm_ready")
    sc_done, scm_ready, av_done, att_ready = sem("sc_done"), sem("scm_ready"), sem("av_done"), sem("att_ready")
    num_out, numT_done = sem("num_out"), sem("numT_done")
    wo_done, r1_ready, y_ready, yb_ready = sem("wo_done"), sem("r1_ready"), sem("y_ready"), sem("yb_ready")
    up_done, gelu_ready, down_done, down_out = sem("up_done"), sem("gelu_ready"), sem("down_done"), sem("down_out")
    zero_ready, zeroed = sem("zero_ready"), sem("zeroed")
    out_done = sem("out_done")
    w_cross_in = sem("w_cross_in")
    w_in_2, ctx_in, a_exp, a_ready = sem("w_in_2"), sem("ctx_in"), sem("a_exp"), sem("a_ready")
    xn_ready, xc_ready, x_kept, xf_kept = sem("xn_ready"), sem("xc_ready"), sem("x_kept"), sem("xf_kept")
    tr2_done, tr2_out = sem("tr2_done"), sem("tr2_out")
    vt_done, vt_ready, nrm_done, nrm_ready, dots_done = (sem(n) for n in ("vt_done", "vt_ready", "nrm_done", "nrm_ready", "dots_done"))
    gate_done, gl_ready, ge_ready, pair_done, eb_ready, sil_ready = (
        sem(n) for n in ("gate_done", "gl_ready", "ge_ready", "pair_done", "eb_ready", "sil_ready"))
    in_done, in_out, conv_ready, xs_ready, xp_done, xp_out = (
        sem(n) for n in ("in_done", "in_out", "conv_ready", "xs_ready", "xp_done", "xp_out"))
    dtp_done, soft_ready, dt_ready, bc_done, bc_out = (sem(n) for n in ("dtp_done", "soft_ready", "dt_ready", "bc_done", "bc_out"))
    da_ready, scan_done, hc_ready, ysum_done, yg_ready, proj_done = (
        sem(n) for n in ("da_ready", "scan_done", "hc_ready", "ysum_done", "yg_ready", "proj_done"))
    qkv_done, qkv_out, s2_done, nm_ready, pexp_ready = (sem(n) for n in ("qkv_done", "qkv_out", "s2_done", "nm_ready", "pexp_ready"))
    pT_done, pT_out, av2_done, at2_ready, wo2_done = (sem(n) for n in ("pT_done", "pT_out", "av2_done", "at2_ready", "wo2_done"))
    route_done, wo2_out = sem("route_done"), sem("wo2_out")
    lost_ready, corrected, start_ready = sem("lost_ready"), sem("corrected"), sem("start_ready")
    u_ready, dtx_ready, bc_split, sel_row_ready = sem("u_ready"), sem("dtx_ready"), sem("bc_split"), sem("sel_row_ready")
    at2T_done, at2T_out = sem("at2T_done"), sem("at2T_out")
    xr_ready, xrT_done, xrT_out = sem("xr_ready"), sem("xrT_done"), sem("xrT_out")
    soft_e_ready, soft_u_ready, abs_ready, relu_ready = sem("soft_e_ready"), sem("soft_u_ready"), sem("abs_ready"), sem("relu_ready")

    logits_ready, sel_ready, rank_done, lt_ready, gexp_ready, places_ready = (
        sem(n) for n in ("logits_ready", "sel_ready", "rank_done", "lt_ready", "gexp_ready", "places_ready"))
    scattered, tr3_done, tr3_out, up3_done, gelu3_ready = (sem(n) for n in ("scattered", "tr3_done", "tr3_out", "up3_done", "gelu3_ready"))
    we_in, xg_in, down3_done, ye_ready, ye_kept = ([sem(f"{n}{j}") for j in range(2)] for n in ("we_in", "xg_in", "down3_done", "ye_ready", "ye_kept"))
    back_in, final_ready = [sem(f"back_in{p}") for p in range(PAIRS)], sem("final_ready")
    HELD[0] = sem("held")
    V_BV, V_BO, V_G1, V_BE1, V_B2, V_G2, V_BE2 = range(7)
    LAYERS_DONE = 2 * PAIRS * (L + 1)
    W2_IN, CROSS_W_IN = 16 * 13, 16 * 6
    GROUPS = PAIRS + 4 * L * PAIRS + PAIRS
    TR2, XN = 8, 4

    def row(i, n):
        return vecs[:, i, :].unsqueeze(1).broadcast_to([P, n, D])

    def two(tile, s):
        return tile[:, 2 * s:2 * s + 2, :]

    block = ctx.enter_context(nc.Block())

    @block.sync
    def _(sp):
        sp.dma_start(const, t["consts"]).then_inc(const_in, 16)
        for p in range(PAIRS):
            sp.dma_start(xst[:, TT * p:TT * p + TT, :],
                         t["x"][p * W:(p + 1) * W, :].rearrange("(t p) d -> p t d", p=P)).then_inc(x_in[p], 16)
        def layer_weights(l, first):
            def after(sem, per_pair):
                if not first:
                    sp.wait_ge(sem, l * PAIRS * per_pair)

            after(v_done, 2)
            for tile, name in ((wq, "L0_attn_Wq"), (wk, "L0_attn_Wk"), (wv, "L0_attn_Wv")):
                sp.dma_start(tile, t[name][l].rearrange("(k p) n -> p k n", p=P)).then_inc(qkv_w_in, 16)
            after(kf_ready, KC)
            sp.dma_start(qkb, t["qk_bias"][l]).then_inc(qkv_w_in, 16)
            after(vaug_ready, 2)
            after(xb_ready, 1)
            sp.dma_start(vecs[:, V_BV:V_G1, :], t["rows"][l, V_BV:V_G1].partition_broadcast(P)).then_inc(bvo_in, 16)
            after(wo_done, 2)
            sp.dma_start(wo, t["L0_attn_Wo"][l].rearrange("(k p) n -> p k n", p=P)).then_inc(wo_in, 16)
            after(y_ready, 2)
            sp.dma_start(vecs[:, V_G1:V_B2, :], t["rows"][l, V_G1:V_B2].partition_broadcast(P)).then_inc(ln1_in, 16)
            after(gelu_ready, FM)
            sp.dma_start(w1, t["L0_attn_W1"][l].rearrange("(k p) n -> p k n", p=P)).then_inc(w1_in, 16)
            sp.dma_start(b1, t["b1_cols"][l]).then_inc(w1_in, 16)
            after(down_done, 2)
            sp.dma_start(w2, t["L0_attn_W2"][l].rearrange("(m p) n -> p m n", p=P)).then_inc(w2_in, 16)
            if not first:
                sp.wait_ge(h_ready, 2 * PAIRS + 2 * l * PAIRS)
            sp.dma_start(vecs[:, V_B2:, :], t["rows"][l, V_B2:].partition_broadcast(P)).then_inc(ln2_in, 16)

        layer_weights(0, True)
        sp.wait_ge(zero_ready, 1)
        for q in range(4):
            sp.dma_start(rows_to.rearrange("(q p r) d -> q p (r d)", q=4, p=P)[q], zero).then_inc(zeroed, 16)
        for dst, name in ((w_sv, "sim_wv"), (w_gate, "gate"), (w_pair, "pair_w"), (w_in, "ssm_in"), (w_xp, "ssm_xp"),
                          (w_out, "ssm_out"), (w_r, "L1_ffn_Wr")):
            sp.dma_start(dst, t[name].rearrange("(k p) n -> p k n", p=P)).then_inc(w_in_2, 16)
        sp.dma_start(w_st[:, 0, :], t["sim_wt"][0:P, :]).then_inc(w_in_2, 16)
        sp.dma_start(w_st[0:CT - P, 1, :], t["sim_wt"][P:CT, :]).then_inc(w_in_2, 16)
        for dst, name in ((w_dt, "ssm_dt"), (cols, "cols"), (acol, "a_log")):
            sp.dma_start(dst, t[name]).then_inc(w_in_2, 16)
        sp.dma_start(rows2, t["rows2"].partition_broadcast(P)).then_inc(w_in_2, 16)
        with sp.Fori(1, L) as l:
            layer_weights(l, False)
        sp.wait_ge(h_ready, LAYERS_DONE)
        for dst, name in ((w_q, "L1_xattn_Wq"), (w_o, "L1_xattn_Wo")):
            sp.dma_start(dst, t[name].rearrange("(k p) n -> p k n", p=P)).then_inc(w_cross_in, 16)
        for dst, name in ((w_k, "L1_xattn_Wk"), (w_v, "L1_xattn_Wv")):
            sp.dma_start(dst[:, 0, :], t[name][0:P, :]).then_inc(w_cross_in, 16)
            sp.dma_start(dst[0:CT - P, 1, :], t[name][P:CT, :]).then_inc(w_cross_in, 16)

        def context(p):
            sp.dma_start(ctxT[:, 0, :], t["ctxT"][0:P, ts(p, W)]).then_inc(ctx_in, 16)
            sp.dma_start(ctxT[0:CT - P, 1, :], t["ctxT"][P:CT, ts(p, W)]).then_inc(ctx_in, 16)

        context(0)
        with sp.Fori(1, PAIRS) as p:
            sp.wait_ge(qkv_done, 12 * p - 4)
            context(p)
        sp.wait_ge(logits_ready, PAIRS)
        for first in (True, False):
            if first:
                loads = ExitStack()
                q = 0
            else:
                loads = sp.Fori(1, NE // 2)
            with loads as at:
                q = 0 if first else at
                for j in range(2):
                    if not first:
                        sp.wait_ge(ye_ready[j], 2 * q)
                    e = 2 * q + j
                    sp.dma_start(w1e[j], t["L1_ffn_W1"][e].rearrange("(k p) n -> p k n", p=P)).then_inc(we_in[j], 16)
                    sp.dma_start(b1e[j], t["b1e_cols"][e]).then_inc(we_in[j], 16)
                    sp.dma_start(w2e[j], t["L1_ffn_W2"][e].rearrange("(m p) n -> p m n", p=P)).then_inc(we_in[j], 16)
                    sp.dma_start(b2e[j], t["L1_ffn_b2"][e].partition_broadcast(P)).then_inc(we_in[j], 16)
                    if first and j == 0:
                        sp.wait_ge(scattered, 16 * 2 * NT)
                    sp.dma_start(xg[j], rows_to[ts(e, CAP), :].rearrange("(t p) d -> p t d", p=P)).then_inc(xg_in[j], 16)
        for p in range(PAIRS):
            sp.wait_ge(final_ready, TT * p + TT)
            sp.dma_start(out[p * W:(p + 1) * W, :].rearrange("(t p) d -> p t d", p=P), xst[:, TT * p:TT * p + TT, :]).then_inc(out_done, 16)
        sp.wait_ge(out_done, 16 * PAIRS)
    @block.gpsimd
    def _(pool):
        step = Steps(pool, pool_step)

        def deviations(n, c, k):
            hold(pool, var_ready, n)
            step.apart(nc.gpsimd.tensor_scalar(ve[:, c:c + k], mv[:, c:c + k, 1], LN_EPS, None, ALU.add))
            nc.gpsimd.tensor_tensor(rstd[:, c:c + k], ve[:, c:c + k], mhalf[:, 0:k], ALU.pow).then_inc(rstd_ready, 1)

        nc.gpsimd.memset(zero, 0.0).then_inc(zero_ready, 1)
        hold(pool, const_in, 16)
        step.enter()
        deviations(1, 0, TT)
        pool.wait_ge(h_ready, 2)
        nc.gpsimd.tensor_copy(hbuf, hst[:, 0:TT, :]).then_inc(hbuf_ready, 1)
        with pool.Fori(1, PAIRS) as p:
            step.at(p)
            deviations(p + 1, 0, TT)
        step.at(PAIRS)
        step.enter()

        def layer(n, attn, ffn, end=None):
            m = n - 1
            if attn:
                la, p = attn
            if attn and ffn:
                hold(pool, h_ready, 2 * n + 2)
                hold(pool, tr_done, 6 * m + 2)
                nc.gpsimd.tensor_copy(hbuf, hst[:, ts(p, TT), :]).then_inc(hbuf_ready, 1)
            if ffn:
                groups = 4 * m if end is None else 4 * m + end
                step.at(groups)
                lf = ffn[0]
                for s in range(2):
                    deviations(PAIRS + groups + s + 1, 2 * s, 2)
            if attn:
                hold(pool, bvo_in, 16 * la + 16)
                if ffn:
                    hold(pool, r1_ready, 2 * m + 2)
                nc.gpsimd.tensor_tensor(xb, hst[:, ts(p, TT), :], row(V_BO, TT), ALU.add).then_inc(xb_ready, 1)
            if ffn:
                hold(pool, ln2_in, 16 * lf + 16)
                for s in range(2):
                    hold(pool, y_ready, 2 * m + s + 1)
                    nc.gpsimd.tensor_tensor(two(yb, s), two(y, s), row(V_B2, 2), ALU.add).then_inc(yb_ready, 1)
                for s in range(2):
                    deviations(PAIRS + groups + 2 + s + 1, 2 * s, 2)
                if end is not None:
                    deviations(PAIRS + groups + 5, 0, TT)

        attention_and_ffn(pool, layer)
        step.at(L * PAIRS * 4 + PAIRS)
        pool.sem_inc(x_kept, 1)
        pool.sem_inc(xf_kept, 1)
        step.enter()

        def mixer(p, q):
            groups = 0 if q is None else 5 * q + 4
            step.at(groups if q is None else groups + q + 1)
            if p is not None:
                for k in range(4):
                    if k == 3:
                        half = slice(IC // 2, IC)
                        hold(pool, lost_ready, p + 1)
                        step.apart(nc.gpsimd.tensor_tensor(soft_e[:, half], soft_e[:, half], soft_r[:, half], ALU.mult))
                        nc.gpsimd.tensor_tensor(dt[:, half], dt[:, half], soft_e[:, half], ALU.add).then_inc(corrected, 1)
                        for i in range(UNITS):
                            g, c = i // IC, i % IC
                            hold(pool, da_ready, UNITS * p + i + 1)
                            nc.gpsimd.memset(dA[i % 2].rearrange("p n (s t) -> p (n s) t", s=2)[:, :, 0], DECAY_TOP).then_inc(start_ready, 1)
                            if i >= len(uh):
                                hold(pool, ysum_done, UNITS * p + i - len(uh) + 1)
                            if i in (0, 1):
                                hold(pool, dtx_ready, 2 * p + 1 + i)
                            if c == 0:
                                hold(pool, bc_out, 32 * p + 2 * NG * (g + 1))
                            nc.gpsimd.tensor_tensor(uh[i % len(uh)], dtx[:, c, :].unsqueeze(1).broadcast_to([P, NG, W]), Bs[g % 2],
                                                    ALU.mult).then_inc(u_ready, 1)
                    deviations(GROUPS + groups + k + 1, 0, TT)
                hold(pool, xc_ready, p + 1)
                nc.gpsimd.tensor_copy(xst[:, ts(p, TT), :], xc).then_inc(x_kept, 1)
            if q is not None:
                deviations(GROUPS + groups + (5 if p is not None else 1), 0, TT)
                hold(pool, xr_ready, q + 1)
                nc.gpsimd.tensor_copy(hst[:, ts(q, TT), :], xr).then_inc(xf_kept, 1)

        ssm_and_cross(pool, mixer)
        pool.wait_ge(zeroed, 16 * 4)
        pool.wait_ge(places_ready, 1)
        pool.wait_ge(xf_kept, PAIRS + 1)
        for i in range(NT):
            for k in range(2):
                nc.gpsimd.indirect_dma_start(
                    out=rows_to, out_offset=bass.IndirectOffsetOnAxis(ap=into[k][:, i:i + 1], axis=0), in_=hst[:, i, :], in_offset=None,
                    bounds_check=NE * CAP - 1, oob_is_err=False).then_inc(scattered, 16)
        with pool.Fori(0, NE // 2) as q:
            for j in range(2):
                hold(pool, ye_ready[j], 2 * q + 2)
                nc.gpsimd.dma_start(rows_back[ts(2 * q + j, CAP), :].rearrange("(t p) d -> p t d", p=P), ye[j]).then_inc(ye_kept[j], 16)
        for j in range(2):
            pool.wait_ge(ye_kept[j], 16 * (NE // 2))
        for i in range(NT):
            for k in range(2):
                nc.gpsimd.indirect_dma_start(
                    out=back[:, 2 * i + k, :], out_offset=None, in_=rows_back,
                    in_offset=bass.IndirectOffsetOnAxis(ap=outof[k][:, i:i + 1], axis=0),
                    bounds_check=NE * CAP - 1, oob_is_err=False).then_inc(back_in[i // TT], 16)

    @block.scalar
    def _(act):
        def layer(n, attn, ffn, end=None):
            m = n - 1

            def evacuate(k, dst, src):
                act.wait_ge(tr_done, 6 * n + k + 1)
                nc.scalar.copy(dst, src).then_inc(tr_out, 1)

            if attn:
                for k in range(KC):
                    evacuate(k, hT[:, k, :], pt[k][:, :])
                for j in range(2 * KC):
                    act.wait_ge(min_ready, 4 * n + j + 1)
                    nc.scalar.activation(expq[:, j, :], expq[:, j, :], ACT.Exp).then_inc(exp_ready, 1)
            if ffn:
                for s in range(2):
                    act.wait_ge(ytr_done, 2 * m + s + 1)
                    nc.scalar.copy(yT[:, :, s * S:(s + 1) * S], pt[s][:, :].rearrange("p (k t) -> p k t", k=KC)).then_inc(ytr_out, 1)
                act.wait_ge(w1_in, 32 * ffn[0] + 32)
            for half in range(2):
                if ffn:
                    for i in range(FM // 2 * half, FM // 2 * (half + 1)):
                        act.wait_ge(up_done, FM * m + i + 1)
                        nc.scalar.activation(gT[:, i, :], pa[i % 4][:, :], ACT.Gelu, bias=b1[:, i:i + 1]).then_inc(gelu_ready, 1)
                if attn and half == 0:
                    for s in range(2):
                        evacuate(2 + s, ktok[:, s, :], pt[s][:, 0:D])
            def weighed(tile):
                act.wait_ge(av_done, 4 * n + tile + 1)
                nc.scalar.copy(num[tile % 2], po[tile % 2][:, :].rearrange("p (b q) -> p b q", b=H // HB)).then_inc(num_out, 1)

            def attention_evacuated(s):
                evacuate(4 + s, attT[:, :, s * S:(s + 1) * S], pt[s][:, :].rearrange("p (k t) -> p k t", k=KC))

            if not ffn:
                act.wait_ge(zeroed, 16 * 4)
            if attn:
                weighed(0)
                weighed(1)
                act.wait_ge(numT_done, 4 * n + 1)
                weighed(2)
                act.wait_ge(numT_done, 4 * n + 2)
                weighed(3)
                attention_evacuated(0)
                attention_evacuated(1)

        attention_and_ffn(act, layer)
        a_ = nc.scalar.activation
        step = Steps(act, act_step)
        act.wait_ge(w_in_2, W2_IN)
        a_(acol, acol, ACT.Exp).then_inc(a_exp, 1)
        step.enter()

        def mixer(p, q):

            def input_transposed(k):
                for s in range(2):
                    act.wait_ge(tr2_done, TR2 * p + k + s + 1)
                    nc.scalar.copy(xnT[:, :, s * S:(s + 1) * S], pt[s][:, :].rearrange("p (k t) -> p k t", k=KC)).then_inc(tr2_out, 1)

            def row_copied(g, k):
                act.wait_ge(bc_done, 32 * p + 2 * NG * g + k + 1)
                if k == 0 and g >= 2:
                    act.wait_ge(hc_ready, UNITS * p + IC * (g - 1))
                nc.scalar.copy((Bs, Cs)[k % 2][g % 2][:, k // 2, :], bank_row[:, :]).then_inc(bc_out, 1)

            def gated(c):
                act.wait_ge(in_done, 8 * p + IC + c + 1)
                a_(zs[:, c, :], gate_banks[c][:, :], ACT.Silu, bias=in_b[:, IC + c:IC + c + 1]).then_inc(in_out, 1)

            def decay(i):
                g, c = i // IC, i % IC
                if i < IC:
                    act.wait_ge(dt_ready, 2 * p + 1 + i // 2)
                if i == 1:
                    act.wait_ge(corrected, p + 1)
                if i >= 2:
                    act.wait_ge(scan_done, UNITS * p + i - 1)
                for n in range(NG):
                    last = a_(dA[i % 2][:, n, :], dt[:, c, :], ACT.Exp, scale=acol[:, c, NG * g + n:NG * g + n + 1])
                step.after(last)
                a_(dA[i % 2], dA[i % 2], ACT.Relu, scale=-1.0, bias=const[:, C_MID:C_MID + 1]).then_inc(da_ready, 1)

            def projected(first, end):
                for r in range(first, end):
                    act.wait_ge(qkv_done, 12 * p + r + 1)
                    bank = (pt[r % 2], pa[2 + r % 2], pa[r % 4])[r // 4]
                    nc.scalar.copy((kT, vv, qT)[r // 4][:, r % 4, :], bank[:, :]).then_inc(qkv_out, 1)

            def cross(i):
                if i % 2 == 0 and 1 <= i // 2 <= 16:
                    u = i // 2 - 1
                    tile, h0 = u // 4, 4 * (u % 4 // 2) + u % 2
                    act.wait_ge(nm_ready, 16 * q + u + 1)
                    if u >= 2:
                        act.wait_ge(pT_done, 16 * q + u - 1)
                    for b in range(2):
                        last = a_(pexp[u % 2][:, b, :], bank_score[:, b * S:(b + 1) * S], ACT.Exp, bias=nm[:, u % 4, b:b + 1], scale=SCALE,
                                  accum_out=sm[:, tile, h0 + 2 * b:h0 + 2 * b + 1])
                    last.then_inc(pexp_ready, 1)
                if i % 2 == 1 and 0 <= (i - 3) // 2 < 16:
                    u = (i - 3) // 2
                    act.wait_ge(pT_done, 16 * q + u + 1)
                    if u >= 2:
                        act.wait_ge(av2_done, 16 * q + u - 1)
                    nc.scalar.copy(pT[u % 2], bank_tr[:, :].rearrange("p (b i) -> p b i", b=4)).then_inc(pT_out, 1)
                if i % 8 == 3 and i >= 11:
                    act.wait_ge(at2T_done, 4 * q + (i - 11) // 8 + 1)
                    nc.scalar.copy(at2T, bank_tr[:, :].rearrange("p (k t) -> p k t", k=QC)).then_inc(at2T_out, 1)

            if p is not None:
                step.at(ACT_STEPS * p)
                for k, (i, full, square, norm, of) in enumerate(((1, tT, tsq, tn, pa[3][:, :]), (0, vT, vsq, vn, pa[2][:, 0:TT]))):
                    if k:
                        input_transposed(0)
                    act.wait_ge(vt_done, 2 * p + k + 1)
                    a_(full, pa[i][:, :], ACT.Identity, bias=sim_b[:, i:i + 1]).then_inc(vt_ready, 1)
                    a_(square, pa[i][:, :], ACT.Square, bias=sim_b[:, i:i + 1]).then_inc(vt_ready, 1)
                    act.wait_ge(nrm_done, 2 * p + k + 1)
                    a_(norm, of, ACT.Sqrt).then_inc(nrm_ready, 1)

                input_transposed(2)
                act.wait_ge(gl_ready, p + 1)
                a_(lg, lg, ACT.Exp).then_inc(ge_ready, 1)
                for i in range(TT):
                    act.wait_ge(eb_ready, TT * p + i + 1)
                    a_(eb[:, i, :], eb[:, i, :], ACT.Silu).then_inc(sil_ready, 1)

                input_transposed(4)
                if q is not None:
                    act.wait_ge(xf_kept, q + 1)
                for c in range(IC):
                    act.wait_ge(in_done, 8 * p + c + 1)
                    a_(xpad[:, c, :, 3:3 + S], pa[c][:, :].rearrange("p (s t) -> p s t", s=2), ACT.Identity,
                       bias=in_b[:, c:c + 1]).then_inc(in_out, 1)
                for c in range(IC):
                    act.wait_ge(conv_ready, IC * p + c + 1)
                    a_(xs[:, c, :], xs[:, c, :], ACT.Silu).then_inc(xs_ready, 1)
                    if c < IC - 1:
                        gated(c)
                act.wait_ge(xp_done, 2 * p + 1)
                nc.scalar.copy(dtr, pa[0][0:DTR, :]).then_inc(xp_out, 1)
                act.wait_ge(xp_done, 2 * p + 2)
                nc.scalar.copy(bc_parts[:, :], pt[1][0:PARTS * BC, :]).then_inc(xp_out, 1)
                gated(IC - 1)
                for c in range(IC):
                    act.wait_ge(dtp_done, IC * p + c + 1)
                    a_(soft_e[:, c, :], pa[c][:, :], ACT.Abs, bias=dt_b[:, c:c + 1]).then_inc(abs_ready, 1)
                act.wait_ge(abs_ready, IC * p + IC)
                halves = [slice(0, IC // 2), slice(IC // 2, IC)]
                for half in halves:
                    a_(soft_e[:, half], soft_e[:, half], ACT.Exp, scale=-1.0).then_inc(soft_e_ready, 1)
                for k, half in enumerate(halves):
                    act.wait_ge(soft_u_ready, 2 * p + k + 1)
                    a_(soft_l[:, half], soft_d[:, half], ACT.Ln).then_inc(soft_ready, 1)
                for k in range(2 * NG):
                    row_copied(0, k)
            for i in range(CROSS_SLOTS):
                if p is not None and i == UNITS + 2:
                    projected(0, 4)
                if p is not None and i < UNITS:
                    decay(i)
                j = i - 1
                if p is not None and 0 <= j < UNITS - IC:
                    row_copied(j // IC + 1, j % IC)
                if q is not None:
                    cross(i)
            if p is not None:
                projected(4, 8)
                input_transposed(6)
                projected(8, 12)
            if q is not None:
                for s in range(2):
                    act.wait_ge(xrT_done, 2 * q + s + 1)
                    nc.scalar.copy(xrT[:, :, s * S:(s + 1) * S], pt[s][:, :].rearrange("p (k t) -> p k t", k=KC)).then_inc(xrT_out, 1)

        ssm_and_cross(act, mixer)
        act.wait_ge(lt_ready, 1)
        a_(gexp, gexp, ACT.Exp).then_inc(gexp_ready, 1)
        with act.Fori(0, NE // 2) as q:
            for j in range(2):
                for s in range(2):
                    act.wait_ge(tr3_done, 4 * q + 2 * j + s + 1)
                    nc.scalar.copy(xgT[:, :, s * S:(s + 1) * S], pt[s][:, :].rearrange("p (k t) -> p k t", k=KC)).then_inc(tr3_out, 1)
                act.wait_ge(we_in[j], 64 * q + 64)
                for m in range(EF // P):
                    act.wait_ge(up3_done, 16 * q + 8 * j + m + 1)
                    a_(gTe[:, m, :], pa[m % 4][:, :], ACT.Gelu, bias=b1e[j][:, m:m + 1]).then_inc(gelu3_ready, 1)

    @block.vector
    def _(dve):
        step = Steps(dve, dve_step)
        v = nc.vector

        def normalise(n, c, src, dst):
            for i, one in enumerate(src):
                last = v.bn_stats(out=stats[:, c + i, :], in_=one)
            step.apart(last)
            for i in range(len(src)):
                last = v.bn_aggr(out=mv[:, c + i, :], in_=stats[:, c + i, :])
            last.then_inc(var_ready, 1)
            dve.wait_ge(rstd_ready, n)
            for i, one in enumerate(src):
                last = v.tensor_scalar(dst[i], one, mv[:, c + i, 0:1], rstd[:, c + i:c + i + 1], ALU.subtract, ALU.mult)
            return last

        step.after(v.memset(vaug, 0.0))
        step.after(v.memset(vaug[:, :, :, HD], 1.0))
        dve.wait_ge(const_in, 16)
        step.enter()

        def first_rows(p):
            step.at(p)
            at = [bass.ds(p * TT + i, 1) for i in range(TT)]
            normalise(p + 1, 0, [xst[:, j, :].rearrange("p a d -> p (a d)") for j in at],
                      [hst[:, j, :].rearrange("p a d -> p (a d)") for j in at]).then_inc(h_ready, 2)

        dve.wait_ge(x_in[0], 16)
        first_rows(0)
        for p in range(1, PAIRS):
            dve.wait_ge(x_in[p], 16)
        with dve.Fori(1, PAIRS) as p:
            first_rows(p)
        step.at(PAIRS)
        step.enter()

        def layer(n, attn, ffn, end=None):
            m = n - 1
            ended = 0 if end is None else end
            step.at(n * ATTN_STEPS + m * FFN_STEPS + ended * END_STEPS if ffn else 0)

            def statistics(s, rows):
                for i in (2 * s, 2 * s + 1):
                    last = v.bn_stats(out=stats[:, i, :], in_=rows[:, i, :])
                step.apart(last)
                for i in (2 * s, 2 * s + 1):
                    last = v.bn_aggr(out=mv[:, i, :], in_=stats[:, i, :])
                last.then_inc(var_ready, 1)

            def scaled(group, s, rows, dst, gamma):
                dve.wait_ge(rstd_ready, PAIRS + 4 * m + ended + group + 1)
                for i in (2 * s, 2 * s + 1):
                    last = v.tensor_scalar(dst[:, i, :], rows[:, i, :], mv[:, i, 0:1], rstd[:, i:i + 1], ALU.subtract, ALU.mult)
                step.after(last)
                step.after(v.tensor_tensor(two(dst, s), two(dst, s), row(gamma, 2), ALU.mult))

            if ffn:
                lf, pf = ffn
                dve.wait_ge(xb_ready, m + 1)
                dve.wait_ge(h_ready, 2 * PAIRS + 2 * m)
                for s in range(2):
                    dve.wait_ge(wo_done, 2 * m + s + 1)
                    v.tensor_tensor(two(r1, s), pa[s][:, :].rearrange("p (t d) -> p t d", t=2), two(xb, s), ALU.add)\
                        .then_inc(r1_ready, 1)
                for s in range(2):
                    dve.wait_ge(r1_ready, 2 * m + s + 1)
                    statistics(s, r1)
                dve.wait_ge(ln1_in, 16 * lf + 16)
                for s in range(2):
                    scaled(s, s, r1, y, V_G1)
                    v.tensor_tensor(two(y, s), two(y, s), row(V_BE1, 2), ALU.add).then_inc(y_ready, 1)
            if attn:
                la = attn[0]
                dve.wait_ge(qkv_w_in, 64 * la + 64)
                step.after(v.tensor_scalar(qkb1, qkb, 1.0, None, ALU.add))
                for j in range(2 * KC):
                    dve.wait_ge(qk_done, 4 * n + j + 1)
                    v.tensor_scalar(expq[:, j, :], pa[j][:, :], qkb[:, j:j + 1], 0.0, ALU.add, ALU.min).then_inc(min_ready, 1)
                for j in range(2 * KC):
                    dve.wait_ge(exp_ready, 4 * n + j + 1)
                    dst = (qf if j < KC else kf)[:, j % KC, :]
                    v.scalar_tensor_tensor(dst, pa[j][:, :], qkb1[:, j:j + 1], expq[:, j, :], ALU.add, ALU.max)\
                        .then_inc(qf_ready if j < KC else kf_ready, 1)
                dve.wait_ge(kf_ready, KC * n + KC)
                v.tensor_scalar(kE, kf, const[:, C_EVEN:C_EVEN + 1], None, ALU.mult).then_inc(keo_ready, 1)
                v.tensor_scalar(kO, kf, const[:, C_ODD:C_ODD + 1], None, ALU.mult).then_inc(keo_ready, 1)
                dve.wait_ge(bvo_in, 16 * la + 16)
                for s in range(2):
                    dve.wait_ge(v_done, 2 * n + s + 1)
                    for i in range(2):
                        last = v.tensor_tensor(vaug[:, 2 * s + i, :, 0:HD],
                                               po[s][:, ts(i, D)].rearrange("p (h e) -> p h e", h=H),
                                               vecs[:, V_BV, :].rearrange("p (h e) -> p h e", h=H), ALU.add)
                    last.then_inc(vaug_ready, 1)
                for i in range(2 * KC):
                    dve.wait_ge(kv_done, 4 * n + i + 1)
                    v.tensor_tensor(kvm[:, i // KC, i % KC, :], pa[i][:, 0:KC * P], head_mask, ALU.mult)\
                        .then_inc(kvm_ready, 1)

            def mask_scores(tile):
                if tile >= 2:
                    dve.wait_ge(av_done, 4 * n + tile - 1)
                for g in range(4):
                    i = 4 * tile + g
                    dve.wait_ge(sc_done, 16 * n + i + 1)
                    v.tensor_tensor(scm[:, i % 8, :, :], pa[g][:, :].rearrange("p (h q) -> p h q", h=4),
                                    tri.unsqueeze(1).broadcast_to([P, 4, P]), ALU.mult).then_inc(scm_ready, 1)

            def divide(tile):
                dve.wait_ge(numT_done, 4 * n + tile + 1)
                num = pt[tile % 2][:, :].rearrange("p (h e) -> p h e", h=H)
                step.after(v.tensor_scalar(den[:, tile, :], num[:, :, HD], ATT_EPS, None, ALU.add))
                step.after(v.reciprocal(den[:, tile, :], den[:, tile, :]))
                v.tensor_tensor(att[:, tile, :].rearrange("p (h e) -> p h e", h=H), num[:, :, 0:HD],
                                den[:, tile, :].unsqueeze(2).broadcast_to([P, H, HD]), ALU.mult).then_inc(att_ready, 1)

            def ffn_residual(s):
                dve.wait_ge(down_done, 2 * m + s + 1)
                dve.wait_ge(yb_ready, 2 * m + s + 1)
                v.tensor_tensor(two(r1, s), po[s][:, :].rearrange("p (t d) -> p t d", t=2), two(yb, s), ALU.add).then_inc(down_out, 1)
                dve.wait_ge(down_out, 2 * m + s + 1)
                statistics(s, r1)

            def ffn_normalised(s):
                scaled(2 + s, s, r1, r1, V_G2)
                v.tensor_tensor(hst[:, bass.ds(pf * TT + 2 * s, 2), :], two(r1, s), row(V_BE2, 2), ALU.add).then_inc(h_ready, 1)

            if attn:
                mask_scores(0)
            if ffn:
                ffn_residual(0)
            if attn:
                mask_scores(1)
            if ffn:
                ffn_residual(1)
            if attn:
                mask_scores(2)
                divide(0)
            if ffn:
                ffn_normalised(0)
            if attn:
                mask_scores(3)
                divide(1)
            if ffn:
                ffn_normalised(1)
            if attn:
                divide(2)
                divide(3)
            if end is not None:
                dve.wait_ge(w_in_2, W2_IN)
                hold(dve, h_ready, 2 * PAIRS + 2 * m + 2)
                rows_of = [hst[:, bass.ds(end * TT + i, 1), :].rearrange("p a d -> p (a d)") for i in range(TT)]
                pair = hst[:, ts(end, TT), :]
                step.after(normalise(PAIRS + 4 * m + ended + 5, 0, rows_of, rows_of))
                for gain, op in ((r_gf, ALU.mult), (r_bef, ALU.add)):
                    step.after(v.tensor_tensor(pair, pair, gain.unsqueeze(1).broadcast_to([P, TT, D]), op))
                step.after(v.tensor_tensor(xst[:, ts(end, TT), :], xst[:, ts(end, TT), :], pair, ALU.add))
            assert step.n == (ATTN_STEPS if attn else 0) + (FFN_STEPS if ffn else 0) + (END_STEPS if end is not None else 0)

        attention_and_ffn(dve, layer)
        step.at(L * PAIRS * (ATTN_STEPS + FFN_STEPS) + PAIRS * END_STEPS)
        dve.wait_ge(w_in_2, W2_IN)
        dve.wait_ge(a_exp, 1)
        dve.wait_ge(h_ready, LAYERS_DONE)
        v.tensor_copy(row_of_bc[:, :], const[0:PARTS * BC, C_ROW:C_ROW + BC]).then_inc(sel_row_ready, 1)
        v.tensor_scalar(acol, acol, -1.0, None, ALU.mult).then_inc(a_ready, 1)
        dve.wait_ge(a_ready, 1)
        step.enter()

        def mixer(p, q):
            step.at((SSM_STEPS * p if p is not None else SSM_STEPS * PAIRS) + (CROSS_STEPS * q if q is not None else 0))
            xct, xnt = [xc[:, i, :] for i in range(TT)], [xn[:, i, :] for i in range(TT)]

            def wide(r, n):
                return r.unsqueeze(1).broadcast_to([P, n, r.shape[1]])

            groups = GROUPS + (0 if q is None else 5 * q + 4)

            def normalised(k):
                normalise(groups + k, 0, xct, xnt).then_inc(xn_ready, 1)

            def cross(i):
                if i % 2 == 0 and i // 2 < 16:
                    u = i // 2
                    dve.wait_ge(s2_done, 16 * q + u + 1)
                    step.after(v.tensor_reduce(mx[:, u % 4, :], bank_score[:, :].rearrange("p (b j) -> p b j", b=2), AX, ALU.max))
                    v.tensor_scalar(nm[:, u % 4, :], mx[:, u % 4, :], -SCALE, None, ALU.mult).then_inc(nm_ready, 1)
                if i % 8 == 0 and i >= 8:
                    tile = i // 8 - 1
                    dve.wait_ge(av2_done, 16 * q + 4 * tile + 4)
                    step.after(v.reciprocal(sm[:, tile, :], sm[:, tile, :]))
                    v.tensor_tensor(at2.rearrange("p (h d) -> p h d", h=QH), bank_av[:, :].rearrange("p (h d) -> p h d", h=QH),
                                    sm[:, tile, :].unsqueeze(2).broadcast_to([P, QH, QD]), ALU.mult).then_inc(at2_ready, 1)
                if i % 8 == 3 and i >= 11:
                    tile = (i - 11) // 8
                    row_of = xst[:, bass.ds(q * TT + tile, 1), :].rearrange("p a d -> p (a d)")
                    dve.wait_ge(wo2_done, 4 * q + tile + 1)
                    if tile == 0:
                        dve.wait_ge(x_kept, q + 2)
                    v.tensor_tensor(row_of, bank_score[:, 0:D], row_of, ALU.add).then_inc(wo2_out, 1)

            def unit(i):
                g, c = i // IC, i % IC
                decay, h = dA[i % 2], uh[i % len(uh)]
                flat = "p n t -> p (n t)"
                dve.wait_ge(start_ready, UNITS * p + i + 1)
                floored = step.mark(v.tensor_scalar(decay, decay, DECAY_GRID, DECAY_GRID + DECAY_TOP, ALU.add, ALU.subtract))
                if q is not None and i:
                    cross(i - 1)
                step.passed(floored)
                dve.wait_ge(u_ready, UNITS * p + i + 1)
                v.tensor_tensor_scan(h.rearrange(flat), decay.rearrange(flat), h.rearrange(flat), 0.0, ALU.mult, ALU.add).then_inc(scan_done, 1)
                dve.wait_ge(scan_done, UNITS * p + i + 1)
                if c == 0:
                    dve.wait_ge(bc_out, 32 * p + 2 * NG * (g + 1))
                v.tensor_tensor(h, h, Cs[g % 2], ALU.mult).then_inc(hc_ready, 1)

            if p is not None:
                if q is not None:
                    hold(dve, tr2_done, TR2 * p)
                rows_of = [xst[:, bass.ds(p * TT + i, 1), :].rearrange("p a d -> p (a d)") for i in range(TT)]
                normalise(groups + 1, 0, rows_of, xnt).then_inc(xn_ready, 1)
                for k, norm in enumerate((tn, vn)):
                    dve.wait_ge(nrm_ready, 2 * p + k + 1)
                    step.after(v.tensor_scalar(norm, norm, NORM_MIN, None, ALU.max))
                    step.after(v.reciprocal(norm, norm))
                for i in range(TT):
                    last = v.tensor_scalar(dn[:, i, :], tn[:, (i // 2) * S:(i // 2 + 1) * S], vn[:, i:i + 1], 1.0 / SIM_EPS, ALU.mult, ALU.min)
                step.after(last)
                for s in range(2):
                    dve.wait_ge(dots_done, 2 * p + s + 1)
                    last = v.tensor_tensor(two(dn, s), po[s][:, :].rearrange("p (t d) -> p t d", t=2), two(dn, s), ALU.mult)
                step.after(last)
                hold(dve, x_kept, p + 1)
                step.after(v.tensor_tensor(xc, xst[:, ts(p, TT), :], dn, ALU.add))

                normalised(2)
                dve.wait_ge(gate_done, p + 1)
                gates = pa[0][:, 0:TT * E0].rearrange("p (t e) -> p t e", t=TT)
                step.after(v.tensor_reduce(gmax, gates, AX, ALU.max))
                v.tensor_tensor(lg, gates, gmax.unsqueeze(2).broadcast_to([P, TT, E0]), ALU.subtract).then_inc(gl_ready, 1)
                dve.wait_ge(ge_ready, p + 1)
                step.after(v.tensor_reduce(gsum, lg, AX, ALU.add))
                step.after(v.reciprocal(gsum, gsum))
                step.after(v.tensor_tensor(lg, lg, gsum.unsqueeze(2).broadcast_to([P, TT, E0]), ALU.mult))
                for e in range(2):
                    step.after(v.tensor_tensor(cmp8, lg, lg[:, :, e:e + 1].broadcast_to([P, TT, E0]), ALU.is_gt))
                    if e:
                        step.after(v.tensor_tensor(cmp8[:, :, 0:e], lg[:, :, 0:e], lg[:, :, e:e + 1].broadcast_to([P, TT, e]), ALU.is_ge))
                    step.after(v.tensor_reduce(cnt2[:, e, :], cmp8, AX, ALU.add))
                    step.after(v.scalar_tensor_tensor(coef[:, e, :], cnt2[:, e, :], float(e), lg[:, :, e], ALU.is_equal, ALU.mult))
                for i in range(TT + 1):
                    if i < TT:
                        dve.wait_ge(pair_done, TT * p + i + 1)
                        v.tensor_tensor(eb[:, i, :], (po[0], pa[1], pa[2], pa[3])[i][:, :], r_pair, ALU.add).then_inc(eb_ready, 1)
                    if i:
                        dve.wait_ge(sil_ready, TT * p + i)
                        for e in range(2):
                            step.after(v.scalar_tensor_tensor(xct[i - 1], eb[:, i - 1, e * D:(e + 1) * D], coef[:, e, i - 1:i],
                                                              xct[i - 1], ALU.mult, ALU.add))

                normalised(3)
                if q is not None:
                    dve.wait_ge(xf_kept, q + 1)
                step.after(v.memset(xpad[:, :, :, 0:3], 0.0))
                for c in range(IC):
                    dve.wait_ge(in_out, 8 * p + c + 1)
                    dst = xs[:, c, :].rearrange("p (s t) -> p s t", s=2)
                    for tap in range(KCONV):
                        at = KCONV - 1 - tap
                        src, w_tap = xpad[:, c, :, at:at + S], cw[:, c, at:at + 1]
                        if tap == 0:
                            last = v.tensor_scalar(dst, src, w_tap, conv_b[:, c:c + 1], ALU.mult, ALU.add)
                        else:
                            last = v.scalar_tensor_tensor(dst, src, w_tap, dst, ALU.mult, ALU.add)
                        if tap < KCONV - 1:
                            step.after(last)
                    last.then_inc(conv_ready, 1)
                dve.wait_ge(xp_out, 2 * p + 2)
                step.after(v.tensor_tensor(bc, pt[1][0:PARTS * BC, :], bc_parts[:, :], ALU.subtract))
                for k in range(1, PARTS):
                    last = v.tensor_copy(bc_parts[ts(k, BC), :], bc[ts(k, BC), :])
                step.after(last)
                step.after(v.tensor_tensor(bc[ts(2, BC), :], bc[ts(2, BC), :], bc_parts[ts(2, BC), :], ALU.subtract))
                step.after(v.tensor_copy(bc_parts[ts(2, BC), :], bc[ts(2, BC), :]))
                odd = bc_parts[:, :].rearrange("r (t two) -> r t two", two=2)[:, :, 1]
                v.tensor_scalar(odd, odd, -1.0, None, ALU.mult).then_inc(bc_split, 1)
                for c in range(IC):
                    dve.wait_ge(abs_ready, IC * p + c + 1)
                    v.tensor_scalar(dt[:, c, :], pa[c][:, :], dt_b[:, c:c + 1], 0.0, ALU.add, ALU.max).then_inc(relu_ready, 1)
                halves = [slice(0, IC // 2), slice(IC // 2, IC)]
                for k, half in enumerate(halves):
                    dve.wait_ge(soft_e_ready, 2 * p + k + 1)
                    v.tensor_scalar(soft_d[:, half], soft_e[:, half], 1.0, None, ALU.add).then_inc(soft_u_ready, 1)
                dve.wait_ge(relu_ready, IC * p + IC)
                step.after(v.tensor_scalar(soft_r, soft_e, 0.5, -1.0, ALU.mult, ALU.add))
                for k, half in enumerate(halves):
                    dve.wait_ge(soft_u_ready, 2 * p + k + 1)
                    ins = v.scalar_tensor_tensor(soft_e[:, half], soft_d[:, half], 1.0, soft_e[:, half], ALU.subtract, ALU.subtract)
                    if k:
                        ins.then_inc(lost_ready, 1)
                    else:
                        lost = step.mark(ins)
                half = halves[0]
                step.passed(lost)
                step.after(v.tensor_tensor(soft_e[:, half], soft_e[:, half], soft_r[:, half], ALU.mult))
                step.after(v.tensor_tensor(dt[:, half], dt[:, half], soft_e[:, half], ALU.add))
                for k, half in enumerate(halves):
                    dve.wait_ge(soft_ready, 2 * p + k + 1)
                    step.after(v.scalar_tensor_tensor(soft_l[:, half], soft_d[:, half], 1.0, soft_l[:, half], ALU.is_gt, ALU.mult))
                    if k:
                        dve.wait_ge(corrected, p + 1)
                    v.tensor_tensor(dt[:, half], dt[:, half], soft_l[:, half], ALU.add).then_inc(dt_ready, 1)
                    dve.wait_ge(dt_ready, 2 * p + k + 1)
                    v.tensor_tensor(dtx[:, half], dt[:, half], xs[:, half], ALU.mult).then_inc(dtx_ready, 1)
            for i in range(UNITS):
                if p is not None:
                    unit(i)
                elif i:
                    cross(i - 1)
            if q is not None:
                cross(UNITS - 1)
            if p is not None:
                for c in range(IC):
                    dve.wait_ge(ysum_done, UNITS * p + UNITS - IC + c + 1)
                    step.after(v.scalar_tensor_tensor(dtx[:, c, :], xs[:, c, :], skip[:, c:c + 1], pa[c][:, :], ALU.mult, ALU.add))
                    v.tensor_tensor(dtx[:, c, :], dtx[:, c, :], zs[:, c, :], ALU.mult).then_inc(yg_ready, 1)
            if q is not None:
                cross(UNITS)
            if p is not None:
                for s in range(2):
                    dve.wait_ge(proj_done, 2 * p + s + 1)
                    step.after(v.tensor_tensor(two(xc, s), pa[s][:, :].rearrange("p (t d) -> p t d", t=2), two(xc, s), ALU.add))
                v.tensor_tensor(xc, xc, wide(r_out, TT), ALU.add).then_inc(xc_ready, 1)
                dve.wait_ge(xc_ready, p + 1)
                normalised(4)
            if q is not None:
                cross(UNITS + 3)
                dve.wait_ge(wo2_out, 4 * q + 4)
                rows_of = [xst[:, bass.ds(q * TT + i, 1), :].rearrange("p a d -> p (a d)") for i in range(TT)]
                step.apart(v.tensor_tensor(xst[:, ts(q, TT), :], xst[:, ts(q, TT), :], wide(r_xo, TT), ALU.add))
                normalise(groups + (5 if p is not None else 1), 0, rows_of, [xr[:, i, :] for i in range(TT)]).then_inc(xr_ready, 1)
                dve.wait_ge(route_done, q + 1)
                v.tensor_tensor(lgall[:, ts(q, TT), :], po[0][:, 0:TT * NE].rearrange("p (t e) -> p t e", t=TT), wide(r_r, TT), ALU.add)\
                    .then_inc(logits_ready, 1)
            assert step.n == (SSM_STEPS if p is not None else 0) + (CROSS_STEPS if q is not None else 0), step.n

        ssm_and_cross(dve, mixer)
        step.at(PAIRS * (SSM_STEPS + CROSS_STEPS))

        def each(row):
            return row.unsqueeze(2).broadcast_to([P, NT, NE])

        dve.wait_ge(logits_ready, PAIRS)
        for e in range(NE):
            if e:
                v.tensor_tensor(cmp3[:, :, 0:e], lgall[:, :, 0:e], lgall[:, :, e:e + 1].broadcast_to([P, NT, e]), ALU.is_ge)
            step.after(v.tensor_tensor(cmp3[:, :, e:NE], lgall[:, :, e:NE], lgall[:, :, e:e + 1].broadcast_to([P, NT, NE - e]), ALU.is_gt))
            step.after(v.tensor_reduce(cnt[:, :, e], cmp3, AX, ALU.add))
        v.tensor_scalar(sel, cnt, 2.0, None, ALU.is_lt).then_inc(sel_ready, 1)
        for k in range(2):
            last = v.tensor_scalar(top[k], cnt, float(k), None, ALU.is_equal)
        step.after(last)
        for k in range(2):
            step.after(v.tensor_tensor(picked, top[k], lgall, ALU.mult))
            step.after(v.tensor_reduce(lt[k], picked, AX, ALU.add))
        v.tensor_tensor(gexp, lt[1], lt[0], ALU.subtract).then_inc(lt_ready, 1)
        dve.wait_ge(rank_done, 1)
        total = pa[1][:, 0:NT * NE].rearrange("p (t e) -> p t e", t=NT)
        step.after(v.memset(before[:, 0, :], 0.0))
        for i in range(1, NT):
            step.after(v.tensor_tensor(before[:, i, :], total[:, i - 1, :], before[:, i - 1, :], ALU.add))
        step.after(v.tensor_tensor(rank, pa[0][:, 0:NT * NE].rearrange("p (t e) -> p t e", t=NT), before, ALU.add))
        dve.wait_ge(gexp_ready, 1)
        step.after(v.tensor_scalar(gate[0], gexp, 1.0, None, ALU.add))
        step.after(v.reciprocal(gate[0], gate[0]))
        step.after(v.tensor_tensor(gate[1], gate[0], gexp, ALU.mult))
        for k in range(2):
            step.after(v.tensor_tensor(picked, top[k], rank, ALU.mult))
            step.after(v.tensor_reduce(rk[k], picked, AX, ALU.add))
            step.after(v.tensor_tensor(picked, top[k], slot0.unsqueeze(1).broadcast_to([P, NT, NE]), ALU.mult))
            step.after(v.tensor_reduce(base[k], picked, AX, ALU.add))
            step.after(v.tensor_scalar(over[k], rk[k], float(CAP), float(NE * CAP), ALU.is_ge, ALU.mult))
            step.after(v.tensor_tensor(over[k], over[k], rk[k], ALU.add))
            step.after(v.tensor_tensor(into[k], over[k], base[k], ALU.add))
            step.after(v.scalar_tensor_tensor(gate[k], rk[k], float(CAP), gate[k], ALU.is_lt, ALU.mult))
            step.after(v.scalar_tensor_tensor(outof[k], rk[k], CAP - 1.0, base[k], ALU.min, ALU.add))
        v.memset(picked, 0.0).then_inc(places_ready, 1)

        def experts_out(q, first):
            for j in range(2):
                dve.wait_ge(we_in[j], 64 * q + 64)
                if not first:
                    dve.wait_ge(ye_kept[j], 16 * q)
                for s in range(2):
                    dve.wait_ge(down3_done[j], 2 * q + s + 1)
                    v.tensor_tensor(two(ye[j], s), po[s][:, :].rearrange("p (t d) -> p t d", t=2),
                                    b2e[j].unsqueeze(1).broadcast_to([P, 2, D]), ALU.add).then_inc(ye_ready[j], 1)

        experts_out(0, True)
        with dve.Fori(1, NE // 2) as q:
            experts_out(q, False)
        dve.wait_ge(x_kept, PAIRS + 1)
        for i in range(NT):
            if i % TT == 0:
                dve.wait_ge(back_in[i // TT], 16 * 2 * TT)
            step.after(v.scalar_tensor_tensor(xst[:, i, :], back[:, 2 * i, :], gate[0][:, i:i + 1], xst[:, i, :], ALU.mult, ALU.add))
            v.scalar_tensor_tensor(xst[:, i, :], back[:, 2 * i + 1, :], gate[1][:, i:i + 1], xst[:, i, :], ALU.mult, ALU.add).then_inc(final_ready, 1)

    @block.tensor
    def _(pe):
        mm = nc.tensor.matmul

        def transposed(dst, src):
            return nc.tensor.transpose(dst, src, ident)

        pe.wait_ge(const_in, 16)
        def layer(n, attn, ffn, end=None):
            m = n - 1

            def scores(tile):
                for e in range(4):
                    for g in range(4):
                        if e == 0 and tile:
                            pe.wait_ge(scm_ready, 16 * n + 4 * tile + g - 3)
                        c = e // 2
                        keys = (kO if e % 2 else kE)[ts(g, 32), c, ts(tile, P)]
                        last = mm(pa[g][:, ts(e, P)], keys, qf[ts(g, 32), c, ts(tile, P)], start=True, stop=True)
                        if e == 3:
                            last.then_inc(sc_done, 1)

            def weigh(tile):
                if tile >= 2:
                    pe.wait_ge(num_out, 4 * n + tile - 1)
                elif ffn:
                    pe.wait_ge(down_out, 2 * m + tile + 1)
                s, bank = tile // 2, po[tile % 2]
                for b in range(H // HB):
                    c, half = b // 2, b % 2
                    if tile % 2:
                        mm(bank[:, ts(b, P)], kvm[:, s, c, ts(half, P)], qf[:, c, ts(tile, P)], start=True, stop=True)
                    for j in range(HB):
                        h = HB * b + j
                        g, e = 2 * half + j // 2, 2 * c + j % 2
                        if c == 0 and j % 2 == 0:
                            pe.wait_ge(scm_ready, 16 * n + 4 * tile + g + 1)
                        last = mm(bank[ts(j, VA), ts(b, P)], vaug[:, tile, h, :], scm[:, (4 * tile + g) % 8, e, :],
                                  start=tile % 2 == 0, stop=True, skip_group_check=True, tile_position=(0, VA * j))
                last.then_inc(av_done, 1)

            def weighed_transposed(tile):
                pe.wait_ge(num_out, 4 * n + tile + 1)
                if tile == 2:
                    pe.wait_ge(tr_out, 6 * n + 5)
                for b in range(H // HB):
                    last = transposed(pt[tile % 2][:, ts(b, P)], num[tile % 2][:, b, :])
                last.then_inc(numT_done, 1)

            def attention_transposed(s):
                pe.wait_ge(att_ready, 4 * n + 2 * s + 2)
                for k in range(KC):
                    for i in range(2):
                        last = transposed(pt[s][:, ts(2 * k + i, P)], att[:, 2 * s + i, ts(k, P)])
                last.then_inc(tr_done, 1)

            def project(s):
                pe.wait_ge(tr_out, 6 * n + 4 + s + 1)
                pe.wait_ge(scm_ready, 16 * n + 13 + s)
                for i in range(2):
                    for k in range(KC):
                        last = mm(pa[s][:, ts(i, D)], attT[:, k, ts(2 * s + i, P)], wo[:, k, :], start=k == 0, stop=k == KC - 1)
                last.then_inc(wo_done, 1)

            def up(half):
                for i in range(FM // 2 * half, FM // 2 * (half + 1)):
                    if half:
                        pe.wait_ge(gelu_ready, FM * m + i - 3)
                    elif attn:
                        pe.wait_ge((qf_ready, kf_ready)[i // KC], KC * n + i % KC + 1)
                    for k in range(KC):
                        last = mm(pa[i % 4][:, :], w1[:, k, ts(i, P)], yT[:, k, :], start=k == 0, stop=k == KC - 1)
                    last.then_inc(up_done, 1)

            def down(s):
                if attn:
                    pe.wait_ge(vaug_ready, 2 * n + s + 1)
                for i in range(2):
                    for c in range(FM):
                        if s == 0 and i == 0:
                            pe.wait_ge(gelu_ready, FM * m + c + 1)
                        last = mm(po[s][:, ts(i, D)], gT[:, c, ts(2 * s + i, P)], w2[:, c, :], start=c == 0, stop=c == FM - 1)
                last.then_inc(down_done, 1)

            if attn:
                la = attn[0]
                pe.wait_ge(hbuf_ready, n + 1)
                if ffn:
                    pe.wait_ge(tr_out, 6 * n)
                for k in range(KC):
                    for i in range(TT):
                        last = transposed(pt[k][:, ts(i, P)], hbuf[:, i, ts(k, P)])
                    last.then_inc(tr_done, 1)
                pe.wait_ge(qkv_w_in, 64 * la + 64)
                pe.wait_ge(tr_out, 6 * n + 2)
                if ffn:
                    pe.wait_ge(scm_ready, 16 * n)
                    pe.wait_ge(r1_ready, 2 * m + 2)
                for j in range(2 * KC):
                    for k in range(KC):
                        last = mm(pa[j][:, :], (wq if j < KC else wk)[:, k, ts(j % KC, P)], hT[:, k, :], start=k == 0, stop=k == KC - 1)
                    last.then_inc(qk_done, 1)
                if ffn:
                    pe.wait_ge(num_out, 4 * n)
                for s in range(2):
                    for i in range(2):
                        for k in range(KC):
                            last = mm(po[s][:, ts(i, D)], hT[:, k, ts(2 * s + i, P)], wv[:, k, :], start=k == 0, stop=k == KC - 1)
                    last.then_inc(v_done, 1)
            if ffn:
                lf = ffn[0]
                pe.wait_ge(tr_out, 6 * n + (2 if attn else 0))
                for s in range(2):
                    pe.wait_ge(y_ready, 2 * m + s + 1)
                    for k in range(KC):
                        for i in range(2):
                            last = transposed(pt[s][:, ts(2 * k + i, P)], y[:, 2 * s + i, ts(k, P)])
                    last.then_inc(ytr_done, 1)
                pe.wait_ge(w1_in, 32 * lf + 32)
                pe.wait_ge(ytr_out, 2 * m + 2)
                up(0)
            if attn:
                pe.wait_ge(kf_ready, KC * n + KC)
                for s in range(2):
                    for c in range(KC):
                        last = transposed(pt[s][:, ts(c, P)], kf[:, c, ts(2 * s, P)])
                    last.then_inc(tr_done, 1)
            if ffn:
                up(1)
            if attn:
                pe.wait_ge(vaug_ready, 2 * n + 2)
                pe.wait_ge(tr_out, 6 * n + 4)
                for i in range(2 * KC):
                    if ffn:
                        pe.wait_ge(gelu_ready, FM * m + i + 5)
                    mm(pa[i][:, 0:KC * P], ktok[:, i // KC, ts(i % KC, P)],
                       vaug[:, 2 * (i // KC), ts(i % KC, H // KC), :].rearrange("p h e -> p (h e)"), start=True, stop=True).then_inc(kv_done, 1)
                pe.wait_ge(keo_ready, 2 * n + 2)
                pe.wait_ge(kvm_ready, 4 * n + 4)
                scores(0)
            if ffn:
                pe.wait_ge(w2_in, 16 * lf + 16)
                down(0)
            if attn:
                scores(1)
                weigh(0)
            if ffn:
                down(1)
            if attn:
                pe.wait_ge(wo_in, 16 * la + 16)
                scores(2)
                weighed_transposed(0)
                weigh(1)
                scores(3)
                weighed_transposed(1)
                weigh(2)
                weigh(3)
                attention_transposed(0)
                weighed_transposed(2)
                project(0)
                weighed_transposed(3)
                attention_transposed(1)
                project(1)

        attention_and_ffn(pe, layer)
        pe.wait_ge(w_in_2, W2_IN)
        def mixer(p, q):
            def input_transposed(k, n):
                pe.wait_ge(xn_ready, XN * p + n)
                for s in range(2):
                    if k:
                        pe.wait_ge(tr2_out, TR2 * p + k + s - 1)
                    for c in range(KC):
                        for i in range(2):
                            last = transposed(pt[s][:, ts(2 * c + i, P)], xn[:, 2 * s + i, ts(c, P)])
                    last.then_inc(tr2_done, 1)
                pe.wait_ge(tr2_out, TR2 * p + k + 2)

            def row_spread(g, k):
                if g or k:
                    pe.wait_ge(bc_out, 32 * p + 2 * NG * g + k)
                r = k % 2 * NS + g * NG + k // 2
                mm(bank_row[:, :], row_of_bc[:, r:r + 1].broadcast_to([PARTS * BC, P]), bc_parts[:, :], start=True, stop=True).then_inc(bc_done, 1)

            def state_sum(i):
                g, c = i // IC, i % IC
                pe.wait_ge(hc_ready, UNITS * p + i + 1)
                for n in range(NG):
                    last = mm(pa[c][:, :], ident, uh[i % len(uh)][:, n, :], start=g == 0 and n == 0, stop=g == NS // NG - 1 and n == NG - 1)
                last.then_inc(ysum_done, 1)

            def scores2(u):
                tile, j, e = u // 4, u % 4 // 2, u % 2
                if u:
                    pe.wait_ge(pexp_ready, 16 * q + u)
                if u >= 6 and u % 4 == 2:
                    pe.wait_ge(wo2_out, 4 * q + u // 4)
                for b in range(2):
                    last = mm(bank_score[:, b * S:(b + 1) * S], qT[ts(e, QD), 2 * j + b, ts(tile, P)],
                              kT[ts(e, QD), 2 * j + b, (tile // 2) * S:(tile // 2 + 1) * S], start=True, stop=True)
                last.then_inc(s2_done, 1)

            def weights_transposed(u):
                pe.wait_ge(pexp_ready, 16 * q + u + 1)
                if u:
                    pe.wait_ge(pT_out, 16 * q + u)
                if u >= 5 and u % 4 == 1:
                    pe.wait_ge(at2T_out, 4 * q + u // 4)
                for b in range(2):
                    for k in range(2):
                        last = transposed(bank_tr[:, ts(2 * b + k, P)], pexp[u % 2][:, b, ts(k, P)])
                last.then_inc(pT_done, 1)

            def weigh2(u):
                tile, h0 = u // 4, 4 * (u % 4 // 2) + u % 2
                pe.wait_ge(pT_out, 16 * q + u + 1)
                if u % 4 == 0 and tile:
                    pe.wait_ge(at2_ready, 4 * q + tile)
                for b in range(2):
                    for k in range(2):
                        last = mm(bank_av[:, ts(h0 + 2 * b, QD)], pT[u % 2][:, 2 * b + k, :],
                                  vv[:, 2 * (tile // 2) + k, ts(h0 + 2 * b, QD)], start=k == 0, stop=k == 1)
                last.then_inc(av2_done, 1)

            def projections(first, end):
                for r in range(first, end):
                    m = r % 4
                    bank = (pt[r % 2], pa[2 + r % 2], pa[m])[r // 4][:, :]
                    if r in (2, 3, 6, 7):
                        pe.wait_ge(qkv_out, 12 * p + r - 1)
                    if r >= 10:
                        pe.wait_ge(qkv_out, 12 * p + 8)
                    if r < 4:
                        mm(bank, w_k[:, 0, ts(m, P)], ctxT[:, 0, :], start=True, stop=False)
                        last = mm(bank, w_k[0:CT - P, 1, ts(m, P)], ctxT[0:CT - P, 1, :], start=False, stop=True)
                    elif r < 8:
                        mm(bank, ctxT[:, 0, ts(m, P)], w_v[:, 0, :], start=True, stop=False)
                        last = mm(bank, ctxT[0:CT - P, 1, ts(m, P)], w_v[0:CT - P, 1, :], start=False, stop=True)
                    else:
                        for c in range(KC):
                            last = mm(bank, w_q[:, c, ts(m, P)], xnT[:, c, :], start=c == 0, stop=c == KC - 1)
                    last.then_inc(qkv_done, 1)

            def cross_scores(i):
                if i % 2 == 0 and i // 2 < 16:
                    scores2(i // 2)

            def cross(i):
                if i % 2 == 1 and i // 2 < 16:
                    weights_transposed(i // 2)
                if i % 2 == 0 and 1 <= i // 2 <= 16:
                    weigh2(i // 2 - 1)
                if i % 8 == 2 and i >= 10:
                    tile = i // 8 - 1
                    pe.wait_ge(at2_ready, 4 * q + tile + 1)
                    pe.wait_ge(pT_out, 16 * q + min(4 * tile + 5, 16))
                    for c in range(QC):
                        last = transposed(bank_tr[:, ts(c, P)], at2[:, ts(c, P)])
                    last.then_inc(at2T_done, 1)
                if i % 8 == 3 and i >= 11:
                    tile = i // 8 - 1
                    pe.wait_ge(at2T_out, 4 * q + tile + 1)
                    pe.wait_ge(pexp_ready, 16 * q + min(4 * tile + 6, 16))
                    for c in range(QC):
                        last = mm(bank_score[:, 0:D], at2T[:, c, :], w_o[:, c, :], start=c == 0, stop=c == QC - 1)
                    last.then_inc(wo2_done, 1)

            if p is not None:
                if q is not None:
                    pe.wait_ge(qkv_out, 12 * p)
                pe.wait_ge(ctx_in, 32 * p + 32)
                mm(pa[1][:, :], w_st[:, 0, :], ctxT[:, 0, :], start=True, stop=False)
                mm(pa[1][:, :], w_st[0:CT - P, 1, :], ctxT[0:CT - P, 1, :], start=False, stop=True).then_inc(vt_done, 1)
                pe.wait_ge(vt_ready, 4 * p + 2)
                mm(pa[3][:, :], ones, tsq, start=True, stop=True).then_inc(nrm_done, 1)
                input_transposed(0, 1)
                for c in range(KC):
                    last = mm(pa[0][:, :], w_sv[:, c, :], xnT[:, c, :], start=c == 0, stop=c == KC - 1)
                last.then_inc(vt_done, 1)
                pe.wait_ge(vt_ready, 4 * p + 4)
                for i in range(TT):
                    last = mm(pa[2][:, i:i + 1], vsq[:, ts(i, P)], ones[:, 0:1], start=True, stop=True)
                last.then_inc(nrm_done, 1)
                for s in range(2):
                    for i in range(2):
                        last = mm(po[s][:, ts(i, S)], vT[:, ts(2 * s + i, P)], tT[:, s * S:(s + 1) * S], start=True, stop=True)
                    last.then_inc(dots_done, 1)
                input_transposed(2, 2)
                for i in range(TT):
                    for c in range(KC):
                        last = mm(pa[0][:, ts(i, E0)], xnT[:, c, ts(i, P)], w_gate[:, c, :], start=c == 0, stop=c == KC - 1)
                last.then_inc(gate_done, 1)
                for i in range(TT):
                    for c in range(KC):
                        last = mm((po[0], pa[1], pa[2], pa[3])[i][:, :], xnT[:, c, ts(i, P)], w_pair[:, c, :], start=c == 0, stop=c == KC - 1)
                    last.then_inc(pair_done, 1)
                input_transposed(4, 3)
                for m in range(2 * IC):
                    bank = gate_banks[m - IC] if m >= IC else pa[m]
                    if m >= IC:
                        used = (0, 0, 2, 5)[m - IC]
                        if used:
                            pe.wait_ge(in_out, 8 * p + used)
                    for c in range(KC):
                        last = mm(bank[:, :], w_in[:, c, ts(m, P)], xnT[:, c, :], start=c == 0, stop=c == KC - 1)
                    last.then_inc(in_done, 1)
                    for c in ((0,), (1,), (2, 3), ())[m - IC] if m >= IC else ():
                        if c == 0:
                            pe.wait_ge(in_out, 8 * p + 1)
                        pe.wait_ge(xs_ready, IC * p + c + 1)
                        to_dt = mm(pa[0][0:DTR, :], w_xp[:, c, 0:DTR], xs[:, c, :], start=c == 0, stop=c == IC - 1)
                        if c == IC - 1:
                            to_dt.then_inc(xp_done, 1)
                        to_bc = mm(pt[1][0:PARTS * BC, :], w_xp[:, c, DTR:], xs[:, c, :], start=c == 0, stop=c == IC - 1)
                        if c == IC - 1:
                            to_bc.then_inc(xp_done, 1)
                pe.wait_ge(xp_out, 2 * p + 1)
                pe.wait_ge(in_out, 8 * p + 7)
                for c in range(IC):
                    mm(pa[c][:, :], w_dt[:, ts(c, P)], dtr, start=True, stop=True).then_inc(dtp_done, 1)

                pe.wait_ge(bc_split, p + 1)
                pe.wait_ge(sel_row_ready, 1)
                for k in range(2 * NG):
                    row_spread(0, k)
                pe.wait_ge(soft_e_ready, 2 * p + 2)
                pe.wait_ge(relu_ready, IC * p + IC)
            if p is not None:
                row_spread(1, 0)
            for i in range(UNITS + 1):
                j = i + 1
                if p is not None and j < UNITS - IC:
                    row_spread(j // IC + 1, j % IC)
                if q is not None:
                    cross_scores(i)
                if p is not None and i:
                    state_sum(i - 1)
                if q is not None:
                    cross(i)
            if p is not None:
                pe.wait_ge(w_cross_in, CROSS_W_IN)
                projections(0, 2)
                pe.wait_ge(yg_ready, IC * p + IC)
                for s in range(2):
                    for i in range(2):
                        for c in range(IC):
                            last = mm(pa[s][:, ts(i, D)], dtx[:, c, ts(2 * s + i, P)], w_out[:, c, :], start=c == 0, stop=c == IC - 1)
                    last.then_inc(proj_done, 1)
                projections(2, 4)
            if q is not None:
                for i in range(UNITS + 1, CROSS_SLOTS):
                    cross(i)
            if q is not None:
                pe.wait_ge(wo2_out, 4 * q + 4)
            if p is not None:
                projections(4, 8)
                pe.wait_ge(qkv_out, 12 * p + 4)
                input_transposed(6, 4)
                projections(8, 12)
            if q is not None:
                pe.wait_ge(xr_ready, q + 1)
                if p is not None:
                    pe.wait_ge(qkv_out, 12 * p + 12)
                for s in range(2):
                    for c in range(KC):
                        for i in range(2):
                            last = transposed(pt[s][:, ts(2 * c + i, P)], xr[:, 2 * s + i, ts(c, P)])
                    last.then_inc(xrT_done, 1)
                pe.wait_ge(xrT_out, 2 * q + 2)
                for i in range(TT):
                    for c in range(KC):
                        last = mm(po[0][:, ts(i, NE)], xrT[:, c, ts(i, P)], w_r[:, c, :], start=c == 0, stop=c == KC - 1)
                last.then_inc(route_done, 1)
            if p is not None:
                pe.wait_ge(qkv_out, 12 * p + 12)

        ssm_and_cross(pe, mixer)
        pe.wait_ge(sel_ready, 1)
        flat_sel = sel.rearrange("p t e -> p (t e)")
        mm(pa[0][:, 0:NT * NE], strict, flat_sel, start=True, stop=True)
        mm(pa[1][:, 0:NT * NE], ones, flat_sel, start=True, stop=True).then_inc(rank_done, 1)
        def experts(q, first):
            for j in range(2):
                pe.wait_ge(xg_in[j], 16 * q + 16)
                for s in range(2):
                    if j:
                        pe.wait_ge(tr3_out, 4 * q + s + 1)
                    for c in range(KC):
                        for i in range(2):
                            last = transposed(pt[s][:, ts(2 * c + i, P)], xg[j][:, 2 * s + i, ts(c, P)])
                    last.then_inc(tr3_done, 1)
                pe.wait_ge(we_in[j], 64 * q + 64)
                pe.wait_ge(tr3_out, 4 * q + 2 * j + 2)
                for m in range(EF // P):
                    if m >= 4:
                        pe.wait_ge(gelu3_ready, 16 * q + 8 * j + m - 3)
                    for c in range(KC):
                        last = mm(pa[m % 4][:, :], w1e[j][:, c, ts(m, P)], xgT[:, c, :], start=c == 0, stop=c == KC - 1)
                    last.then_inc(up3_done, 1)
                if j or not first:
                    pe.wait_ge(ye_ready[1 - j], 2 * q + 2 * j)
                for s in range(2):
                    for i in range(2):
                        for m in range(EF // P):
                            if s == 0 and i == 0:
                                pe.wait_ge(gelu3_ready, 16 * q + 8 * j + m + 1)
                            last = mm(po[s][:, ts(i, D)], gTe[:, m, ts(2 * s + i, P)], w2e[j][:, m, :], start=m == 0, stop=m == EF // P - 1)
                    last.then_inc(down3_done[j], 1)

        experts(0, True)
        with pe.Fori(1, NE // 2) as q:
            experts(q, False)

    ctx.close()


def host_arrays(inputs):
    f = {k: np.asarray(a) for k, a in inputs.items()}
    c = np.ascontiguousarray
    rows = [f["L0_attn_" + n] for n in ("bv", "bo", "g1", "be1", "b2", "g2", "be2")]
    cols = lambda a: a.reshape(L, -1, P).transpose(0, 2, 1)
    arrays = {
        "consts": shape_constants(),
        "x": f["x"].reshape(N, D),
        "rows": np.stack(rows, 1),
        "qk_bias": np.concatenate([cols(f["L0_attn_bq"]), cols(f["L0_attn_bk"])], 2),
        "b1_cols": cols(f["L0_attn_b1"]),
    }
    arrays["b1e_cols"] = f["L1_ffn_b1"].reshape(NE, EF // P, P).transpose(0, 2, 1)
    for n in ("W1", "W2", "b2"):
        arrays["L1_ffn_" + n] = f["L1_ffn_" + n]
    for n in ("Wq", "Wk", "Wv", "Wo", "W1", "W2"):
        arrays["L0_attn_" + n] = f["L0_attn_" + n]
    chunks = lambda a: a.reshape(-1, P).T
    arrays |= {
        "ctxT": f["ctx_768"].reshape(N, CT).T,
        "sim_wv": f["L0_xattn_Wv"].T, "sim_wt": f["L0_xattn_Wt"].T,
        "gate": f["L0_ffn_gate_w"], "pair_w": np.concatenate([f["L0_ffn_w0"].T, f["L0_ffn_w1"].T], 1),
        "ssm_in": f["L1_attn_in_proj_w"].T, "ssm_xp": np.concatenate([f["L1_attn_x_proj_w"].T] + 2 * [f["L1_attn_x_proj_w"][DTR:].T], 1), "ssm_dt": f["L1_attn_dt_proj_w"].T,
        "ssm_out": f["L1_attn_out_proj_w"].T,
        "a_log": f["L1_attn_A_log"].reshape(IC, P, NS).transpose(1, 0, 2),
        "cols": np.concatenate([
            chunks(f["L0_xattn_bv"]), chunks(f["L0_xattn_bt"]), chunks(f["L1_attn_in_proj_b"]),
            f["L1_attn_conv_w"].reshape(IC, P, KCONV).transpose(1, 0, 2).reshape(P, -1),
            chunks(f["L1_attn_conv_b"]), chunks(f["L1_attn_dt_proj_b"]), chunks(f["L1_attn_D"])], 1),
        "rows2": np.concatenate([f["L0_attn_gf"], f["L0_attn_bef"], f["L1_attn_out_proj_b"], f["L1_xattn_bo"],
                                 f["L0_ffn_b0"], f["L0_ffn_b1"], f["L1_ffn_br"]]),
    }
    for n in ("L1_xattn_Wq", "L1_xattn_Wk", "L1_xattn_Wv", "L1_xattn_Wo", "L1_ffn_Wr"):
        arrays[n] = f[n]
    return {k: c(a) for k, a in arrays.items()}


def kernel(**inputs):
    import concourse.bacc as bacc
    from concourse.bass_utils import run_bass_kernel_spmd as run
    arrays = host_arrays(inputs)
    nc = bacc.Bacc("TRN2", target_bir_lowering=False, num_devices=1)
    aps = {k: nc.dram_tensor("in_" + k, a.shape, F32, kind="ExternalInput").ap() for k, a in arrays.items()}
    out = nc.dram_tensor("out", (N, D), F32, kind="ExternalOutput").ap()
    decoder(nc, aps, out)
    r = run(nc, [{"in_" + k: a for k, a in arrays.items()}], core_ids=[0])
    return r.results[0]["out"].reshape(B, S, D)
```
